# Optimizing a Trainium2 kernel written in Bass

```python
import numpy as np
import jax
import jax.numpy as jnp

def _softmax(x, axis=-1):
    return jax.nn.softmax(x, axis=axis)

def _gelu(x):
    return jax.nn.gelu(x, approximate=True)

def _silu(x):
    return jax.nn.silu(x)

def _sigmoid(x):
    return jax.nn.sigmoid(x)

def _layernorm(x, axis=-1, eps=1e-05):
    m = jnp.mean(x, axis=axis, keepdims=True)
    v = jnp.var(x, axis=axis, keepdims=True)
    return (x - m) / jnp.sqrt(v + eps)

def _scatter_add(tgt, idx, src, axis=0):
    return tgt.at[idx].add(src)

def _segment_sum(src, seg, n):
    return jax.ops.segment_sum(src, seg, n)
kernel_name = 'mk_xattn_seq_d4_seqx_r4_721b7e'

def setup_inputs(seed: int=0):
    np.random.seed(seed)
    _w = jnp.asarray

    def _rec_inputs():
        import jax
        import jax.numpy as jnp
        _rk = jax.random.key(seed)
        x = 7.22e-05 + 1 * jax.random.normal(jax.random.fold_in(_rk, 1), (32, 128, 256), jnp.float32)
        _lenS = 128 - jax.random.randint(jax.random.fold_in(_rk, 7), (32,), 0, max(1, 128 // 4) + 1, jnp.int32)
        _lenS2 = 128 - jax.random.randint(jax.random.fold_in(_rk, 8), (32,), 0, max(1, 128 // 4) + 1, jnp.int32)
        _ctx_1024P = jax.random.normal(jax.random.fold_in(_rk, 11), (32, 16, 256), jnp.float32)
        _ctx_1024c = jax.random.dirichlet(jax.random.fold_in(_rk, 511), 0.3 * jnp.ones((16,), jnp.float32), (32, 128))
        _ctx_1024t = jnp.einsum('bsk,bkd->bsd', _ctx_1024c, _ctx_1024P)
        _ctx_1024t = _ctx_1024t * jax.lax.rsqrt(jnp.mean(jnp.square(_ctx_1024t)) + 1e-12) * 0.953939
        ctx_1024 = 4.13588e-05 + 0.999923 * (_ctx_1024t + 0.3 * jax.random.normal(jax.random.fold_in(_rk, 611), (32, 128, 256), jnp.float32))
        _validS = jnp.arange(128)[None, :] < _lenS[:, None]
        _validS2 = jnp.arange(128)[None, :] < _lenS2[:, None]
        _causal = jnp.tril(jnp.ones((128, 128), dtype=bool))
        mask_1xS2_bf0 = jnp.logical_not(jnp.ones((1, 128), dtype=bool))
        return (x, ctx_1024, mask_1xS2_bf0)
    x, ctx_1024, mask_1xS2_bf0 = _rec_inputs()

    def _L0_xattn_setup():
        import jax, jax.numpy as jnp
        import numpy as np
        NH = 16
        key = jax.random.key(seed)
        ks = jax.random.split(key, 5)
        B, N, D = (4, 512, 256)
        return {'tgt': jax.random.normal(ks[0], (B, N, D), dtype=jnp.float32), 'memory': jax.random.normal(ks[1], (B, N, D), dtype=jnp.float32), 'Wq': jax.random.normal(ks[2], (D, D), dtype=jnp.float32) * (1.0 / np.sqrt(D)), 'Wk': jax.random.normal(ks[3], (D, D), dtype=jnp.float32) * (1.0 / np.sqrt(D)), 'Wv': jax.random.normal(ks[4], (D, D), dtype=jnp.float32) * (1.0 / np.sqrt(D))}
    _L0_xattn_all = _L0_xattn_setup()
    _L0_xattn_in = {k: v for k, v in _L0_xattn_all.items() if k in ('Wq', 'Wk', 'Wv')}
    del _L0_xattn_all

    def _L1_xattn_setup():
        import jax, jax.numpy as jnp
        import numpy as np
        D = 256
        D_STATE = 128
        N_HEADS = 8
        D_INNER = 2 * D
        HEADDIM = 64
        H_M = D_INNER // HEADDIM
        D_CONV = 4
        CONV_DIM = D_INNER + 2 * D_STATE
        D_IN_PROJ = 2 * D_INNER + 2 * D_STATE + H_M
        B = 1
        LQ = 256
        LK = 512
        EPS = 1e-05

        def _rms(x, w):
            return x * jax.lax.rsqrt(jnp.mean(x * x, axis=-1, keepdims=True) + EPS) * w

        def _ln(x, w, b):
            mu = jnp.mean(x, axis=-1, keepdims=True)
            v = jnp.mean((x - mu) ** 2, axis=-1, keepdims=True)
            return (x - mu) * jax.lax.rsqrt(v + EPS) * w + b

        def _mamba2_block(x, norm_w, in_proj_w, conv_w, conv_b, dt_bias, A_log, D_skip, gnorm_w, out_proj_w):
            b, L, _ = x.shape
            resid = x
            zxbcdt = _rms(x, norm_w) @ in_proj_w
            z = zxbcdt[..., :D_INNER]
            xBC = zxbcdt[..., D_INNER:D_INNER + CONV_DIM]
            dt = jax.nn.softplus(zxbcdt[..., -H_M:] + dt_bias)
            padded = jnp.pad(xBC, ((0, 0), (D_CONV - 1, 0), (0, 0)))
            conv = conv_b + sum((padded[:, k:k + L, :] * conv_w[:, k] for k in range(D_CONV)))
            xBC = jax.nn.silu(conv)
            xh = xBC[..., :D_INNER].reshape(b, L, H_M, HEADDIM)
            Bm = xBC[..., D_INNER:D_INNER + D_STATE]
            Cm = xBC[..., D_INNER + D_STATE:]
            A = -jnp.exp(A_log)
            decay = jnp.exp(dt * A)
            dbx = dt[..., None] * xh

            def step(h, inp):
                dec, u, bt, ct = inp
                h = h * dec[:, :, None, None] + u[..., None] * bt[:, None, None, :]
                y = jnp.einsum('bhpn,bn->bhp', h, ct)
                return (h, y)
            h0 = jnp.zeros((b, H_M, HEADDIM, D_STATE), x.dtype)
            xs = (decay.transpose(1, 0, 2), dbx.transpose(1, 0, 2, 3), Bm.transpose(1, 0, 2), Cm.transpose(1, 0, 2))
            _, ys = jax.lax.scan(step, h0, xs)
            y = ys.transpose(1, 0, 2, 3) + D_skip[None, None, :, None] * xh
            u = _rms(y.reshape(b, L, D_INNER) * jax.nn.silu(z), gnorm_w)
            return resid + u @ out_proj_w

        def _cross_attention(x, enc, pad_mask, ln_w, ln_b, Wq, Wk, Wv, Wo):
            b, Lq, _ = x.shape
            Lk = enc.shape[1]
            dh = D // N_HEADS
            resid = x
            xn = _ln(x, ln_w, ln_b)
            q = (xn @ Wq).reshape(b, Lq, N_HEADS, dh)
            k = (enc @ Wk).reshape(b, Lk, N_HEADS, dh)
            v = (enc @ Wv).reshape(b, Lk, N_HEADS, dh)
            scores = jnp.einsum('bqhd,bkhd->bhqk', q, k) * np.float32(1.0 / np.sqrt(dh))
            scores = jnp.where(pad_mask[:, None, None, :], jnp.float32(-1000000000.0), scores)
            p = jax.nn.softmax(scores, axis=-1)
            ctx = jnp.einsum('bhqk,bkhd->bqhd', p, v).reshape(b, Lq, D)
            return resid + ctx @ Wo
        key = jax.random.key(seed)
        ks = jax.random.split(key, 10)
        s = 0.02
        return {'x': jax.random.normal(ks[0], (B, LQ, D), jnp.float32), 'encoder_out': jax.random.normal(ks[1], (B, LK, D), jnp.float32), 'encoder_padding_mask': jnp.zeros((B, LK), dtype=bool), 'm_norm_w': jnp.ones((D,), jnp.float32), 'in_proj_w': s * jax.random.normal(ks[2], (D, D_IN_PROJ), jnp.float32), 'conv_w': s * jax.random.normal(ks[3], (CONV_DIM, D_CONV), jnp.float32), 'conv_b': jnp.zeros((CONV_DIM,), jnp.float32), 'dt_bias': jnp.full((H_M,), float(np.log(np.expm1(0.01))), jnp.float32), 'A_log': jnp.log(jnp.linspace(1.0, 16.0, H_M)).astype(jnp.float32), 'D_skip': jnp.ones((H_M,), jnp.float32), 'gnorm_w': jnp.ones((D_INNER,), jnp.float32), 'out_proj_w': s * jax.random.normal(ks[4], (D_INNER, D), jnp.float32), 'ca_ln_w': jnp.ones((D,), jnp.float32), 'ca_ln_b': jnp.zeros((D,), jnp.float32), 'Wq': s * jax.random.normal(ks[5], (D, D), jnp.float32), 'Wk': s * jax.random.normal(ks[6], (D, D), jnp.float32), 'Wv': s * jax.random.normal(ks[7], (D, D), jnp.float32), 'Wo': s * jax.random.normal(ks[8], (D, D), jnp.float32)}
    _L1_xattn_all = _L1_xattn_setup()
    _L1_xattn_in = {k: v for k, v in _L1_xattn_all.items() if k in ('m_norm_w', 'in_proj_w', 'conv_w', 'conv_b', 'dt_bias', 'A_log', 'D_skip', 'gnorm_w', 'out_proj_w', 'ca_ln_w', 'ca_ln_b', 'Wq', 'Wk', 'Wv', 'Wo')}
    del _L1_xattn_all

    def _L2_xattn_setup():
        import jax, jax.numpy as jnp
        import numpy as np
        EPS = 1e-05

        def _layernorm(x, g, b):
            m = jnp.mean(x, axis=-1, keepdims=True)
            v = jnp.mean((x - m) ** 2, axis=-1, keepdims=True)
            return (x - m) / jnp.sqrt(v + EPS) * g + b

        def _mha(x, kv, Wq, Wk, Wv, mask, causal):
            m = mask[:, None]
            Q = jnp.einsum('bsd,hdk->bhsk', x, Wq) * m
            K = jnp.einsum('bsd,hdk->bhsk', kv, Wk) * m
            V = jnp.einsum('bsd,hdk->bhsk', kv, Wv) * m
            energy = jnp.einsum('bhsk,bhtk->bhst', Q, K)
            S = energy.shape[-1]
            lengths = jnp.sum(energy[:, :, 0, :] != 0, axis=-1)
            cols = jnp.arange(S)
            energy = jnp.where(cols[None, None, None, :] >= lengths[:, :, None, None], -jnp.inf, energy)
            if causal:
                energy = jnp.where(cols[None, :] > cols[:, None], -jnp.inf, energy)
            dk = Wq.shape[-1]
            score = jax.nn.softmax(energy / jnp.sqrt(jnp.asarray(dk, energy.dtype)), axis=-1)
            out = jnp.einsum('bhst,bhtk->bhsk', score, V) * m
            B, H, Sx, dkk = out.shape
            return out.transpose(0, 2, 1, 3).reshape(B, Sx, H * dkk)
        key = jax.random.key(seed)
        ks = jax.random.split(key, 20)
        B, S, D, H = (2, 512, 256, 16)
        dk = D // H
        sd = 0.02
        inp = {'x': jax.random.normal(ks[0], (B, S, D), jnp.float32), 'context': jax.random.normal(ks[1], (B, S, D), jnp.float32), 'Wq1': jax.random.normal(ks[2], (H, D, dk), jnp.float32) * sd, 'Wk1': jax.random.normal(ks[3], (H, D, dk), jnp.float32) * sd, 'Wv1': jax.random.normal(ks[4], (H, D, dk), jnp.float32) * sd, 'Wq2': jax.random.normal(ks[5], (H, D, dk), jnp.float32) * sd, 'Wk2': jax.random.normal(ks[6], (H, D, dk), jnp.float32) * sd, 'Wv2': jax.random.normal(ks[7], (H, D, dk), jnp.float32) * sd, 'ln1_g': jnp.ones((D,), jnp.float32), 'ln1_b': jnp.zeros((D,), jnp.float32), 'ln2_g': jnp.ones((D,), jnp.float32), 'ln2_b': jnp.zeros((D,), jnp.float32), 'ln3_g': jnp.ones((D,), jnp.float32), 'ln3_b': jnp.zeros((D,), jnp.float32), 'fc1_w': jax.random.normal(ks[8], (D, D), jnp.float32) * sd, 'fc1_b': jnp.zeros((D,), jnp.float32), 'fc2_w': jax.random.normal(ks[9], (D, D), jnp.float32) * sd, 'fc2_b': jnp.zeros((D,), jnp.float32)}
        return inp
    _L2_xattn_all = _L2_xattn_setup()
    _L2_xattn_in = {k: v for k, v in _L2_xattn_all.items() if k in ('Wq1', 'Wk1', 'Wv1', 'Wq2', 'Wk2', 'Wv2', 'ln1_g', 'ln1_b', 'ln2_g', 'ln2_b', 'ln3_g', 'ln3_b', 'fc1_w', 'fc1_b', 'fc2_w', 'fc2_b')}
    del _L2_xattn_all

    def _L3_xattn_setup():
        import jax, jax.numpy as jnp
        import numpy as np
        B, S, D_MODEL, H, D_FF = (2, 512, 256, 16, 1024)
        D_HEAD = D_MODEL // H
        LN_EPS = 1e-05

        def _xavier(key, shape):
            fan_out, fan_in = shape
            std = (2.0 / (fan_in + fan_out)) ** 0.5
            return jax.random.normal(key, shape, dtype=jnp.float32) * std

        def _layer_norm(x, g, b):
            mu = jnp.mean(x, axis=-1, keepdims=True)
            var = jnp.mean((x - mu) ** 2, axis=-1, keepdims=True)
            return (x - mu) * jax.lax.rsqrt(var + LN_EPS) * g + b
        key = jax.random.key(seed)
        ks = jax.random.split(key, 8)
        return {'q': jax.random.normal(ks[0], (B, S, D_MODEL), dtype=jnp.float32), 'k': jax.random.normal(ks[1], (B, S, D_MODEL), dtype=jnp.float32), 'Wq': _xavier(ks[2], (D_MODEL, D_MODEL)), 'bq': jnp.zeros((D_MODEL,), jnp.float32), 'Wk': _xavier(ks[3], (D_MODEL, D_MODEL)), 'bk': jnp.zeros((D_MODEL,), jnp.float32), 'Wv': _xavier(ks[4], (D_MODEL, D_MODEL)), 'bv': jnp.zeros((D_MODEL,), jnp.float32), 'W1': _xavier(ks[5], (D_FF, D_MODEL)), 'b1': jnp.zeros((D_FF,), jnp.float32), 'W2': _xavier(ks[6], (D_MODEL, D_FF)), 'b2': jnp.zeros((D_MODEL,), jnp.float32), 'ln_g': jnp.ones((D_MODEL,), jnp.float32), 'ln_b': jnp.zeros((D_MODEL,), jnp.float32), 'use_causal_mask': 1}
    _L3_xattn_all = _L3_xattn_setup()
    _L3_xattn_in = {k: v for k, v in _L3_xattn_all.items() if k in ('Wq', 'bq', 'Wk', 'bk', 'Wv', 'bv', 'W1', 'b1', 'W2', 'b2', 'ln_g', 'ln_b')}
    del _L3_xattn_all
    return {'x': x, 'ctx_1024': ctx_1024, 'mask_1xS2_bf0': mask_1xS2_bf0, 'L0_xattn_Wq': _L0_xattn_in['Wq'], 'L0_xattn_Wk': _L0_xattn_in['Wk'], 'L0_xattn_Wv': _L0_xattn_in['Wv'], 'L1_xattn_m_norm_w': _L1_xattn_in['m_norm_w'], 'L1_xattn_in_proj_w': _L1_xattn_in['in_proj_w'], 'L1_xattn_conv_w': _L1_xattn_in['conv_w'], 'L1_xattn_conv_b': _L1_xattn_in['conv_b'], 'L1_xattn_dt_bias': _L1_xattn_in['dt_bias'], 'L1_xattn_A_log': _L1_xattn_in['A_log'], 'L1_xattn_D_skip': _L1_xattn_in['D_skip'], 'L1_xattn_gnorm_w': _L1_xattn_in['gnorm_w'], 'L1_xattn_out_proj_w': _L1_xattn_in['out_proj_w'], 'L1_xattn_ca_ln_w': _L1_xattn_in['ca_ln_w'], 'L1_xattn_ca_ln_b': _L1_xattn_in['ca_ln_b'], 'L1_xattn_Wq': _L1_xattn_in['Wq'], 'L1_xattn_Wk': _L1_xattn_in['Wk'], 'L1_xattn_Wv': _L1_xattn_in['Wv'], 'L1_xattn_Wo': _L1_xattn_in['Wo'], 'L2_xattn_Wq1': _L2_xattn_in['Wq1'], 'L2_xattn_Wk1': _L2_xattn_in['Wk1'], 'L2_xattn_Wv1': _L2_xattn_in['Wv1'], 'L2_xattn_Wq2': _L2_xattn_in['Wq2'], 'L2_xattn_Wk2': _L2_xattn_in['Wk2'], 'L2_xattn_Wv2': _L2_xattn_in['Wv2'], 'L2_xattn_ln1_g': _L2_xattn_in['ln1_g'], 'L2_xattn_ln1_b': _L2_xattn_in['ln1_b'], 'L2_xattn_ln2_g': _L2_xattn_in['ln2_g'], 'L2_xattn_ln2_b': _L2_xattn_in['ln2_b'], 'L2_xattn_ln3_g': _L2_xattn_in['ln3_g'], 'L2_xattn_ln3_b': _L2_xattn_in['ln3_b'], 'L2_xattn_fc1_w': _L2_xattn_in['fc1_w'], 'L2_xattn_fc1_b': _L2_xattn_in['fc1_b'], 'L2_xattn_fc2_w': _L2_xattn_in['fc2_w'], 'L2_xattn_fc2_b': _L2_xattn_in['fc2_b'], 'L3_xattn_Wq': _L3_xattn_in['Wq'], 'L3_xattn_bq': _L3_xattn_in['bq'], 'L3_xattn_Wk': _L3_xattn_in['Wk'], 'L3_xattn_bk': _L3_xattn_in['bk'], 'L3_xattn_Wv': _L3_xattn_in['Wv'], 'L3_xattn_bv': _L3_xattn_in['bv'], 'L3_xattn_W1': _L3_xattn_in['W1'], 'L3_xattn_b1': _L3_xattn_in['b1'], 'L3_xattn_W2': _L3_xattn_in['W2'], 'L3_xattn_b2': _L3_xattn_in['b2'], 'L3_xattn_ln_g': _L3_xattn_in['ln_g'], 'L3_xattn_ln_b': _L3_xattn_in['ln_b']}

def reference(x, ctx_1024, mask_1xS2_bf0, L0_xattn_Wq, L0_xattn_Wk, L0_xattn_Wv, L1_xattn_m_norm_w, L1_xattn_in_proj_w, L1_xattn_conv_w, L1_xattn_conv_b, L1_xattn_dt_bias, L1_xattn_A_log, L1_xattn_D_skip, L1_xattn_gnorm_w, L1_xattn_out_proj_w, L1_xattn_ca_ln_w, L1_xattn_ca_ln_b, L1_xattn_Wq, L1_xattn_Wk, L1_xattn_Wv, L1_xattn_Wo, L2_xattn_Wq1, L2_xattn_Wk1, L2_xattn_Wv1, L2_xattn_Wq2, L2_xattn_Wk2, L2_xattn_Wv2, L2_xattn_ln1_g, L2_xattn_ln1_b, L2_xattn_ln2_g, L2_xattn_ln2_b, L2_xattn_ln3_g, L2_xattn_ln3_b, L2_xattn_fc1_w, L2_xattn_fc1_b, L2_xattn_fc2_w, L2_xattn_fc2_b, L3_xattn_Wq, L3_xattn_bq, L3_xattn_Wk, L3_xattn_bk, L3_xattn_Wv, L3_xattn_bv, L3_xattn_W1, L3_xattn_b1, L3_xattn_W2, L3_xattn_b2, L3_xattn_ln_g, L3_xattn_ln_b):
    import jax
    import jax.numpy as jnp

    def _L0_xattn_ref(tgt, memory, Wq, Wk, Wv):
        import jax, jax.numpy as jnp
        import numpy as np
        NH = 16
        B, N, D = tgt.shape
        dk = D // NH
        scale = 1.0 / np.sqrt(dk)
        q = (tgt @ Wq.T).reshape(B, N, NH, dk).transpose(0, 2, 1, 3)
        k = (memory @ Wk.T).reshape(B, N, NH, dk).transpose(0, 2, 1, 3)
        v = (memory @ Wv.T).reshape(B, N, NH, dk).transpose(0, 2, 1, 3)
        scores = jnp.einsum('bhqd,bhkd->bhqk', q, k) * scale
        probs = jax.nn.softmax(scores, axis=-1)
        att = jnp.einsum('bhqk,bhkd->bhqd', probs, v)
        att = att.transpose(0, 2, 1, 3).reshape(B, N, D)
        tgt2 = att[0]
        return tgt + tgt2

    def _L1_xattn_ref(x, encoder_out, encoder_padding_mask, m_norm_w, in_proj_w, conv_w, conv_b, dt_bias, A_log, D_skip, gnorm_w, out_proj_w, ca_ln_w, ca_ln_b, Wq, Wk, Wv, Wo):
        import jax, jax.numpy as jnp
        import numpy as np
        D = 256
        D_STATE = 128
        N_HEADS = 8
        D_INNER = 2 * D
        HEADDIM = 64
        H_M = D_INNER // HEADDIM
        D_CONV = 4
        CONV_DIM = D_INNER + 2 * D_STATE
        D_IN_PROJ = 2 * D_INNER + 2 * D_STATE + H_M
        B = 1
        LQ = 256
        LK = 512
        EPS = 1e-05

        def _rms(x, w):
            return x * jax.lax.rsqrt(jnp.mean(x * x, axis=-1, keepdims=True) + EPS) * w

        def _ln(x, w, b):
            mu = jnp.mean(x, axis=-1, keepdims=True)
            v = jnp.mean((x - mu) ** 2, axis=-1, keepdims=True)
            return (x - mu) * jax.lax.rsqrt(v + EPS) * w + b

        def _mamba2_block(x, norm_w, in_proj_w, conv_w, conv_b, dt_bias, A_log, D_skip, gnorm_w, out_proj_w):
            b, L, _ = x.shape
            resid = x
            zxbcdt = _rms(x, norm_w) @ in_proj_w
            z = zxbcdt[..., :D_INNER]
            xBC = zxbcdt[..., D_INNER:D_INNER + CONV_DIM]
            dt = jax.nn.softplus(zxbcdt[..., -H_M:] + dt_bias)
            padded = jnp.pad(xBC, ((0, 0), (D_CONV - 1, 0), (0, 0)))
            conv = conv_b + sum((padded[:, k:k + L, :] * conv_w[:, k] for k in range(D_CONV)))
            xBC = jax.nn.silu(conv)
            xh = xBC[..., :D_INNER].reshape(b, L, H_M, HEADDIM)
            Bm = xBC[..., D_INNER:D_INNER + D_STATE]
            Cm = xBC[..., D_INNER + D_STATE:]
            A = -jnp.exp(A_log)
            decay = jnp.exp(dt * A)
            dbx = dt[..., None] * xh

            def step(h, inp):
                dec, u, bt, ct = inp
                h = h * dec[:, :, None, None] + u[..., None] * bt[:, None, None, :]
                y = jnp.einsum('bhpn,bn->bhp', h, ct)
                return (h, y)
            h0 = jnp.zeros((b, H_M, HEADDIM, D_STATE), x.dtype)
            xs = (decay.transpose(1, 0, 2), dbx.transpose(1, 0, 2, 3), Bm.transpose(1, 0, 2), Cm.transpose(1, 0, 2))
            _, ys = jax.lax.scan(step, h0, xs)
            y = ys.transpose(1, 0, 2, 3) + D_skip[None, None, :, None] * xh
            u = _rms(y.reshape(b, L, D_INNER) * jax.nn.silu(z), gnorm_w)
            return resid + u @ out_proj_w

        def _cross_attention(x, enc, pad_mask, ln_w, ln_b, Wq, Wk, Wv, Wo):
            b, Lq, _ = x.shape
            Lk = enc.shape[1]
            dh = D // N_HEADS
            resid = x
            xn = _ln(x, ln_w, ln_b)
            q = (xn @ Wq).reshape(b, Lq, N_HEADS, dh)
            k = (enc @ Wk).reshape(b, Lk, N_HEADS, dh)
            v = (enc @ Wv).reshape(b, Lk, N_HEADS, dh)
            scores = jnp.einsum('bqhd,bkhd->bhqk', q, k) * np.float32(1.0 / np.sqrt(dh))
            scores = jnp.where(pad_mask[:, None, None, :], jnp.float32(-1000000000.0), scores)
            p = jax.nn.softmax(scores, axis=-1)
            ctx = jnp.einsum('bhqk,bkhd->bqhd', p, v).reshape(b, Lq, D)
            return resid + ctx @ Wo
        h = _mamba2_block(x, m_norm_w, in_proj_w, conv_w, conv_b, dt_bias, A_log, D_skip, gnorm_w, out_proj_w)
        return _cross_attention(h, encoder_out, encoder_padding_mask, ca_ln_w, ca_ln_b, Wq, Wk, Wv, Wo)

    def _L2_xattn_ref(x, context, Wq1, Wk1, Wv1, Wq2, Wk2, Wv2, ln1_g, ln1_b, ln2_g, ln2_b, ln3_g, ln3_b, fc1_w, fc1_b, fc2_w, fc2_b):
        import jax, jax.numpy as jnp
        import numpy as np
        EPS = 1e-05

        def _layernorm(x, g, b):
            m = jnp.mean(x, axis=-1, keepdims=True)
            v = jnp.mean((x - m) ** 2, axis=-1, keepdims=True)
            return (x - m) / jnp.sqrt(v + EPS) * g + b

        def _mha(x, kv, Wq, Wk, Wv, mask, causal):
            m = mask[:, None]
            Q = jnp.einsum('bsd,hdk->bhsk', x, Wq) * m
            K = jnp.einsum('bsd,hdk->bhsk', kv, Wk) * m
            V = jnp.einsum('bsd,hdk->bhsk', kv, Wv) * m
            energy = jnp.einsum('bhsk,bhtk->bhst', Q, K)
            S = energy.shape[-1]
            lengths = jnp.sum(energy[:, :, 0, :] != 0, axis=-1)
            cols = jnp.arange(S)
            energy = jnp.where(cols[None, None, None, :] >= lengths[:, :, None, None], -jnp.inf, energy)
            if causal:
                energy = jnp.where(cols[None, :] > cols[:, None], -jnp.inf, energy)
            dk = Wq.shape[-1]
            score = jax.nn.softmax(energy / jnp.sqrt(jnp.asarray(dk, energy.dtype)), axis=-1)
            out = jnp.einsum('bhst,bhtk->bhsk', score, V) * m
            B, H, Sx, dkk = out.shape
            return out.transpose(0, 2, 1, 3).reshape(B, Sx, H * dkk)
        mask0 = 1.0 - jnp.all(x == 0, axis=2, keepdims=True).astype(x.dtype)
        z = _mha(x, x, Wq1, Wk1, Wv1, mask0, causal=True)
        x1 = _layernorm(x + z, ln1_g, ln1_b)
        mask1 = 1.0 - jnp.all(x1 == 0, axis=2, keepdims=True).astype(x1.dtype)
        z = _mha(x1, context, Wq2, Wk2, Wv2, mask1, causal=False)
        x2 = _layernorm(x1 + z, ln2_g, ln2_b)
        z = jnp.maximum(x2 @ fc1_w.T + fc1_b, 0.0) * mask0
        z = (z @ fc2_w.T + fc2_b) * mask0
        return _layernorm(x2 + z, ln3_g, ln3_b)

    def _L3_xattn_ref(q, k, Wq, bq, Wk, bk, Wv, bv, W1, b1, W2, b2, ln_g, ln_b, use_causal_mask):
        import jax, jax.numpy as jnp
        import numpy as np
        B, S, D_MODEL, H, D_FF = (2, 512, 256, 16, 1024)
        D_HEAD = D_MODEL // H
        LN_EPS = 1e-05

        def _xavier(key, shape):
            fan_out, fan_in = shape
            std = (2.0 / (fan_in + fan_out)) ** 0.5
            return jax.random.normal(key, shape, dtype=jnp.float32) * std

        def _layer_norm(x, g, b):
            mu = jnp.mean(x, axis=-1, keepdims=True)
            var = jnp.mean((x - mu) ** 2, axis=-1, keepdims=True)
            return (x - mu) * jax.lax.rsqrt(var + LN_EPS) * g + b
        Bq, Sq, _ = q.shape
        Sk = k.shape[1]
        Q = q @ Wq.T + bq
        K = k @ Wk.T + bk
        V = k @ Wv.T + bv
        Q_ = Q.reshape(Bq, Sq, H, D_HEAD).transpose(0, 2, 1, 3)
        K_ = K.reshape(Bq, Sk, H, D_HEAD).transpose(0, 2, 1, 3)
        V_ = V.reshape(Bq, Sk, H, D_HEAD).transpose(0, 2, 1, 3)
        scores = jnp.einsum('bhqd,bhkd->bhqk', Q_, K_) / D_HEAD ** 0.5
        if use_causal_mask:
            causal = jnp.tril(jnp.ones((Sq, Sk), dtype=bool))
            scores = jnp.where(causal, scores, jnp.float32(-1000000000.0))
        sim = jax.nn.softmax(scores, axis=-1)
        att = jnp.einsum('bhqk,bhkd->bhqd', sim, V_)
        att_h = att.transpose(0, 2, 1, 3).reshape(Bq, Sq, D_MODEL)
        att_h = att_h + q
        att_h = _layer_norm(att_h, ln_g, ln_b)
        ff = jax.nn.gelu(att_h @ W1.T + b1, approximate=False) @ W2.T + b2
        return ff + att_h
    x = _L0_xattn_ref(x, ctx_1024, L0_xattn_Wq, L0_xattn_Wk, L0_xattn_Wv)
    x = _L1_xattn_ref(x, ctx_1024, mask_1xS2_bf0, L1_xattn_m_norm_w, L1_xattn_in_proj_w, L1_xattn_conv_w, L1_xattn_conv_b, L1_xattn_dt_bias, L1_xattn_A_log, L1_xattn_D_skip, L1_xattn_gnorm_w, L1_xattn_out_proj_w, L1_xattn_ca_ln_w, L1_xattn_ca_ln_b, L1_xattn_Wq, L1_xattn_Wk, L1_xattn_Wv, L1_xattn_Wo)
    x = _L2_xattn_ref(x, ctx_1024, L2_xattn_Wq1, L2_xattn_Wk1, L2_xattn_Wv1, L2_xattn_Wq2, L2_xattn_Wk2, L2_xattn_Wv2, L2_xattn_ln1_g, L2_xattn_ln1_b, L2_xattn_ln2_g, L2_xattn_ln2_b, L2_xattn_ln3_g, L2_xattn_ln3_b, L2_xattn_fc1_w, L2_xattn_fc1_b, L2_xattn_fc2_w, L2_xattn_fc2_b)
    x = _L3_xattn_ref(x, ctx_1024, L3_xattn_Wq, L3_xattn_bq, L3_xattn_Wk, L3_xattn_bk, L3_xattn_Wv, L3_xattn_bv, L3_xattn_W1, L3_xattn_b1, L3_xattn_W2, L3_xattn_b2, L3_xattn_ln_g, L3_xattn_ln_b, 1)
    return x

_drawn_inputs = setup_inputs


def setup_inputs(seed=0):
    import zlib

    import numpy as np

    out = dict(_drawn_inputs(seed))
    spreads = {'L1_xattn_m_norm_w': (1.0, 0.2),
     'L1_xattn_conv_b': (0.0, 0.1),
     'L1_xattn_dt_bias': (-4.600165843963623, 0.6),
     'L1_xattn_D_skip': (1.0, 0.2),
     'L1_xattn_gnorm_w': (1.0, 0.2),
     'L1_xattn_ca_ln_w': (1.0, 0.6),
     'L1_xattn_ca_ln_b': (0.0, 0.8),
     'L2_xattn_ln1_g': (1.0, 0.2),
     'L2_xattn_ln1_b': (0.0, 0.1),
     'L2_xattn_ln2_g': (1.0, 0.2),
     'L2_xattn_ln2_b': (0.0, 0.1),
     'L2_xattn_ln3_g': (1.0, 0.2),
     'L2_xattn_ln3_b': (0.0, 0.1),
     'L2_xattn_fc1_b': (0.0, 0.39),
     'L2_xattn_fc2_b': (0.0, 0.1),
     'L3_xattn_bq': (0.0, 0.377),
     'L3_xattn_bk': (0.0, 0.8),
     'L3_xattn_bv': (0.0, 0.1),
     'L3_xattn_b1': (0.0, 0.1),
     'L3_xattn_b2': (0.0, 0.1),
     'L3_xattn_ln_g': (1.0, 0.2),
     'L3_xattn_ln_b': (0.0, 0.1)}
    factors = {'L1_xattn_A_log': 8.0,
     'L1_xattn_Wq': 8.0,
     'L1_xattn_Wk': 8.0,
     'L2_xattn_Wq1': 8.0,
     'L2_xattn_Wk1': 8.0,
     'L2_xattn_Wq2': 8.0,
     'L2_xattn_Wk2': 8.0}
    for name, (base, spread) in spreads.items():
        noise = np.random.default_rng([zlib.crc32(name.encode()), seed]).standard_normal(out[name].shape)
        drawn = base * np.exp(spread * noise) if base else spread * noise
        out[name] = jnp.asarray(drawn.astype(out[name].dtype))
    for name, factor in factors.items():
        out[name] = (out[name] * factor).astype(out[name].dtype)
    return out
```

```python
from contextlib import ExitStack

import concourse.bass as bass
from concourse import mybir

F32 = mybir.dt.float32
BF16 = mybir.dt.bfloat16
I32 = mybir.dt.int32
U8 = mybir.dt.uint8
ALU = mybir.AluOpType
ACT = mybir.ActivationFunctionType
AX_X = mybir.AxisListType.X

P = 128
B = 32
D = 256
DC = D // P
G = 4
ITERS = B // G
INNER = 512
IC = INNER // P
STATE = 128
MH = 8
MD = INNER // MH
TAPS = 4
XBC = (INNER + 2 * STATE) // P
BCH, CCH = XBC - 2, XBC - 1
IN_PROJ = 2 * INNER + 2 * STATE + MH
FF = 1024
FC = FF // P
H16, DH16 = 16, 16
H8, DH8 = 8, 32
EPS = 1e-5
MASKED = -float(2 ** 30)
SCALE8 = 0.1767766922712326
MAGIC = float(0x5F3759DF)
NEWTON = 3
LOG1P_TERMS = 8
UNITS = 2 * G

CONST_COLS = dict(ident=P, before=P, gate=P, after=P, causal=P, causal_t=P, even_odd=2, head=8, index=1)
CONST_AT = {n: sum(list(CONST_COLS.values())[:i]) for i, n in enumerate(CONST_COLS)}
CONST_WIDTH = sum(CONST_COLS.values())
VECTORS = dict(m_norm=DC, g_norm=IC, conv_w=XBC * TAPS, conv_b=XBC, ca_w=DC, ca_b=DC, fc1_b=DC, q4_b=DC, k4_b=DC, up_b=FC)
VECTOR_AT = {n: sum(list(VECTORS.values())[:i]) for i, n in enumerate(VECTORS)}
VECTOR_WIDTH = sum(VECTORS.values())
ROWS = dict(g1=D, b1=D, g2=D, b2=D, g3=D, b3=D, g4=D, b4=D, fc2=D, v4=D, down=D, dt_bias=MH, A_log=MH, D_skip=MH)
ROW_AT = {n: sum(list(ROWS.values())[:i]) for i, n in enumerate(ROWS)}
ROW_WIDTH = sum(ROWS.values())

def ring_jobs():
    jobs = [("ctxT", l) for l in range(G)]
    jobs += [(w, l) for l in range(G) for w in ("K1", "V1")]
    jobs += [("xhatT", l) for l in range(G)]
    jobs += [(w, l) for l in range(G) for w in ("xbc0", "xbc1", "z")]
    jobs += [(w, l) for l in range(G) for w in ("CB", "xh")]
    jobs += [("Y", l) for l in range(G)] + [("uT", l) for l in range(G)] + [("proj", l) for l in range(G)]
    jobs += pipelined("xnT", ["Q1"])
    jobs += [("O1", l) for l in range(G)]
    jobs += pipelined("oT", ["Wo"])
    jobs += pipelined("x2T", ["Q2", "K2", "V2"])
    jobs += [("e2", l) for l in range(G)] + [("n2", l) for l in range(G)] + [("O2", l) for l in range(G)]
    jobs += pipelined("x3T", ["Q3", "V3", "row", "K3"])
    jobs += [("e3", l) for l in range(G)] + [("n3", l) for l in range(G)] + [("O3", l) for l in range(G)]
    jobs += pipelined("x4T", ["fc1"])
    jobs += [("fc2", l) for l in range(G)]
    jobs += [(w, l) for l in range(G) for w in ("K4", "V4")]
    jobs += pipelined("x5T", ["Q4"])
    jobs += [("O4", l) for l in range(G)]
    jobs += pipelined("x6T", ["up0", "up1"])
    jobs += [("down", l) for l in range(G)]
    return jobs


def pipelined(first, then):
    order = [(first, 0)]
    for l in range(G):
        if l + 1 < G:
            order.append((first, l + 1))
        order += [(w, l) for w in then]
    return order


BANKS = 4
JOBS = ring_jobs()
JOB_AT = {job: n for n, job in enumerate(JOBS)}
assert len(JOB_AT) == len(JOBS) and len(JOBS) % BANKS == 0
USES = len(JOBS) // BANKS
FIRST_JOBS = ["x0T", "c0T", "Q0", "K0", "V0", "O0", "bias0", "bias1"]
FIRST_USES = len(FIRST_JOBS) // BANKS


def job(it, what, lane=0):
    if what in FIRST_JOBS:
        n = FIRST_JOBS.index(what)
        return n % BANKS, n // BANKS
    n = JOB_AT[what, lane]
    return n % BANKS, it * USES + (FIRST_USES + n // BANKS)


def nth(it, lane):
    return it * G + (lane + 1)


def nth_unit(it, n):
    return it * UNITS + (n + 1)


class Chain:

    def __init__(self, eng, sem):
        self.eng, self.sem, self.count = eng, sem, 0
        eng.sem_clear(sem)

    def __call__(self, instruction):
        self.count += 1
        instruction.then_inc(self.sem, 1)
        self.eng.wait_ge(self.sem, self.count)


def decoder_stack(nc, a, out):
    ctx = ExitStack()
    with ctx:
        def sb(name, shape, dt=F32):
            return ctx.enter_context(nc.sbuf_tensor(name, shape, dt))

        def pb(name, shape):
            return ctx.enter_context(nc.psum_tensor(name, shape, F32))

        def sem(name):
            return ctx.enter_context(nc.semaphore(name))

        const = sb("const", [P, CONST_WIDTH])

        def con(name):
            return const[:, CONST_AT[name]:CONST_AT[name] + CONST_COLS[name]]

        ident, before, gate_mask, after = con("ident"), con("before"), con("gate"), con("after")
        even_odd, head8, index = con("even_odd"), con("head"), con("index")
        ident_bf = sb("ident_bf", [P, P], BF16)
        ones_bf = sb("ones_bf", [P, P], BF16)
        causal_bf = sb("causal_bf", [P, P], BF16)
        causal_t_bf = sb("causal_t_bf", [P, P], BF16)

        w_in = sb("w_in", [P, DC, IN_PROJ])
        w_out = sb("w_out", [P, IC, D])
        square = {n: sb(f"w_{n}", [P, DC, D]) for n in (
            "q1", "k1", "v1", "o1", "q2", "k2", "v2", "q3", "k3", "v3", "fc1", "fc2", "q4", "k4", "v4")}
        w_up = sb("w_up", [P, DC, FF])
        w_down = sb("w_down", [P, FC, D])
        vectors = sb("vectors", [P, VECTOR_WIDTH])

        def vec(name):
            return vectors[:, VECTOR_AT[name]:VECTOR_AT[name] + VECTORS[name]]

        m_norm, g_norm, conv_b, ca_w, ca_b = (vec(n) for n in ("m_norm", "g_norm", "conv_b", "ca_w", "ca_b"))
        conv_w = vec("conv_w").rearrange("p (c k) -> p c k", c=XBC)
        fc1_b, q4_b, k4_b, up_b = (vec(n) for n in ("fc1_b", "q4_b", "k4_b", "up_b"))
        q1_bias = sb("q1_bias", [P, DC])
        q4_bias = sb("q4_bias", [P, DC, 2])
        row_all = sb("row_all", [P, ROW_WIDTH])
        rows = {n: row_all[:, ROW_AT[n]:ROW_AT[n] + ROWS[n]] for n in ROWS}
        dt_bias, decay_rate, skip = rows["dt_bias"], rows["A_log"], rows["D_skip"]
        pad_u8 = sb("pad_u8", [P, P], U8)
        pad_col_u8 = sb("pad_col_u8", [P, 1], U8)
        keep_row = sb("keep_row", [P, P])
        padding_bf = sb("padding_bf", [P, P], BF16)
        pad_bias = sb("pad_bias", [P, 1])

        x_in = sb("x_in", [P, G, D])
        c_in = sb("c_in", [P, G, D])
        cT = sb("cT", [P, G, DC, P])
        att0 = sb("att0", [P, D])
        res = sb("res", [P, G, D])
        nrm = sb("nrm", [P, G, D])
        actT = sb("actT", [P, G, DC, P])
        raw = sb("raw", [P, G, XBC, TAPS - 1 + P])
        conv = sb("conv", [P, G, XBC, P])
        zs = sb("zs", [P, G, INNER])
        tz = sb("tz", [P, G, INNER])
        decay = sb("decay", [P, G, MH, P])
        dbx = sb("dbx", [P, G, INNER])
        dx = sb("dx", [P, G, INNER])
        att = sb("att", [P, G, D])
        plus = sb("plus", [P, G, D])
        result = sb("result", [P, G, D])
        fc1T = sb("fc1T", [P, G, DC, P])
        state_gate = sb("state_gate", [P, G, P])
        stat = sb("stat", [P, G, 16])
        bn = sb("bn", [P, G, 6])
        dts = sb("dts", [P, G, 12, MH])
        rec = sb("rec", [P, G, H16])
        mask0 = sb("mask0", [P, G, 2])
        mask1 = sb("mask1", [P, G, 2])
        mask1_bf = sb("mask1_bf", [P, G], BF16)
        row_mask = sb("row_mask", [P, G, P])
        q_first = sb("q_first", [P, G, DC, 8])
        nonzero = sb("nonzero", [P, G, H16], BF16)
        keep = sb("keep", [P, G, H16])
        neg_max = sb("neg_max", [P, 2, 8], BF16)

        K1 = sb("K1", [P, G, DC, P])
        K1_bf = sb("K1_bf", [P, G, DC, P], BF16)
        V1 = sb("V1", [P, G, H8, DH8 + 1])
        dbx_flat = dbx[:, :, :].rearrange("p g n -> p (g n)")
        K2 = dbx_flat[:, 0:G * D].rearrange("p (g c k) -> p g c k", g=G, c=DC)
        K2_bf = dbx_flat[:, G * D:G * D + G * D // 2].bitcast(BF16).rearrange("p (g c k) -> p g c k", g=G, c=DC)
        V2 = dx[:, :, :].rearrange("p g n -> p (g n)")[:, 0:G * H16 * (DH16 + 1)].rearrange(
            "p (g h e) -> p g h e", g=G, h=H16)
        conv_flat = conv[:, :, :, :].rearrange("p g c k -> p (g c k)")
        Q = conv_flat[:, 0:G * DC * 2 * P].rearrange("p (g c j k) -> p g c j k", g=G, c=DC, j=2)
        Q_bf = conv_flat[:, G * DC * 2 * P:G * DC * 3 * P].bitcast(BF16).rearrange(
            "p (g c j k) -> p g c j k", g=G, c=DC, j=2)
        weights = zs[:, :, :].rearrange("p g n -> p (g n)").rearrange("p (s b n) -> p s b n", s=2, b=2)
        uT = tz[:, :, :].rearrange("p g (c k) -> p g c k", c=IC)
        gT = decay
        decay_flat = decay[:, :, :, :].rearrange("p g h k -> p (g h k)")
        w0 = {n: decay_flat[:, i * DC * D:(i + 1) * DC * D].rearrange("p (c n) -> p c n", c=DC)
              for i, n in enumerate(("q0", "k0", "v0"))}

        bank = [pb(f"ring{i}", [P, 512]) for i in range(BANKS)]
        smax = pb("smax", [P, 2, 512])
        sexp = pb("sexp", [P, 2, 512])

        bank_full = [sem(f"bank_full{i}") for i in range(BANKS)]
        bank_read = [sem(f"bank_read{i}") for i in range(BANKS)]
        S = {n: sem(n) for n in (
            "const_in w0_in wmamba_in w1_in w2_in w3_in x_in c_in stored "
            "ready_consts ready_weights ones_col pads_zero rates pads att0 q0 k0 q0_bf k0_bf "
            "dve_first pool_first act_first "
            "dve_step pool_step pool_waits "
            "x1 ss1 seed1 rstd1 xhat ctx_free K1 K1_bf V1 near0 edt dt am conv tanh xbc gated "
            "log_decay decay M u ss2 seed2 rstd2 seed3 rstd3 xn "
            "Q1 Q1_bf O1half o1 Q2 Q2_bf K2_bf q2_first nz2 keep2 V2 O2half seed4 rstd4 t4 x3 m1 "
            "Q3 Q3_bf K3_bf q3_first nz3 keep3 V3 O3half seed5 rstd5 t5 x4 fc1 seed6 rstd6 t6 x5 "
            "Q4 Q4_bf K4_bf V4 V4ones O4half seed7 rstd7 t7 x6 plus gelu result "
            "smax0 maxima0 sexp0 weights0 smax1 maxima1 sexp1 weights1 smax2 maxima2 sexp2 weights2 "
            "smax3 maxima3 sexp3 weights3 smax4 maxima4 sexp4 weights4 O0half").split()}

        x_v = a["x"].rearrange("(i g) t d -> i t g d", g=G)
        c_v = a["ctx_1024"].rearrange("(i g) t d -> i t g d", g=G)
        o_v = out.rearrange("(i g) t d -> i t g d", g=G)
        block = ctx.enter_context(nc.Block())

        def heads_of(two, u):
            n = 2 if two else 1
            return [(b, 2 * u + b, c, j, (4 * c + 2 * u + b) * n + j)
                    for b in range(2) for c in range(DC) for j in range(n)]

        def lanes_units(lanes):
            return [(l, u) for l in lanes for u in range(2)]

        @block.sync
        def _(sp):
            def chunks(name):
                return a[name].rearrange("(c p) n -> p c n", p=P)

            sp.sem_inc(S["stored"], 16)
            sp.dma_start(const[:, :], a["const"]).then_inc(S["const_in"], 16)
            sp.dma_start(x_in[:, :, :], x_v[0]).then_inc(S["x_in"], 16)
            sp.dma_start(c_in[:, :, :], c_v[0]).then_inc(S["c_in"], 16)
            for n in ("q0", "k0", "v0"):
                sp.dma_start(w0[n], chunks(n)).then_inc(S["w0_in"], 16)
            for dst, src in ((w_in[:, :, :], chunks("in_proj")), (w_out[:, :, :], chunks("out_proj")),
                             (vectors[:, :], a["vectors"]), (row_all[:, :], a["rows"].partition_broadcast(P)),
                             (pad_u8[:, :], a["pad"].bitcast(U8)[0].partition_broadcast(P)),
                             (pad_col_u8[:, :], a["pad"].bitcast(U8).rearrange("a k -> k a"))):
                sp.dma_start(dst, src).then_inc(S["wmamba_in"], 16)
            for n in ("q1", "k1", "v1", "o1"):
                sp.dma_start(square[n][:, :, :], chunks(n)).then_inc(S["w1_in"], 16)
            for n in ("q2", "k2", "v2", "q3", "k3", "v3", "fc1", "fc2"):
                sp.dma_start(square[n][:, :, :], chunks(n)).then_inc(S["w2_in"], 16)
            for dst, src in ([(square[n][:, :, :], chunks(n)) for n in ("q4", "k4", "v4")]
                             + [(w_up[:, :, :], chunks("up")), (w_down[:, :, :], chunks("down"))]):
                sp.dma_start(dst, src).then_inc(S["w3_in"], 16)

            def store(it):
                b, use = job(it, "down", G - 1)
                sp.wait_ge(bank_read[b], use + 1)
                sp.dma_start(o_v[it], result[:, :, :]).then_inc(S["stored"], 16)

            with sp.Fori(0, ITERS - 1) as it:
                sp.wait_ge(S["x1"], nth(it, G - 1))
                sp.dma_start(x_in[:, :, :], x_v[it + 1]).then_inc(S["x_in"], 16)
                bank_, use = job(it, "ctxT", G - 1)
                sp.wait_ge(bank_full[bank_], use + 1)
                sp.dma_start(c_in[:, :, :], c_v[it + 1]).then_inc(S["c_in"], 16)
                store(it)
            store(ITERS - 1)
            sp.wait_ge(S["stored"], 16 * (ITERS + 1))

        @block.tensor
        def _(pe):
            mm = nc.tensor.matmul

            def claim(it, what, lane=0):
                b, use = job(it, what, lane)
                if what not in FIRST_JOBS or use:
                    pe.wait_ge(bank_read[b], use)
                return bank[b], bank_full[b]

            def evacuated(it, what, lane=0):
                b, use = job(it, what, lane)
                pe.wait_ge(bank_read[b], use + 1)

            def flip(it, what, lane, src, n):
                t, full = claim(it, what, lane)
                for c in range(n):
                    last = nc.tensor.transpose(t[:, c * P:(c + 1) * P], src[:, c * P:(c + 1) * P], ident)
                last.then_inc(full, 1)

            def to_channels(t, at, w, cols, xT, n=DC):
                for c in range(n):
                    last = mm(t[:, at:at + P], w[:, c, cols:cols + P], xT[:, c, :], start=(c == 0), stop=(c == n - 1))
                return last

            def to_tokens(t, at, w, lo, hi, xT, n=DC):
                for c in range(n):
                    last = mm(t[:, at:at + hi - lo], xT[:, c, :], w[:, c, lo:hi], start=(c == 0), stop=(c == n - 1))
                return last

            def project_T(it, what, lane, w, xT):
                t, full = claim(it, what, lane)
                for m in range(DC):
                    last = to_channels(t, m * P, w, m * P, xT)
                last.then_inc(full, 1)

            def project(it, what, lane, w, xT, n=DC):
                t, full = claim(it, what, lane)
                to_tokens(t, 0, w, 0, D, xT, n).then_inc(full, 1)

            def attention(it, a_, lanes, two, mask, Kf, Kb, V, k_ready, v_ready, dh, half):
                units = lanes_units(lanes)
                n_heads = 2 if two else 1
                width = DC * n_heads * P

                def count(n):
                    return nth_unit(it, n)

                def for_maxima(n):
                    l, u = units[n]
                    if n:
                        pe.wait_ge(S[f"maxima{a_}"], count(n - 1))
                    if u == 0:
                        pe.wait_ge(S[f"Q{a_}_bf" if a_ else "q0_bf"], nth(it, l))
                        pe.wait_ge(S[k_ready], nth(it, l))
                    hs = heads_of(two, u)
                    for k, (b, r, c, j, h) in enumerate(hs):
                        at = (c * n_heads + j) * P
                        closes = mask is None and at + P == width
                        last = mm(smax[:, b, at:at + P], Q_bf[32 * r:32 * r + 32, l, c, j, :],
                                  Kb[32 * r:32 * r + 32, l, c, :], start=(at == 0), stop=closes)
                    for b in range(2):
                        if mask == "causal":
                            last = mm(smax[:, b, :], ident_bf[:, :],
                                      causal_bf[:, :].unsqueeze(1).broadcast_to((P, 4, P)), start=False, stop=True)
                        if mask == "padding":
                            last = mm(smax[:, b, 0:width], ident_bf[:, :],
                                      padding_bf[:, :].unsqueeze(1).broadcast_to((P, DC, P)), start=False, stop=True)
                    last.then_inc(S[f"smax{a_}"], 1)

                def for_weights(n):
                    l, u = units[n]
                    if n:
                        pe.wait_ge(S[f"weights{a_}"], count(n - 1))
                    for b in range(2):
                        r = 2 * u + b
                        for c in range(DC):
                            mm(sexp[:, b, c * n_heads * P:(c + 1) * n_heads * P], Kf[32 * r:32 * r + 32, l, c, :],
                               Q[32 * r:32 * r + 32, l, c, 0:n_heads, :], start=(c == 0), stop=False)

                def shift(n):
                    l, u = units[n]
                    pe.wait_ge(S[f"maxima{a_}"], count(n))
                    for k, (b, r, c, j, h) in enumerate(heads_of(two, u)):
                        at = (c * n_heads + j) * P
                        last = mm(sexp[:, b, at:at + P], neg_max[:, n % 2, k:k + 1].broadcast_to((P, P)),
                                  ident_bf[:, :], start=False, stop=(mask != "causal" and at + P == width))
                    if mask == "causal":
                        for b in range(2):
                            last = mm(sexp[:, b, :], ident_bf[:, :],
                                      causal_t_bf[:, :].unsqueeze(1).broadcast_to((P, 4, P)), start=False, stop=True)
                    last.then_inc(S[f"sexp{a_}"], 1)

                def values(n):
                    l, u = units[n]
                    b_, use = job(it, f"O{a_}", l)
                    if u == 0:
                        claim(it, f"O{a_}", l)
                        if v_ready is None:
                            evacuated(it, f"V{a_}", l)
                        else:
                            pe.wait_ge(S[v_ready], nth(it, l))
                    pe.wait_ge(S[f"weights{a_}"], count(n))
                    for k, (b, r, c, j, h) in enumerate(heads_of(two, u)):
                        at = (c * n_heads + j) * P
                        last = mm(bank[b_][:, h * (dh + 1):(h + 1) * (dh + 1)], weights[:, n % 2, b, at:at + P],
                                  V[:, l, h, :], start=True, stop=True)
                    last.then_inc(bank_full[b_] if u else S[half], 1)

                for_maxima(0)
                for n in range(len(units)):
                    for_weights(n)
                    if n + 1 < len(units):
                        for_maxima(n + 1)
                    shift(n)
                    if n:
                        values(n - 1)
                values(len(units) - 1)

            pe.wait_ge(S["const_in"], 16)
            pe.wait_ge(S["x_in"], 16)
            flip(0, "x0T", 0, x_in[:, 0, :], DC)
            pe.wait_ge(S["c_in"], 16)
            flip(0, "c0T", 0, c_in[:, 0, :], DC)
            pe.wait_ge(S["w0_in"], 16 * 3)
            evacuated(0, "x0T")
            project_T(0, "Q0", 0, w0["q0"], actT[:, 0])
            evacuated(0, "c0T")
            project_T(0, "K0", 0, w0["k0"], cT[:, 0])
            project(0, "V0", 0, w0["v0"], cT[:, 0])
            pe.wait_ge(S["ready_consts"], 1)
            pe.wait_ge(S["ones_col"], 2)
            attention(0, 0, [0], True, None, K2, K2_bf, V2, "k0_bf", None, DH16, "O0half")
            pe.wait_ge(S["wmamba_in"], 16 * 6)
            pe.wait_ge(S["w1_in"], 16 * 4)
            for m in range(DC):
                t, full = claim(0, f"bias{m}")
                for c in range(DC):
                    last = mm(t[:, 0:1], square["q1"][:, c, m * P:(m + 1) * P], ca_b[:, c:c + 1],
                              start=(c == 0), stop=(c == DC - 1))
                last.then_inc(full, 1)
            pe.wait_ge(S["ready_weights"], 1)
            pe.wait_ge(S["w2_in"], 16 * 8)
            pe.wait_ge(S["w3_in"], 16 * 5)

            def stages(it):
                pe.wait_ge(S["c_in"], it * 16 + 16)
                for l in range(G):
                    flip(it, "ctxT", l, c_in[:, l, :], DC)
                for l in range(G):
                    evacuated(it, "ctxT", l)
                    project_T(it, "K1", l, square["k1"], cT[:, l])
                    project(it, "V1", l, square["v1"], cT[:, l])
                for l in range(G):
                    pe.wait_ge(S["xhat"], nth(it, l))
                    flip(it, "xhatT", l, nrm[:, l, :], DC)
                for l in range(G):
                    evacuated(it, "xhatT", l)
                    for half in range(2):
                        t, full = claim(it, f"xbc{half}", l)
                        for k in range(XBC // 2):
                            last = to_channels(t, k * P, w_in, INNER + (half * XBC // 2 + k) * P, actT[:, l])
                        if half == 0:
                            last = to_tokens(t, XBC // 2 * P, w_in, IN_PROJ - MH, IN_PROJ, actT[:, l])
                        last.then_inc(full, 1)
                    t, full = claim(it, "z", l)
                    to_tokens(t, 0, w_in, 0, INNER, actT[:, l]).then_inc(full, 1)
                for l in range(G):
                    pe.wait_ge(S["xbc"], nth(it, l))
                    t, full = claim(it, "CB", l)
                    mm(t[:, 0:P], conv[:, l, BCH, :], conv[:, l, CCH, :], start=True, stop=True).then_inc(full, 1)
                    flip(it, "xh", l, conv[:, l, 0:IC, :].rearrange("p c k -> p (c k)"), IC)
                    pe.wait_ge(S["am"], nth(it, l))
                    if l:
                        pe.wait_ge(S["decay"], nth(it, l - 1))
                    for h in range(MH):
                        b, at = h // 4, h % 4 * P
                        last = mm(sexp[:, b, at:at + P], decay[:, l, h, :], before, start=(at == 0), stop=(h % 4 == 3))
                    last.then_inc(S["log_decay"], 1)
                for l in range(G):
                    t, full = claim(it, "Y", l)
                    evacuated(it, "xh", l)
                    pe.wait_ge(S["M"], nth(it, l))
                    for h in range(MH):
                        last = mm(t[:, h * MD:(h + 1) * MD], decay[:, l, h, :], dbx[:, l, h * MD:(h + 1) * MD],
                                  start=True, stop=True)
                    last.then_inc(full, 1)
                for l in range(G):
                    pe.wait_ge(S["u"], nth(it, l))
                    flip(it, "uT", l, zs[:, l, :], IC)
                for l in range(G):
                    evacuated(it, "uT", l)
                    project(it, "proj", l, w_out, uT[:, l], IC)

                def flip_nrm(l):
                    pe.wait_ge(S["xn"], nth(it, l))
                    flip(it, "xnT", l, nrm[:, l, :], DC)

                flip_nrm(0)
                for l in range(G):
                    if l + 1 < G:
                        flip_nrm(l + 1)
                    evacuated(it, "xnT", l)
                    project_T(it, "Q1", l, square["q1"], actT[:, l])
                attention(it, 1, range(G), False, "padding", K1, K1_bf, V1, "K1_bf", None, DH8, "O1half")

                def flip_att(l):
                    evacuated(it, "O1", l)
                    flip(it, "oT", l, att[:, l, :], DC)

                flip_att(0)
                for l in range(G):
                    if l + 1 < G:
                        flip_att(l + 1)
                    evacuated(it, "oT", l)
                    project(it, "Wo", l, square["o1"], actT[:, l])

                def flip_x2(l):
                    evacuated(it, "Wo", l)
                    flip(it, "x2T", l, res[:, l, :], DC)

                flip_x2(0)
                for l in range(G):
                    if l + 1 < G:
                        flip_x2(l + 1)
                    evacuated(it, "x2T", l)
                    project_T(it, "Q2", l, square["q2"], actT[:, l])
                    project_T(it, "K2", l, square["k2"], actT[:, l])
                    project(it, "V2", l, square["v2"], actT[:, l])

                def lengths(a_):
                    for l in range(G):
                        t, full = claim(it, f"e{a_}", l)
                        evacuated(it, f"K{a_}", l)
                        pe.wait_ge(S[f"q{a_}_first"], nth(it, l))
                        for c in range(DC):
                            last = mm(t[:, c * 8:c * 8 + 8], K2[:, l, c, :], q_first[:, l, c, :], start=True, stop=True)
                        last.then_inc(full, 1)
                    for l in range(G):
                        t, full = claim(it, f"n{a_}", l)
                        evacuated(it, f"e{a_}", l)
                        mm(t[:, 0:H16], ones_bf[:, :], nonzero[:, l, :], start=True, stop=True).then_inc(full, 1)

                lengths(2)
                attention(it, 2, range(G), True, "causal", K2, K2_bf, V2, "K2_bf", "V2", DH16, "O2half")

                def flip_x3(l):
                    pe.wait_ge(S["x3"], nth(it, l))
                    flip(it, "x3T", l, res[:, l, :], DC)

                flip_x3(0)
                for l in range(G):
                    if l + 1 < G:
                        flip_x3(l + 1)
                    evacuated(it, "x3T", l)
                    project_T(it, "Q3", l, square["q3"], actT[:, l])
                    project(it, "V3", l, square["v3"], cT[:, l])
                    t, full = claim(it, "row", l)
                    pe.wait_ge(S["m1"], nth(it, l))
                    mm(t[:, 0:P], mask1_bf[:, l:l + 1].broadcast_to((P, P)), ident_bf[:, :],
                       start=True, stop=True).then_inc(full, 1)
                    project_T(it, "K3", l, square["k3"], cT[:, l])
                lengths(3)
                attention(it, 3, range(G), True, None, K2, K2_bf, V2, "K3_bf", "V3", DH16, "O3half")

                def flip_x4(l):
                    pe.wait_ge(S["x4"], nth(it, l))
                    flip(it, "x4T", l, res[:, l, :], DC)

                flip_x4(0)
                for l in range(G):
                    if l + 1 < G:
                        flip_x4(l + 1)
                    evacuated(it, "x4T", l)
                    project_T(it, "fc1", l, square["fc1"], actT[:, l])
                for l in range(G):
                    evacuated(it, "fc1", l)
                    project(it, "fc2", l, square["fc2"], fc1T[:, l])

                for l in range(G):
                    project_T(it, "K4", l, square["k4"], cT[:, l])
                    project(it, "V4", l, square["v4"], cT[:, l])

                def flip_x5(l):
                    pe.wait_ge(S["x5"], nth(it, l))
                    flip(it, "x5T", l, res[:, l, :], DC)

                flip_x5(0)
                for l in range(G):
                    if l + 1 < G:
                        flip_x5(l + 1)
                    evacuated(it, "x5T", l)
                    project_T(it, "Q4", l, square["q4"], actT[:, l])
                attention(it, 4, range(G), True, "causal", K2, K2_bf, V2, "K4_bf", "V4ones", DH16, "O4half")

                def flip_x6(l):
                    pe.wait_ge(S["x6"], nth(it, l))
                    flip(it, "x6T", l, res[:, l, :], DC)

                flip_x6(0)
                for l in range(G):
                    if l + 1 < G:
                        flip_x6(l + 1)
                    evacuated(it, "x6T", l)
                    for half in range(2):
                        t, full = claim(it, f"up{half}", l)
                        for k in range(FC // 2):
                            last = to_channels(t, k * P, w_up, (half * FC // 2 + k) * P, actT[:, l])
                        last.then_inc(full, 1)
                for l in range(G):
                    evacuated(it, "up0", l)
                    evacuated(it, "up1", l)
                    project(it, "down", l, w_down, gT[:, l], FC)

            with pe.Fori(0, ITERS) as it:
                stages(it)

        @block.scalar
        def _(act):
            run = nc.scalar.activation

            def filled(it, what, lane=0):
                b, use = job(it, what, lane)
                act.wait_ge(bank_full[b], use + 1)
                return bank[b], bank_read[b]

            def copy_out(it, what, lane, dst, n):
                t, read = filled(it, what, lane)
                nc.scalar.copy(dst.rearrange("p c k -> p (c k)"), t[:, 0:n]).then_inc(read, 1)

            def split_heads(it, what, lane):
                t, read = filled(it, what, lane)
                for j in range(2):
                    last = run(Q[:, lane, :, j, :], t[:, 0:D].rearrange("p (c k) -> p c k", c=DC), ACT.Copy,
                               scale=even_odd[:, j:j + 1])
                last.then_inc(read, 1)

            def values_out(it, what, lane, V, heads, dh, scale=1.0):
                t, read = filled(it, what, lane)
                run(V[:, lane, :, 0:dh], t[:, 0:D].rearrange("p (h e) -> p h e", h=heads), ACT.Copy,
                    scale=scale).then_inc(read, 1)

            def exponentials(it, a_, lanes, two, scale, half, bias=None):
                units = lanes_units(lanes)
                width = DC * (2 if two else 1) * P
                for n in range(len(units)):
                    act.wait_ge(S[f"sexp{a_}"], nth_unit(it, n))
                    if n >= 2:
                        l, u = units[n - 2]
                        if u:
                            filled(it, f"O{a_}", l)
                        else:
                            act.wait_ge(S[half], nth(it, l))
                    if bias is None:
                        e = run(weights[:, n % 2, :, 0:width], sexp[:, :, 0:width], ACT.Exp, scale=scale)
                    else:
                        e = run(weights[:, n % 2, :, 0:width], sexp[:, :, 0:width], ACT.Exp, scale=scale, bias=bias)
                    e.then_inc(S[f"weights{a_}"], 1)

            copy_out(0, "x0T", 0, actT[:, 0], D)
            copy_out(0, "c0T", 0, cT[:, 0], D)
            split_heads(0, "Q0", 0)
            copy_out(0, "K0", 0, K2[:, 0], D)
            values_out(0, "V0", 0, V2, H16, DH16)
            exponentials(0, 0, [0], True, 0.25, "O0half")
            act.wait_ge(S["wmamba_in"], 16 * 6)
            run(decay_rate, decay_rate, ACT.Exp).then_inc(S["rates"], 1)
            act.wait_ge(S["ready_weights"], 1)

            def stages(it):
                for l in range(G):
                    copy_out(it, "ctxT", l, cT[:, l], D)
                for l in range(G):
                    act.wait_ge(S["x1"], nth(it, l))
                    run(nrm[:, l, :], res[:, l, :], ACT.Square, accum_out=stat[:, l, 12:13]).then_inc(S["ss1"], 1)
                for l in range(G):
                    values_out(it, "V1", l, V1, H8, DH8)
                for l in range(G):
                    copy_out(it, "xhatT", l, actT[:, l], D)

                def mamba_inputs(l):
                    for half in range(2):
                        t, read = filled(it, f"xbc{half}", l)
                        n = XBC // 2
                        for k in range(n):
                            c = half * n + k
                            run(conv[:, l, c, :], t[:, k * P:(k + 1) * P], ACT.Identity,
                                scale=conv_w[:, c, TAPS - 1:TAPS], bias=conv_b[:, c:c + 1])
                        if half == 0:
                            nc.scalar.copy(dts[:, l, 0, :], t[:, n * P:n * P + MH])
                        nc.scalar.copy(raw[:, l, half * n:(half + 1) * n, TAPS - 1:],
                                       t[:, 0:n * P].rearrange("p (c k) -> p c k", c=n)).then_inc(read, 1)
                    t, read = filled(it, "z", l)
                    nc.scalar.copy(zs[:, l, :], t[:, :])
                    run(tz[:, l, :], t[:, :], ACT.Tanh, scale=0.5).then_inc(read, 1)

                def mamba_curves(l):
                    act.wait_ge(S["near0"], nth(it, l))
                    run(dts[:, l, 4, :], dts[:, l, 2, :], ACT.Exp).then_inc(S["edt"], 1)
                    act.wait_ge(S["conv"], nth(it, l))
                    run(raw[:, l, :, TAPS - 1:], conv[:, l, :, :], ACT.Tanh, scale=0.5).then_inc(S["tanh"], 1)

                mamba_inputs(0)
                for l in range(G):
                    if l + 1 < G:
                        mamba_inputs(l + 1)
                    mamba_curves(l)
                for l in range(G):
                    act.wait_ge(S["log_decay"], nth(it, l))
                    run(decay[:, l, :, :].rearrange("p (b h) k -> p b (h k)", b=2), sexp[:, :, :],
                        ACT.Exp).then_inc(S["decay"], 1)
                for l in range(G):
                    act.wait_ge(S["u"], nth(it, l))
                    run(dx[:, l, :], zs[:, l, :], ACT.Square, accum_out=stat[:, l, 12:13]).then_inc(S["ss2"], 1)
                for l in range(G):
                    copy_out(it, "uT", l, uT[:, l], INNER)

                copy_out(it, "xnT", 0, actT[:, 0], D)
                for l in range(G):
                    if l + 1 < G:
                        copy_out(it, "xnT", l + 1, actT[:, l + 1], D)
                    t, read = filled(it, "Q1", l)
                    for c in range(DC):
                        last = run(Q[:, l, c, 0, :], t[:, c * P:(c + 1) * P], ACT.Identity, bias=q1_bias[:, c:c + 1])
                    last.then_inc(read, 1)
                exponentials(it, 1, range(G), False, SCALE8, "O1half", pad_bias[:, :])
                for l in range(G):
                    copy_out(it, "oT", l, actT[:, l], D)

                copy_out(it, "x2T", 0, actT[:, 0], D)
                for l in range(G):
                    if l + 1 < G:
                        copy_out(it, "x2T", l + 1, actT[:, l + 1], D)
                    split_heads(it, "Q2", l)
                    copy_out(it, "K2", l, K2[:, l], D)
                    values_out(it, "V2", l, V2, H16, DH16)
                exponentials(it, 2, range(G), True, 0.25, "O2half")

                copy_out(it, "x3T", 0, actT[:, 0], D)
                for l in range(G):
                    if l + 1 < G:
                        copy_out(it, "x3T", l + 1, actT[:, l + 1], D)
                    split_heads(it, "Q3", l)
                    act.wait_ge(S["m1"], nth(it, l))
                    values_out(it, "V3", l, V2, H16, DH16, mask1[:, l, 1:2])
                    t, read = filled(it, "row", l)
                    nc.scalar.copy(row_mask[:, l, :], t[:, 0:P]).then_inc(read, 1)
                exponentials(it, 3, range(G), True, 0.25, "O3half")

                copy_out(it, "x4T", 0, actT[:, 0], D)
                for l in range(G):
                    if l + 1 < G:
                        copy_out(it, "x4T", l + 1, actT[:, l + 1], D)
                    t, read = filled(it, "fc1", l)
                    for c in range(DC):
                        last = run(fc1T[:, l, c, :], t[:, c * P:(c + 1) * P], ACT.Relu, bias=fc1_b[:, c:c + 1])
                    last.then_inc(read, 1)

                for l in range(G):
                    t, read = filled(it, "K4", l)
                    for c in range(DC):
                        last = run(K2[:, l, c, :], t[:, c * P:(c + 1) * P], ACT.Identity, bias=k4_b[:, c:c + 1])
                    last.then_inc(read, 1)
                copy_out(it, "x5T", 0, actT[:, 0], D)
                for l in range(G):
                    if l + 1 < G:
                        copy_out(it, "x5T", l + 1, actT[:, l + 1], D)
                    t, read = filled(it, "Q4", l)
                    for c in range(DC):
                        for j in range(2):
                            last = run(Q[:, l, c, j, :], t[:, c * P:(c + 1) * P], ACT.Identity,
                                       scale=even_odd[:, j:j + 1], bias=q4_bias[:, c, j:j + 1])
                    last.then_inc(read, 1)
                exponentials(it, 4, range(G), True, 0.25, "O4half")

                copy_out(it, "x6T", 0, actT[:, 0], D)
                for l in range(G):
                    if l + 1 < G:
                        copy_out(it, "x6T", l + 1, actT[:, l + 1], D)
                    for half in range(2):
                        t, read = filled(it, f"up{half}", l)
                        for k in range(FC // 2):
                            c = half * FC // 2 + k
                            last = run(gT[:, l, c, :], t[:, k * P:(k + 1) * P], ACT.Gelu, bias=up_b[:, c:c + 1])
                        last.then_inc(read, 1)

            with act.Fori(0, ITERS) as it:
                stages(it)

        @block.vector
        def _(dve):
            tt, ts, stt = nc.vector.tensor_tensor, nc.vector.tensor_scalar, nc.vector.scalar_tensor_tensor

            def filled(it, what, lane=0):
                b, use = job(it, what, lane)
                dve.wait_ge(bank_full[b], use + 1)
                return bank[b], bank_read[b]

            def evacuated(it, what, lane=0):
                b, use = job(it, what, lane)
                dve.wait_ge(bank_read[b], use + 1)

            def root_guess(l, step, src, scale, offset, done):
                step(ts(stat[:, l, 2:3], src, scale, offset, ALU.mult, ALU.add))
                step(ts(stat[:, l, 3:4].bitcast(I32), stat[:, l, 2:3].bitcast(I32), 1, None, ALU.logical_shift_right))
                ts(stat[:, l, 4:5].bitcast(I32), stat[:, l, 3:4].bitcast(I32), -1.0, MAGIC,
                   ALU.mult, ALU.add).then_inc(done, 1)

            def moments(l, step, done):
                step(nc.vector.bn_stats(bn[:, l, :], res[:, l, :]))
                step(nc.vector.bn_aggr(stat[:, l, 0:2], bn[:, l, :]))
                root_guess(l, step, stat[:, l, 1:2], 1.0, EPS, done)

            def normalise(it, l, root, done):
                dve.wait_ge(S[root], nth(it, l))
                ts(nrm[:, l, :], res[:, l, :], stat[:, l, 0:1], stat[:, l, 10:11],
                   ALU.subtract, ALU.mult).then_inc(S[done], 1)

            def maxima(it, a_, n, two):
                dve.wait_ge(S[f"smax{a_}"], nth_unit(it, n))
                heads = 4 if two else 2
                nc.vector.tensor_reduce(
                    neg_max[:, n % 2, 0:2 * heads].rearrange("p (b h) -> p b h", b=2),
                    smax[:, :, 0:heads * P].rearrange("p b (h k) -> p b h k", h=heads), AX_X, ALU.max,
                    negate=True).then_inc(S[f"maxima{a_}"], 1)

            def weighted(it, a_, l, step, heads, dh, dst, mask=None):
                t, read = filled(it, f"O{a_}", l)
                o = t[:, 0:heads * (dh + 1)].rearrange("p (h e) -> p h e", h=heads)
                step(nc.vector.reciprocal(rec[:, l, 0:heads], o[:, :, dh]))
                if mask is not None:
                    step(ts(rec[:, l, 0:heads], rec[:, l, 0:heads], mask, None, ALU.mult))
                tt(dst.rearrange("p (h e) -> p h e", h=heads), o[:, :, 0:dh],
                   rec[:, l, 0:heads].unsqueeze(2).broadcast_to((P, heads, dh)), ALU.mult).then_inc(read, 1)
                evacuated(it, f"O{a_}", l)

            def attention(it, a_, two, finish, later):
                for n in range(UNITS):
                    maxima(it, a_, n, two)
                    if n >= 3 and n % 2:
                        l = (n - 3) // 2
                        finish(l)
                        if l:
                            later(l - 1)
                finish(G - 1)
                later(G - 2)
                later(G - 1)

            step = Chain(dve, S["dve_first"])
            dve.wait_ge(S["const_in"], 16)
            nc.vector.memset(ones_bf[:, :], 1.0)
            nc.vector.tensor_copy(ident_bf[:, :], ident)
            nc.vector.tensor_copy(causal_bf[:, :], con("causal"))
            nc.vector.tensor_copy(causal_t_bf[:, :], con("causal_t")).then_inc(S["ready_consts"], 1)
            for n in range(2):
                maxima(0, 0, n, True)
            weighted(0, 0, 0, step, H16, DH16, att0[:, :])
            dve.wait_ge(S["wmamba_in"], 16 * 6)
            ts(keep_row[:, :], pad_u8[:, :], -1.0, 1.0, ALU.mult, ALU.add)
            ts(padding_bf[:, :], pad_u8[:, :], MASKED, None, ALU.mult)
            ts(pad_bias[:, :], pad_col_u8[:, :], MASKED * SCALE8, None, ALU.mult)
            ts(skip, skip, 0.5, None, ALU.mult)
            for c in range(DC):
                ts(w_in[:, c, :], w_in[:, c, :], m_norm[:, c:c + 1], None, ALU.mult)
            for c in range(IC):
                ts(w_out[:, c, :], w_out[:, c, :], g_norm[:, c:c + 1], None, ALU.mult)
            for m in range(DC):
                t, read = filled(0, f"bias{m}")
                nc.vector.tensor_copy(q1_bias[:, m:m + 1], t[:, 0:1]).then_inc(read, 1)
            for c in range(DC):
                ts(square["q1"][:, c, :], square["q1"][:, c, :], ca_w[:, c:c + 1], None, ALU.mult)
            dve.wait_ge(S["rates"], 1)
            ts(decay_rate, decay_rate, -1.0, None, ALU.mult)
            dve.wait_ge(S["w2_in"], 16 * 8)
            dve.wait_ge(S["w3_in"], 16 * 5)
            dve.wait_ge(S["pads_zero"], 1)
            step(tt(q4_bias[:, :, :], q4_b.unsqueeze(2).broadcast_to((P, DC, 2)),
                    even_odd.unsqueeze(1).broadcast_to((P, DC, 2)), ALU.mult))
            nc.vector.memset(stat[:, :, :], 1.0).then_inc(S["ready_weights"], 1)
            dve.wait_ge(S["ready_weights"], 1)

            def stages(it):
                step = Chain(dve, S["dve_step"])
                dve.wait_ge(S["x_in"], it * 16 + 16)
                for l in range(G):
                    tt(res[:, l, :], x_in[:, l, :], att0[:, :], ALU.add).then_inc(S["x1"], 1)
                for l in range(G):
                    dve.wait_ge(S["ss1"], nth(it, l))
                    root_guess(l, step, stat[:, l, 12:13], 1.0 / D, EPS, S["seed1"])
                for l in range(G):
                    t, read = filled(it, "K1", l)
                    tt(K1[:, l, :, :], t[:, 0:D].rearrange("p (c k) -> p c k", c=DC),
                       keep_row[:, :].unsqueeze(1).broadcast_to((P, DC, P)), ALU.mult).then_inc(read, 1)
                for l in range(G):
                    dve.wait_ge(S["rstd1"], nth(it, l))
                    ts(nrm[:, l, :], res[:, l, :], stat[:, l, 10:11], None, ALU.mult).then_inc(S["xhat"], 1)

                def convolve(l):
                    n = XBC // 2
                    for half in range(2):
                        evacuated(it, f"xbc{half}", l)
                        for k in range(TAPS - 1):
                            for c in range(half * n, (half + 1) * n):
                                last = stt(conv[:, l, c, :], raw[:, l, c, k:k + P], conv_w[:, c, k:k + 1],
                                           conv[:, l, c, :], ALU.mult, ALU.add)
                            if half == 0 or k < TAPS - 2:
                                step(last)
                    last.then_inc(S["conv"], 1)

                def silu(l):
                    dve.wait_ge(S["tanh"], nth(it, l))
                    stt(conv[:, l, :, :], raw[:, l, :, TAPS - 1:], 1.0, conv[:, l, :, :],
                        ALU.add, ALU.mult).then_inc(S["xbc"], 1)

                def softplus(l):
                    def d(k):
                        return dts[:, l, k, :]
                    dve.wait_ge(S["edt"], nth(it, l))
                    step(ts(d(5), d(4), 2.0, None, ALU.add))
                    step(nc.vector.reciprocal(d(6), d(5)))
                    step(tt(d(7), d(4), d(6), ALU.mult))
                    step(tt(d(8), d(7), d(7), ALU.mult))
                    step(ts(d(9), d(8), 1.0 / (2 * LOG1P_TERMS - 1), None, ALU.mult))
                    for k in range(LOG1P_TERMS - 2, 0, -1):
                        step(stt(d(9), d(9), 1.0 / (2 * k + 1), d(8), ALU.add, ALU.mult))
                    step(stt(d(9), d(9), 1.0, d(7), ALU.add, ALU.mult))
                    step(stt(d(10), d(9), 2.0, d(3), ALU.mult, ALU.add))
                    ts(d(11), d(10), 0.5, None, ALU.mult).then_inc(S["dt"], 1)

                convolve(0)
                for l in range(G):
                    softplus(l)
                    if l + 1 < G:
                        convolve(l + 1)
                    silu(l)

                def token_pairs(l):
                    t, read = filled(it, "CB", l)
                    tt(state_gate[:, l, :], t[:, 0:P], gate_mask, ALU.mult).then_inc(read, 1)
                    t, read = filled(it, "xh", l)
                    x3 = t[:, :].rearrange("p (h e) -> p h e", h=MH)
                    tt(dbx[:, l, :].rearrange("p (h e) -> p h e", h=MH), x3,
                       dts[:, l, 11, :].unsqueeze(2).broadcast_to((P, MH, MD)), ALU.mult)
                    tt(dx[:, l, :].rearrange("p (h e) -> p h e", h=MH), x3,
                       skip.unsqueeze(2).broadcast_to((P, MH, MD)), ALU.mult).then_inc(read, 1)

                def decayed(l):
                    dve.wait_ge(S["decay"], nth(it, l))
                    evacuated(it, "CB", l)
                    tt(decay[:, l, :, :], decay[:, l, :, :],
                       state_gate[:, l, :].unsqueeze(1).broadcast_to((P, MH, P)), ALU.mult).then_inc(S["M"], 1)

                token_pairs(0)
                for l in range(G):
                    if l + 1 < G:
                        token_pairs(l + 1)
                    decayed(l)

                def gate(l):
                    t, read = filled(it, "Y", l)
                    evacuated(it, "xh", l)
                    dve.wait_ge(S["gated"], nth(it, l))
                    tt(tz[:, l, :], t[:, :], dx[:, l, :], ALU.add).then_inc(read, 1)
                    evacuated(it, "Y", l)
                    tt(zs[:, l, :], tz[:, l, :], zs[:, l, :], ALU.mult).then_inc(S["u"], 1)

                def gate_norm(l):
                    dve.wait_ge(S["ss2"], nth(it, l))
                    root_guess(l, step, stat[:, l, 12:13], 1.0 / INNER, 4.0 * EPS, S["seed2"])

                gate(0)
                for l in range(G):
                    if l + 1 < G:
                        gate(l + 1)
                    gate_norm(l)

                def mamba_out(l):
                    dve.wait_ge(S["rstd2"], nth(it, l))
                    t, read = filled(it, "proj", l)
                    stt(res[:, l, :], t[:, 0:D], stat[:, l, 10:11], res[:, l, :], ALU.mult, ALU.add).then_inc(read, 1)
                    evacuated(it, "proj", l)
                    moments(l, step, S["seed3"])

                mamba_out(0)
                for l in range(G):
                    if l + 1 < G:
                        mamba_out(l + 1)
                    normalise(it, l, "rstd3", "xn")

                attention(it, 1, False, lambda l: weighted(it, 1, l, step, H8, DH8, att[:, l, :]), lambda l: None)
                for l in range(G):
                    t, read = filled(it, "Wo", l)
                    tt(res[:, l, :], t[:, 0:D], res[:, l, :], ALU.add).then_inc(read, 1)
                    evacuated(it, "Wo", l)
                    step(nc.vector.tensor_reduce(mask0[:, l, 0:1], res[:, l, :], AX_X, ALU.max, apply_absolute_value=True))
                    step(ts(mask0[:, l, 1:2], mask0[:, l, 0:1], 0.0, None, ALU.is_gt))

                def lengths(a_):
                    for l in range(G):
                        t, read = filled(it, f"e{a_}", l)
                        ts(nonzero[:, l, :], t[:, 0:H16], 0.0, None, ALU.not_equal).then_inc(read, 1)
                    for l in range(G):
                        t, read = filled(it, f"n{a_}", l)
                        ts(keep[:, l, :], t[:, 0:H16], index, None, ALU.is_gt).then_inc(read, 1)

                def add_attention(a_, mask, seed):
                    def finish(l):
                        weighted(it, a_, l, step, H16, DH16, att[:, l, :], mask and mask(l))
                        step(tt(res[:, l, :], att[:, l, :], res[:, l, :], ALU.add))
                        moments(l, step, S[seed])
                    return finish

                lengths(2)
                attention(it, 2, True, add_attention(2, lambda l: mask0[:, l, 1:2], "seed4"),
                          lambda l: normalise(it, l, "rstd4", "t4"))

                def token_mask(l):
                    dve.wait_ge(S["x3"], nth(it, l))
                    step(nc.vector.tensor_reduce(mask1[:, l, 0:1], res[:, l, :], AX_X, ALU.max, apply_absolute_value=True))
                    step(ts(mask1[:, l, 1:2], mask1[:, l, 0:1], 0.0, None, ALU.is_gt))
                    ts(mask1_bf[:, l:l + 1], mask1[:, l, 0:1], 0.0, None, ALU.is_gt).then_inc(S["m1"], 1)

                token_mask(0)
                for l in range(G):
                    if l + 1 < G:
                        token_mask(l + 1)
                    evacuated(it, "row", l)
                    t, read = filled(it, "K3", l)
                    tt(K2[:, l, :, :], t[:, 0:D].rearrange("p (c k) -> p c k", c=DC),
                       row_mask[:, l, :].unsqueeze(1).broadcast_to((P, DC, P)), ALU.mult).then_inc(read, 1)
                lengths(3)
                attention(it, 3, True, add_attention(3, lambda l: mask1[:, l, 1:2], "seed5"),
                          lambda l: normalise(it, l, "rstd5", "t5"))

                def feed_forward(l):
                    t, read = filled(it, "fc2", l)
                    tt(att[:, l, :], t[:, 0:D], rows["fc2"], ALU.add).then_inc(read, 1)
                    evacuated(it, "fc2", l)
                    step(stt(res[:, l, :], att[:, l, :], mask0[:, l, 1:2], res[:, l, :], ALU.mult, ALU.add))
                    moments(l, step, S["seed6"])

                def values_biased(l):
                    t, read = filled(it, "V4", l)
                    tt(V2[:, l, :, 0:DH16], t[:, 0:D].rearrange("p (h e) -> p h e", h=H16),
                       rows["v4"].rearrange("p (h e) -> p h e", h=H16), ALU.add).then_inc(read, 1)

                feed_forward(0)
                for l in range(1, G):
                    feed_forward(l)
                    normalise(it, l - 1, "rstd6", "t6")
                for l in range(G - 1):
                    values_biased(l)
                normalise(it, G - 1, "rstd6", "t6")
                values_biased(G - 1)

                attention(it, 4, True, add_attention(4, None, "seed7"), lambda l: normalise(it, l, "rstd7", "t7"))
                dve.wait_ge(S["stored"], it * 16 + 16)
                for l in range(G):
                    t, read = filled(it, "down", l)
                    dve.wait_ge(S["plus"], nth(it, l))
                    tt(result[:, l, :], t[:, 0:D], plus[:, l, :], ALU.add).then_inc(read, 1)

            with dve.Fori(0, ITERS) as it:
                stages(it)

        @block.gpsimd
        def _(pool):
            tt, ts, copy = nc.gpsimd.tensor_tensor, nc.gpsimd.tensor_scalar, nc.gpsimd.tensor_copy

            def wait_for(semaphore, value):
                pool.wait_ge(semaphore, value)
                pool.sem_inc(S["pool_waits"], 1)

            def evacuated(it, what, lane=0):
                b, use = job(it, what, lane)
                wait_for(bank_read[b], use + 1)

            nc.gpsimd.memset(V2[:, 0, :, DH16], 1.0).then_inc(S["ones_col"], 1)
            nc.gpsimd.memset(V1[:, :, :, DH8], 1.0).then_inc(S["ones_col"], 1)
            nc.gpsimd.memset(raw[:, :, :, 0:TAPS - 1], 0.0).then_inc(S["pads_zero"], 1)
            evacuated(0, "Q0")
            copy(Q_bf[:, 0], Q[:, 0]).then_inc(S["q0_bf"], 1)
            evacuated(0, "K0")
            copy(K2_bf[:, 0], K2[:, 0]).then_inc(S["k0_bf"], 1)
            pool.wait_ge(S["ready_weights"], 1)

            def stages(it):
                step = Chain(pool, S["pool_step"])

                def root(l, seed, done):
                    wait_for(S[seed], nth(it, l))
                    step(ts(stat[:, l, 5:6], stat[:, l, 2:3], 0.5, None, ALU.mult))
                    y = stat[:, l, 4:5]
                    for k in range(NEWTON):
                        step(ts(stat[:, l, 6:7], y, y, stat[:, l, 5:6], ALU.mult, ALU.mult))
                        step(ts(stat[:, l, 7:8], stat[:, l, 6:7], -1.0, 1.5, ALU.mult, ALU.add))
                        last = ts(stat[:, l, 8 + k:9 + k], y, stat[:, l, 7:8], None, ALU.mult)
                        if k + 1 < NEWTON:
                            step(last)
                        y = stat[:, l, 8 + k:9 + k]
                    last.then_inc(S[done], 1)

                def gain(l, t_ready, g, b, done):
                    wait_for(S[t_ready], nth(it, l))
                    step(tt(nrm[:, l, :], nrm[:, l, :], rows[g], ALU.mult))
                    tt(res[:, l, :], nrm[:, l, :], rows[b], ALU.add).then_inc(S[done], 1)

                def norms(seed, rstd, t_ready, g, b, done, after=None):
                    root(0, seed, rstd)
                    for l in range(G):
                        if l + 1 < G:
                            root(l + 1, seed, rstd)
                        gain(l, t_ready, g, b, done)
                        if after:
                            after(l)

                for l in range(G):
                    root(l, "seed1", "rstd1")
                for l in range(G):
                    evacuated(it, "K1", l)
                    copy(K1_bf[:, l], K1[:, l]).then_inc(S["K1_bf"], 1)

                def near0(l):
                    def d(k):
                        return dts[:, l, k, :]
                    evacuated(it, "xbc0", l)
                    step(tt(d(0), d(0), dt_bias, ALU.add))
                    step(ts(d(3), d(0), 0.0, None, ALU.max))
                    step(ts(d(1), d(3), -2.0, None, ALU.mult))
                    tt(d(2), d(0), d(1), ALU.add).then_inc(S["near0"], 1)

                def gated(l):
                    evacuated(it, "z", l)
                    step(ts(tz[:, l, :], tz[:, l, :], 1.0, None, ALU.add))
                    tt(zs[:, l, :], tz[:, l, :], zs[:, l, :], ALU.mult).then_inc(S["gated"], 1)

                def log_decays(l):
                    wait_for(S["dt"], nth(it, l))
                    step(tt(dts[:, l, 5, :], dts[:, l, 10, :], decay_rate, ALU.mult))
                    tt(decay[:, l, :, :], after.unsqueeze(1).broadcast_to((P, MH, P)),
                       dts[:, l, 5, :].unsqueeze(2).broadcast_to((P, MH, P)), ALU.mult).then_inc(S["am"], 1)

                near0(0)
                for l in range(G):
                    if l + 1 < G:
                        near0(l + 1)
                    log_decays(l)
                    gated(l)
                for l in range(G):
                    root(l, "seed2", "rstd2")
                for l in range(G):
                    root(l, "seed3", "rstd3")
                for l in range(G):
                    evacuated(it, "Q1", l)
                    copy(Q_bf[:, l, :, 0, :], Q[:, l, :, 0, :]).then_inc(S["Q1_bf"], 1)

                def narrow(a_, first):
                    for l in range(G):
                        evacuated(it, f"Q{a_}", l)
                        if first:
                            tt(q_first[:, l, :, :].rearrange("p c (r j) -> p c r j", j=2),
                               Q[:, l, :, :, 0].unsqueeze(2).broadcast_to((P, DC, 4, 2)),
                               head8.rearrange("p (r j) -> p r j", j=2).unsqueeze(1).broadcast_to((P, DC, 4, 2)),
                               ALU.mult).then_inc(S[f"q{a_}_first"], 1)
                        copy(Q_bf[:, l], Q[:, l]).then_inc(S[f"Q{a_}_bf"], 1)
                        evacuated(it, f"K{a_}", l)
                        copy(K2_bf[:, l], K2[:, l]).then_inc(S[f"K{a_}_bf"], 1)

                def drop(a_):
                    for l in range(G):
                        evacuated(it, f"V{a_}", l)
                        evacuated(it, f"n{a_}", l)
                        step(tt(V2[:, l, :, 0:DH16], V2[:, l, :, 0:DH16],
                                keep[:, l, :].unsqueeze(2).broadcast_to((P, H16, DH16)), ALU.mult))
                        copy(V2[:, l, :, DH16], keep[:, l, :]).then_inc(S[f"V{a_}"], 1)

                narrow(2, True)
                drop(2)
                norms("seed4", "rstd4", "t4", "g1", "b1", "x3")
                narrow(3, True)
                drop(3)
                norms("seed5", "rstd5", "t5", "g2", "b2", "x4")
                norms("seed6", "rstd6", "t6", "g3", "b3", "x5")
                for l in range(G):
                    evacuated(it, "V4", l)
                    nc.gpsimd.memset(V2[:, l, :, DH16], 1.0).then_inc(S["V4ones"], 1)
                narrow(4, False)

                def plus_bias(l):
                    wait_for(S["x6"], nth(it, l))
                    tt(plus[:, l, :], res[:, l, :], rows["down"], ALU.add).then_inc(S["plus"], 1)

                norms("seed7", "rstd7", "t7", "g4", "b4", "x6", plus_bias)

            with pool.Fori(0, ITERS) as it:
                stages(it)


def constants():
    import numpy as np

    p, k = np.arange(P)[:, None], np.arange(P)[None, :]
    c = {
        "ident": p == k,
        "before": p <= k,
        "gate": 0.25 * (p <= k),
        "after": p > k,
        "causal": np.where(k > p, MASKED, 0),
        "causal_t": np.where(p > k, MASKED, 0),
        "even_odd": (p // DH16) % 2 == np.arange(2)[None, :],
        "head": p // DH16 == np.arange(8)[None, :],
        "index": p,
    }
    return np.concatenate([np.asarray(c[n], np.float32) for n in CONST_COLS], axis=1)


def kernel(**inputs):
    import numpy as np
    import concourse.bacc as bacc
    from concourse.bass_utils import run_bass_kernel_spmd

    def arr(name):
        return np.asarray(inputs[name])

    def by_head(name):
        w = arr(name)
        return w.transpose(1, 0, 2).reshape(w.shape[1], -1)

    a = {"x": arr("x"), "ctx_1024": arr("ctx_1024"), "const": constants(), "pad": arr("mask_1xS2_bf0").view(np.int32)}
    for n in "qkv":
        a[n + "0"] = arr(f"L0_xattn_W{n}").T
        a[n + "1"] = arr(f"L1_xattn_W{n}")
        a[n + "2"] = by_head(f"L2_xattn_W{n}1")
        a[n + "3"] = by_head(f"L2_xattn_W{n}2")
        a[n + "4"] = arr(f"L3_xattn_W{n}").T
    a["o1"] = arr("L1_xattn_Wo")
    a["in_proj"], a["out_proj"] = arr("L1_xattn_in_proj_w"), arr("L1_xattn_out_proj_w")
    a["fc1"], a["fc2"] = arr("L2_xattn_fc1_w").T, arr("L2_xattn_fc2_w").T
    a["up"], a["down"] = arr("L3_xattn_W1").T, arr("L3_xattn_W2").T
    vectors = dict(
        m_norm="L1_xattn_m_norm_w", g_norm="L1_xattn_gnorm_w", conv_w="L1_xattn_conv_w", conv_b="L1_xattn_conv_b",
        ca_w="L1_xattn_ca_ln_w", ca_b="L1_xattn_ca_ln_b", fc1_b="L2_xattn_fc1_b", q4_b="L3_xattn_bq",
        k4_b="L3_xattn_bk", up_b="L3_xattn_b1")
    a["vectors"] = np.concatenate(
        [arr(vectors[n]).reshape(-1, P, arr(vectors[n]).size // len(arr(vectors[n])))
         .transpose(1, 0, 2).reshape(P, VECTORS[n]) for n in VECTORS], axis=1)
    rows = dict(
        g1="L2_xattn_ln1_g", b1="L2_xattn_ln1_b", g2="L2_xattn_ln2_g", b2="L2_xattn_ln2_b", g3="L2_xattn_ln3_g",
        b3="L2_xattn_ln3_b", g4="L3_xattn_ln_g", b4="L3_xattn_ln_b", fc2="L2_xattn_fc2_b", v4="L3_xattn_bv",
        down="L3_xattn_b2", dt_bias="L1_xattn_dt_bias", A_log="L1_xattn_A_log", D_skip="L1_xattn_D_skip")
    a["rows"] = np.concatenate([arr(rows[n]) for n in ROWS])

    nc = bacc.Bacc("TRN2", target_bir_lowering=False, num_devices=1)
    arrays, views = {}, {}
    for n, v in a.items():
        v = np.ascontiguousarray(v)
        arrays["in_" + n] = v
        views[n] = nc.dram_tensor("in_" + n, v.shape, mybir.dt.from_np(v.dtype), kind="ExternalInput").ap()
    out = nc.dram_tensor("out_0", (B, P, D), F32, kind="ExternalOutput").ap()
    decoder_stack(nc, views, out)
    r = run_bass_kernel_spmd(nc, [arrays], core_ids=[0])
    return r.results[0]["out_0"]
```

```python
from contextlib import ExitStack

import concourse.bass as bass
from concourse import mybir

F32 = mybir.dt.float32
BF16 = mybir.dt.bfloat16
I32 = mybir.dt.int32
U8 = mybir.dt.uint8
ALU = mybir.AluOpType
ACT = mybir.ActivationFunctionType
AX_X = mybir.AxisListType.X

P = 128
B = 32
D = 256
DC = D // P
G = 4
ITERS = B // G
INNER = 512
IC = INNER // P
STATE = 128
MH = 8
MD = INNER // MH
TAPS = 4
XBC = (INNER + 2 * STATE) // P
BCH, CCH = XBC - 2, XBC - 1
IN_PROJ = 2 * INNER + 2 * STATE + MH
FF = 1024
FC = FF // P
H16, DH16 = 16, 16
H8, DH8 = 8, 32
EPS = 1e-5
MASKED = -float(2 ** 30)
SCALE8 = 0.1767766922712326
MAGIC = float(0x5F3759DF)
NEWTON = 3
LOG1P_TERMS = 8
HEADS = 4
PARTS = {0: 4, 1: 2, 2: 4, 3: 4, 4: 4}
SCORE_BANKS = 3
SHIFTED_BUFFERS = 4
WEIGHT_BUFFERS = 4

CONST_COLS = dict(ident=P, before=P, gate=P, after=P, causal=P, head16=8, head32=4, index=1)
CONST_AT = {n: sum(list(CONST_COLS.values())[:i]) for i, n in enumerate(CONST_COLS)}
CONST_WIDTH = sum(CONST_COLS.values())
VECTORS = dict(m_norm=DC, g_norm=IC, conv_w=XBC * TAPS, conv_b=XBC, ca_w=DC, ca_b=DC, fc1_b=DC, q4_b=DC, k4_b=DC, up_b=FC)
VECTOR_AT = {n: sum(list(VECTORS.values())[:i]) for i, n in enumerate(VECTORS)}
VECTOR_WIDTH = sum(VECTORS.values())
ROWS = dict(g1=D, b1=D, g2=D, b2=D, g3=D, b3=D, g4=D, b4=D, fc2=D, v4=D, down=D, dt_bias=MH, A_log=MH, D_skip=MH)
ROW_AT = {n: sum(list(ROWS.values())[:i]) for i, n in enumerate(ROWS)}
ROW_WIDTH = sum(ROWS.values())

def ring_jobs():
    jobs = [("ctxT", l) for l in range(G)]
    jobs += [(w, l) for l in range(G) for w in ("K1", "V1")]
    jobs += [("xhatT", l) for l in range(G)]
    jobs += [(w, l) for l in range(G) for w in ("xbc0", "xbc1", "z")]
    jobs += [(w, l) for l in range(G) for w in ("CB", "xh")]
    jobs += [("Y", l) for l in range(G)] + [("uT", l) for l in range(G)] + [("proj", l) for l in range(G)]
    jobs += pipelined("xnT", ["Q1"])
    jobs += [("O1", l) for l in range(G)]
    jobs += pipelined("oT", ["Wo"])
    jobs += pipelined("x2T", ["Q2", "K2", "V2"])
    jobs += [("e2", l) for l in range(G)] + [("n2", l) for l in range(G)] + [("O2", l) for l in range(G)]
    jobs += pipelined("x3T", ["Q3", "V3", "row", "K3"])
    jobs += [("e3", l) for l in range(G)] + [("n3", l) for l in range(G)] + [("O3", l) for l in range(G)]
    jobs += pipelined("x4T", ["fc1"])
    jobs += [("fc2", l) for l in range(G)]
    jobs += [(w, l) for l in range(G) for w in ("K4", "V4")]
    jobs += pipelined("x5T", ["Q4"])
    jobs += [("O4", l) for l in range(G)]
    jobs += pipelined("x6T", ["up0", "up1"])
    jobs += [("down", l) for l in range(G)]
    return jobs


def pipelined(first, then):
    order = [(first, 0)]
    for l in range(G):
        if l + 1 < G:
            order.append((first, l + 1))
        order += [(w, l) for w in then]
    return order


BANKS = 4
JOBS = ring_jobs()
JOB_AT = {job: n for n, job in enumerate(JOBS)}
assert len(JOB_AT) == len(JOBS) and len(JOBS) % BANKS == 0
USES = len(JOBS) // BANKS
FIRST_JOBS = ["x0T", "c0T", "Q0", "K0", "V0", "O0", "bias0", "bias1"]
FIRST_USES = len(FIRST_JOBS) // BANKS


def job(it, what, lane=0):
    if what in FIRST_JOBS:
        n = FIRST_JOBS.index(what)
        return n % BANKS, n // BANKS
    n = JOB_AT[what, lane]
    return n % BANKS, it * USES + (FIRST_USES + n // BANKS)


def nth(it, lane):
    return it * G + (lane + 1)


FIRST_PARTS = PARTS[0]
PART_AT = {a_: G * sum(PARTS[b] for b in range(1, a_)) for a_ in range(1, 5)}


def part(it, a_, n):
    if a_ == 0:
        return n
    return it * (G * sum(PARTS[b] for b in range(1, 5))) + (FIRST_PARTS + PART_AT[a_] + n)


def keyed(it, a_, l):
    return 1 if a_ == 0 else it * 4 * G + (1 + (a_ - 1) * G + l + 1)


class Chain:

    def __init__(self, eng, sem):
        self.eng, self.sem, self.count = eng, sem, 0
        eng.sem_clear(sem)

    def __call__(self, instruction):
        self.count += 1
        instruction.then_inc(self.sem, 1)
        self.eng.wait_ge(self.sem, self.count)


def decoder_stack(nc, a, out):
    ctx = ExitStack()
    with ctx:
        def sb(name, shape, dt=F32):
            return ctx.enter_context(nc.sbuf_tensor(name, shape, dt))

        def pb(name, shape):
            return ctx.enter_context(nc.psum_tensor(name, shape, F32))

        def sem(name):
            return ctx.enter_context(nc.semaphore(name))

        const = sb("const", [P, CONST_WIDTH])

        def con(name):
            return const[:, CONST_AT[name]:CONST_AT[name] + CONST_COLS[name]]

        ident, before, gate_mask, after = con("ident"), con("before"), con("gate"), con("after")
        head16, head32, index = con("head16"), con("head32"), con("index")
        ident_bf = sb("ident_bf", [P, P], BF16)
        ones_bf = sb("ones_bf", [P, P], BF16)
        causal_bf = sb("causal_bf", [P, P], BF16)

        w_in = sb("w_in", [P, DC, IN_PROJ])
        w_out = sb("w_out", [P, IC, D])
        square = {n: sb(f"w_{n}", [P, DC, D]) for n in (
            "q1", "k1", "v1", "o1", "q2", "k2", "v2", "q3", "k3", "v3", "fc1", "fc2", "q4", "k4", "v4")}
        w_up = sb("w_up", [P, DC, FF])
        w_down = sb("w_down", [P, FC, D])
        vectors = sb("vectors", [P, VECTOR_WIDTH])

        def vec(name):
            return vectors[:, VECTOR_AT[name]:VECTOR_AT[name] + VECTORS[name]]

        m_norm, g_norm, conv_b, ca_w, ca_b = (vec(n) for n in ("m_norm", "g_norm", "conv_b", "ca_w", "ca_b"))
        conv_w = vec("conv_w").rearrange("p (c k) -> p c k", c=XBC)
        fc1_b, q4_b, k4_b, up_b = (vec(n) for n in ("fc1_b", "q4_b", "k4_b", "up_b"))
        q1_bias = sb("q1_bias", [P, DC])
        row_all = sb("row_all", [P, ROW_WIDTH])
        rows = {n: row_all[:, ROW_AT[n]:ROW_AT[n] + ROWS[n]] for n in ROWS}
        dt_bias, decay_rate, skip = rows["dt_bias"], rows["A_log"], rows["D_skip"]
        pad_u8 = sb("pad_u8", [P, P], U8)
        keep_row = sb("keep_row", [P, P])
        padding_bf = sb("padding_bf", [P, P], BF16)

        x_in = sb("x_in", [P, G, D])
        c_in = sb("c_in", [P, G, D])
        cT = sb("cT", [P, G, DC, P])
        att0 = sb("att0", [P, D])
        res = sb("res", [P, G, D])
        nrm = sb("nrm", [P, G, D])
        actT = sb("actT", [P, G, DC, P])
        raw = sb("raw", [P, G, XBC, TAPS - 1 + P])
        att = sb("att", [P, G, D])
        result = sb("result", [P, G, D])
        fc1T = sb("fc1T", [P, G, DC, P])
        plus = fc1T[:, :, :, :].rearrange("p g c k -> p g (c k)")
        state_gate = sb("state_gate", [P, G, P])
        stat = sb("stat", [P, G, 16])
        bn = sb("bn", [P, G, 6])
        dts = sb("dts", [P, G, 12, MH])
        rec = sb("rec", [P, G, H16])
        mask0 = sb("mask0", [P, G, 2])
        mask1 = sb("mask1", [P, G, 2])
        mask1_bf = sb("mask1_bf", [P, G], BF16)
        row_mask = sb("row_mask", [P, G, P])
        q_first = sb("q_first", [P, G, DC, 8])
        nonzero = sb("nonzero", [P, G, H16], BF16)
        keep = sb("keep", [P, G, H16])
        neg_max = sb("neg_max", [P, 2, HEADS])
        K1 = sb("K1", [P, G, DC, P])
        V1 = sb("V1", [P, G, H8, DH8 + 1])
        V2 = sb("V2", [P, G, H16, DH16 + 1])

        MAMBA = dict(decay=G * MH * P, conv=G * XBC * P, dbx=G * INNER, dx=G * INNER, zs=G * INNER, tz=G * INNER)
        space = sb("space", [P, sum(MAMBA.values())])
        at, mamba = 0, {}
        for n, width in MAMBA.items():
            mamba[n] = space[:, at:at + width]
            at += width
        decay = mamba["decay"].rearrange("p (g h k) -> p g h k", g=G, h=MH)
        conv = mamba["conv"].rearrange("p (g c k) -> p g c k", g=G, c=XBC)
        dbx, dx, zs, tz = (mamba[n].rearrange("p (g n) -> p g n", g=G) for n in ("dbx", "dx", "zs", "tz"))
        uT = mamba["tz"].rearrange("p (g c k) -> p g c k", g=G, c=IC)
        keys32 = space[:, 0:G * DC * 4 * P].rearrange("p (g c h k) -> p g c h k", g=G, c=DC, h=4)
        keys16 = space[:, 0:G * DC * 8 * P].rearrange("p (g c h k) -> p g c h k", g=G, c=DC, h=8)
        Q = space[:, G * DC * 8 * P:G * DC * 9 * P].rearrange("p (g c k) -> p g c k", g=G, c=DC)
        assert G * DC * 9 * P <= MAMBA["decay"] + MAMBA["conv"] + MAMBA["dbx"]
        shifted = mamba["dx"].rearrange("p (s n) -> p s n", s=SHIFTED_BUFFERS)
        weights = mamba["zs"].rearrange("p (s n) -> p s n", s=WEIGHT_BUFFERS)
        K2 = mamba["tz"][:, 0:G * D].rearrange("p (g c k) -> p g c k", g=G, c=DC)
        gT = decay
        w0 = {n: mamba["conv"][:, i * DC * D:(i + 1) * DC * D].rearrange("p (c n) -> p c n", c=DC)
              for i, n in enumerate(("q0", "k0", "v0"))}

        bank = [pb(f"ring{i}", [P, 512]) for i in range(BANKS)]
        score = pb("score", [P, SCORE_BANKS, 512])
        turned = pb("turned", [P, 512])

        bank_full = [sem(f"bank_full{i}") for i in range(BANKS)]
        bank_read = [sem(f"bank_read{i}") for i in range(BANKS)]
        S = {n: sem(n) for n in (
            "const_in w0_in wmamba_in w1_in w2_in w3_in x_in c_in stored "
            "ready_consts ready_weights ones_col pads_zero rates "
            "dve_first pool_first act_first "
            "dve_step pool_step pool_waits "
            "x1 ss1 seed1 rstd1 xhat near0 edt dt am conv tanh xbc gated "
            "log_decay decay M u ss2 seed2 rstd2 seed3 rstd3 xn "
            "q2_first keep2 V2 seed4 rstd4 t4 x3 m1 q3_first keep3 V3 seed5 rstd5 t5 x4 "
            "seed6 rstd6 t6 x5 V4ones seed7 rstd7 t7 x6 plus "
            "keys_dve keys_act keys_pool scores shifted exps turned weights").split()}

        x_v = a["x"].rearrange("(i g) t d -> i t g d", g=G)
        c_v = a["ctx_1024"].rearrange("(i g) t d -> i t g d", g=G)
        o_v = out.rearrange("(i g) t d -> i t g d", g=G)
        block = ctx.enter_context(nc.Block())

        def lanes_parts(a_, lanes):
            return [(l, t) for l in lanes for t in range(PARTS[a_])]

        SHARE16 = dict(dve=range(0, 4), act=range(4, 6), pool=range(6, 8))
        SHARE32 = dict(dve=range(0, 2), act=range(2, 3), pool=range(3, 4))

        @block.sync
        def _(sp):
            def chunks(name):
                return a[name].rearrange("(c p) n -> p c n", p=P)

            sp.sem_inc(S["stored"], 16)
            sp.dma_start(const[:, :], a["const"]).then_inc(S["const_in"], 16)
            sp.dma_start(x_in[:, :, :], x_v[0]).then_inc(S["x_in"], 16)
            sp.dma_start(c_in[:, :, :], c_v[0]).then_inc(S["c_in"], 16)
            for n in ("q0", "k0", "v0"):
                sp.dma_start(w0[n], chunks(n)).then_inc(S["w0_in"], 16)
            for dst, src in ((w_in[:, :, :], chunks("in_proj")), (w_out[:, :, :], chunks("out_proj")),
                             (vectors[:, :], a["vectors"]), (row_all[:, :], a["rows"].partition_broadcast(P)),
                             (pad_u8[:, :], a["pad"].bitcast(U8)[0].partition_broadcast(P))):
                sp.dma_start(dst, src).then_inc(S["wmamba_in"], 16)
            for n in ("q1", "k1", "v1", "o1"):
                sp.dma_start(square[n][:, :, :], chunks(n)).then_inc(S["w1_in"], 16)
            for n in ("q2", "k2", "v2", "q3", "k3", "v3", "fc1", "fc2"):
                sp.dma_start(square[n][:, :, :], chunks(n)).then_inc(S["w2_in"], 16)
            for dst, src in ([(square[n][:, :, :], chunks(n)) for n in ("q4", "k4", "v4")]
                             + [(w_up[:, :, :], chunks("up")), (w_down[:, :, :], chunks("down"))]):
                sp.dma_start(dst, src).then_inc(S["w3_in"], 16)

            def store(it):
                b, use = job(it, "down", G - 1)
                sp.wait_ge(bank_read[b], use + 1)
                sp.dma_start(o_v[it], result[:, :, :]).then_inc(S["stored"], 16)

            with sp.Fori(0, ITERS - 1) as it:
                sp.wait_ge(S["x1"], nth(it, G - 1))
                sp.dma_start(x_in[:, :, :], x_v[it + 1]).then_inc(S["x_in"], 16)
                bank_, use = job(it, "ctxT", G - 1)
                sp.wait_ge(bank_full[bank_], use + 1)
                sp.dma_start(c_in[:, :, :], c_v[it + 1]).then_inc(S["c_in"], 16)
                store(it)
            store(ITERS - 1)
            sp.wait_ge(S["stored"], 16 * (ITERS + 1))

        @block.tensor
        def _(pe):
            mm = nc.tensor.matmul

            def claim(it, what, lane=0):
                b, use = job(it, what, lane)
                if what not in FIRST_JOBS or use:
                    pe.wait_ge(bank_read[b], use)
                return bank[b], bank_full[b]

            def evacuated(it, what, lane=0):
                b, use = job(it, what, lane)
                pe.wait_ge(bank_read[b], use + 1)

            def flip(it, what, lane, src, n):
                t, full = claim(it, what, lane)
                for c in range(n):
                    last = nc.tensor.transpose(t[:, c * P:(c + 1) * P], src[:, c * P:(c + 1) * P], ident)
                last.then_inc(full, 1)

            def to_channels(t, at, w, cols, xT, n=DC):
                for c in range(n):
                    last = mm(t[:, at:at + P], w[:, c, cols:cols + P], xT[:, c, :], start=(c == 0), stop=(c == n - 1))
                return last

            def to_tokens(t, at, w, lo, hi, xT, n=DC):
                for c in range(n):
                    last = mm(t[:, at:at + hi - lo], xT[:, c, :], w[:, c, lo:hi], start=(c == 0), stop=(c == n - 1))
                return last

            def project_T(it, what, lane, w, xT):
                t, full = claim(it, what, lane)
                for m in range(DC):
                    last = to_channels(t, m * P, w, m * P, xT)
                last.then_inc(full, 1)

            def project(it, what, lane, w, xT, n=DC):
                t, full = claim(it, what, lane)
                to_tokens(t, 0, w, 0, D, xT, n).then_inc(full, 1)

            def attention(it, a_, lanes, mask, keys, V, v_ready, dh):
                parts = lanes_parts(a_, lanes)
                last_part = PARTS[a_] - 1

                def scores(n):
                    l, t = parts[n]
                    c = t * DC // PARTS[a_]
                    if n >= SCORE_BANKS:
                        pe.wait_ge(S["shifted"], part(it, a_, n - SCORE_BANKS) + 1)
                    elif a_:
                        pe.wait_ge(S["shifted"], part(it, a_, 0))
                    if t == 0:
                        evacuated(it, f"Q{a_}", l)
                        for eng in ("dve", "act", "pool"):
                            pe.wait_ge(S[f"keys_{eng}"], keyed(it, a_, l))
                    h = t % (PARTS[a_] // DC) * HEADS
                    to = score[:, n % SCORE_BANKS, :]
                    last = mm(to, Q[:, l, c, :], keys[:, l, c, h:h + HEADS, :], start=True, stop=(mask is None))
                    if mask is not None:
                        last = mm(to, ident_bf[:, :], mask[:, :].unsqueeze(1).broadcast_to((P, HEADS, P)),
                                  start=False, stop=True)
                    last.then_inc(S["scores"], 1)

                def turn(n):
                    if part(0, a_, n):
                        pe.wait_ge(S["weights"], part(it, a_, n))
                    pe.wait_ge(S["exps"], part(it, a_, n) + 1)
                    for i in range(HEADS):
                        last = nc.tensor.transpose(turned[:, i * P:(i + 1) * P],
                                                   shifted[:, n % SHIFTED_BUFFERS, i * P:(i + 1) * P], ident)
                    last.then_inc(S["turned"], 1)

                def values(n):
                    l, t = parts[n]
                    b_, use = job(it, f"O{a_}", l)
                    if t == 0:
                        claim(it, f"O{a_}", l)
                        if v_ready is None:
                            evacuated(it, f"V{a_}", l)
                        else:
                            pe.wait_ge(S[v_ready], nth(it, l))
                    pe.wait_ge(S["weights"], part(it, a_, n) + 1)
                    for i in range(HEADS):
                        h = t * HEADS + i
                        last = mm(bank[b_][:, h * (dh + 1):(h + 1) * (dh + 1)],
                                  weights[:, n % WEIGHT_BUFFERS, i * P:(i + 1) * P], V[:, l, h, :], start=True, stop=True)
                    if t == last_part:
                        last.then_inc(bank_full[b_], 1)

                for n in range(len(parts) + 3):
                    if n < len(parts):
                        scores(n)
                    if 0 <= n - 2 < len(parts):
                        turn(n - 2)
                    if n >= 3:
                        values(n - 3)

            pe.wait_ge(S["const_in"], 16)
            pe.wait_ge(S["x_in"], 16)
            flip(0, "x0T", 0, x_in[:, 0, :], DC)
            pe.wait_ge(S["c_in"], 16)
            flip(0, "c0T", 0, c_in[:, 0, :], DC)
            pe.wait_ge(S["w0_in"], 16 * 3)
            evacuated(0, "x0T")
            project_T(0, "Q0", 0, w0["q0"], actT[:, 0])
            evacuated(0, "c0T")
            project_T(0, "K0", 0, w0["k0"], cT[:, 0])
            project(0, "V0", 0, w0["v0"], cT[:, 0])
            pe.wait_ge(S["ready_consts"], 1)
            pe.wait_ge(S["ones_col"], 2)
            attention(0, 0, [0], None, keys16, V2, None, DH16)
            pe.wait_ge(S["wmamba_in"], 16 * 5)
            pe.wait_ge(S["w1_in"], 16 * 4)
            for m in range(DC):
                t, full = claim(0, f"bias{m}")
                for c in range(DC):
                    last = mm(t[:, 0:1], square["q1"][:, c, m * P:(m + 1) * P], ca_b[:, c:c + 1],
                              start=(c == 0), stop=(c == DC - 1))
                last.then_inc(full, 1)
            pe.wait_ge(S["ready_weights"], 1)
            pe.wait_ge(S["w2_in"], 16 * 8)
            pe.wait_ge(S["w3_in"], 16 * 5)

            def stages(it):
                pe.wait_ge(S["c_in"], it * 16 + 16)
                for l in range(G):
                    flip(it, "ctxT", l, c_in[:, l, :], DC)
                for l in range(G):
                    evacuated(it, "ctxT", l)
                    project_T(it, "K1", l, square["k1"], cT[:, l])
                    project(it, "V1", l, square["v1"], cT[:, l])
                for l in range(G):
                    pe.wait_ge(S["xhat"], nth(it, l))
                    flip(it, "xhatT", l, nrm[:, l, :], DC)
                for l in range(G):
                    evacuated(it, "xhatT", l)
                    for half in range(2):
                        t, full = claim(it, f"xbc{half}", l)
                        for k in range(XBC // 2):
                            last = to_channels(t, k * P, w_in, INNER + (half * XBC // 2 + k) * P, actT[:, l])
                        if half == 0:
                            last = to_tokens(t, XBC // 2 * P, w_in, IN_PROJ - MH, IN_PROJ, actT[:, l])
                        last.then_inc(full, 1)
                    t, full = claim(it, "z", l)
                    to_tokens(t, 0, w_in, 0, INNER, actT[:, l]).then_inc(full, 1)
                for l in range(G):
                    pe.wait_ge(S["xbc"], nth(it, l))
                    t, full = claim(it, "CB", l)
                    mm(t[:, 0:P], conv[:, l, BCH, :], conv[:, l, CCH, :], start=True, stop=True).then_inc(full, 1)
                    flip(it, "xh", l, conv[:, l, 0:IC, :].rearrange("p c k -> p (c k)"), IC)
                    pe.wait_ge(S["am"], nth(it, l))
                    if l:
                        pe.wait_ge(S["decay"], nth(it, l - 1))
                    for h in range(MH):
                        b, at = h // 4, h % 4 * P
                        last = mm(score[:, b, at:at + P], decay[:, l, h, :], before, start=(at == 0), stop=(h % 4 == 3))
                    last.then_inc(S["log_decay"], 1)
                for l in range(G):
                    t, full = claim(it, "Y", l)
                    evacuated(it, "xh", l)
                    pe.wait_ge(S["M"], nth(it, l))
                    for h in range(MH):
                        last = mm(t[:, h * MD:(h + 1) * MD], decay[:, l, h, :], dbx[:, l, h * MD:(h + 1) * MD],
                                  start=True, stop=True)
                    last.then_inc(full, 1)
                for l in range(G):
                    pe.wait_ge(S["u"], nth(it, l))
                    flip(it, "uT", l, zs[:, l, :], IC)
                for l in range(G):
                    evacuated(it, "uT", l)
                    project(it, "proj", l, w_out, uT[:, l], IC)

                def flip_nrm(l):
                    pe.wait_ge(S["xn"], nth(it, l))
                    flip(it, "xnT", l, nrm[:, l, :], DC)

                flip_nrm(0)
                for l in range(G):
                    if l + 1 < G:
                        flip_nrm(l + 1)
                    evacuated(it, "xnT", l)
                    project_T(it, "Q1", l, square["q1"], actT[:, l])
                attention(it, 1, range(G), padding_bf, keys32, V1, None, DH8)

                def flip_att(l):
                    evacuated(it, "O1", l)
                    flip(it, "oT", l, att[:, l, :], DC)

                flip_att(0)
                for l in range(G):
                    if l + 1 < G:
                        flip_att(l + 1)
                    evacuated(it, "oT", l)
                    project(it, "Wo", l, square["o1"], actT[:, l])

                def flip_x2(l):
                    evacuated(it, "Wo", l)
                    flip(it, "x2T", l, res[:, l, :], DC)

                flip_x2(0)
                for l in range(G):
                    if l + 1 < G:
                        flip_x2(l + 1)
                    evacuated(it, "x2T", l)
                    project_T(it, "Q2", l, square["q2"], actT[:, l])
                    project_T(it, "K2", l, square["k2"], actT[:, l])
                    project(it, "V2", l, square["v2"], actT[:, l])

                def lengths(a_):
                    for l in range(G):
                        t, full = claim(it, f"e{a_}", l)
                        evacuated(it, f"K{a_}", l)
                        pe.wait_ge(S[f"q{a_}_first"], nth(it, l))
                        for c in range(DC):
                            last = mm(t[:, c * 8:c * 8 + 8], K2[:, l, c, :], q_first[:, l, c, :], start=True, stop=True)
                        last.then_inc(full, 1)
                    for l in range(G):
                        t, full = claim(it, f"n{a_}", l)
                        evacuated(it, f"e{a_}", l)
                        mm(t[:, 0:H16], ones_bf[:, :], nonzero[:, l, :], start=True, stop=True).then_inc(full, 1)

                lengths(2)
                attention(it, 2, range(G), causal_bf, keys16, V2, "V2", DH16)

                def flip_x3(l):
                    pe.wait_ge(S["x3"], nth(it, l))
                    flip(it, "x3T", l, res[:, l, :], DC)

                flip_x3(0)
                for l in range(G):
                    if l + 1 < G:
                        flip_x3(l + 1)
                    evacuated(it, "x3T", l)
                    project_T(it, "Q3", l, square["q3"], actT[:, l])
                    project(it, "V3", l, square["v3"], cT[:, l])
                    t, full = claim(it, "row", l)
                    pe.wait_ge(S["m1"], nth(it, l))
                    mm(t[:, 0:P], mask1_bf[:, l:l + 1].broadcast_to((P, P)), ident_bf[:, :],
                       start=True, stop=True).then_inc(full, 1)
                    project_T(it, "K3", l, square["k3"], cT[:, l])
                lengths(3)
                attention(it, 3, range(G), None, keys16, V2, "V3", DH16)

                def flip_x4(l):
                    pe.wait_ge(S["x4"], nth(it, l))
                    flip(it, "x4T", l, res[:, l, :], DC)

                flip_x4(0)
                for l in range(G):
                    if l + 1 < G:
                        flip_x4(l + 1)
                    evacuated(it, "x4T", l)
                    project_T(it, "fc1", l, square["fc1"], actT[:, l])
                for l in range(G):
                    evacuated(it, "fc1", l)
                    project(it, "fc2", l, square["fc2"], fc1T[:, l])

                for l in range(G):
                    project_T(it, "K4", l, square["k4"], cT[:, l])
                    project(it, "V4", l, square["v4"], cT[:, l])

                def flip_x5(l):
                    pe.wait_ge(S["x5"], nth(it, l))
                    flip(it, "x5T", l, res[:, l, :], DC)

                flip_x5(0)
                for l in range(G):
                    if l + 1 < G:
                        flip_x5(l + 1)
                    evacuated(it, "x5T", l)
                    project_T(it, "Q4", l, square["q4"], actT[:, l])
                attention(it, 4, range(G), causal_bf, keys16, V2, "V4ones", DH16)

                def flip_x6(l):
                    pe.wait_ge(S["x6"], nth(it, l))
                    flip(it, "x6T", l, res[:, l, :], DC)

                flip_x6(0)
                for l in range(G):
                    if l + 1 < G:
                        flip_x6(l + 1)
                    evacuated(it, "x6T", l)
                    for half in range(2):
                        t, full = claim(it, f"up{half}", l)
                        for k in range(FC // 2):
                            last = to_channels(t, k * P, w_up, (half * FC // 2 + k) * P, actT[:, l])
                        last.then_inc(full, 1)
                for l in range(G):
                    evacuated(it, "up0", l)
                    evacuated(it, "up1", l)
                    project(it, "down", l, w_down, gT[:, l], FC)

            with pe.Fori(0, ITERS) as it:
                stages(it)

        @block.scalar
        def _(act):
            run = nc.scalar.activation

            def filled(it, what, lane=0):
                b, use = job(it, what, lane)
                act.wait_ge(bank_full[b], use + 1)
                return bank[b], bank_read[b]

            def copy_out(it, what, lane, dst, n):
                t, read = filled(it, what, lane)
                nc.scalar.copy(dst.rearrange("p c k -> p (c k)"), t[:, 0:n]).then_inc(read, 1)

            def by_head(it, a_, lane):
                evacuated(it, f"K{a_}", lane)
                if a_ == 1:
                    filled(it, "Y", lane)
                    K, keys, heads, share = K1, keys32, head32, SHARE32["act"]
                else:
                    K, keys, heads, share = K2, keys16, head16, SHARE16["act"]
                for h in share:
                    last = run(keys[:, lane, :, h, :], K[:, lane, :, :], ACT.Copy, scale=heads[:, h:h + 1])
                last.then_inc(S["keys_act"], 1)

            def evacuated(it, what, lane=0):
                b, use = job(it, what, lane)
                act.wait_ge(bank_read[b], use + 1)

            def values_out(it, what, lane, V, heads, dh, scale=1.0):
                t, read = filled(it, what, lane)
                run(V[:, lane, :, 0:dh], t[:, 0:D].rearrange("p (h e) -> p h e", h=heads), ACT.Copy,
                    scale=scale).then_inc(read, 1)

            def exponentials(it, a_, lanes, scale):
                parts = lanes_parts(a_, lanes)
                for n in range(len(parts) + 2):
                    if n >= 2:
                        act.wait_ge(S["turned"], part(it, a_, n - 2) + 1)
                        nc.scalar.copy(weights[:, (n - 2) % WEIGHT_BUFFERS, :], turned[:, :]).then_inc(S["weights"], 1)
                    if n < len(parts):
                        act.wait_ge(S["shifted"], part(it, a_, n) + 1)
                        e = shifted[:, n % SHIFTED_BUFFERS, :]
                        run(e, e, ACT.Exp, scale=scale).then_inc(S["exps"], 1)

            copy_out(0, "x0T", 0, actT[:, 0], D)
            copy_out(0, "c0T", 0, cT[:, 0], D)
            copy_out(0, "Q0", 0, Q[:, 0], D)
            copy_out(0, "K0", 0, K2[:, 0], D)
            by_head(0, 0, 0)
            values_out(0, "V0", 0, V2, H16, DH16)
            exponentials(0, 0, [0], 0.25)
            act.wait_ge(S["wmamba_in"], 16 * 5)
            run(decay_rate, decay_rate, ACT.Exp).then_inc(S["rates"], 1)
            act.wait_ge(S["ready_weights"], 1)

            def stages(it):
                for l in range(G):
                    copy_out(it, "ctxT", l, cT[:, l], D)
                for l in range(G):
                    act.wait_ge(S["x1"], nth(it, l))
                    run(nrm[:, l, :], res[:, l, :], ACT.Square, accum_out=stat[:, l, 12:13]).then_inc(S["ss1"], 1)
                for l in range(G):
                    values_out(it, "V1", l, V1, H8, DH8)
                for l in range(G):
                    copy_out(it, "xhatT", l, actT[:, l], D)

                def mamba_inputs(l):
                    for half in range(2):
                        t, read = filled(it, f"xbc{half}", l)
                        n = XBC // 2
                        for k in range(n):
                            c = half * n + k
                            run(conv[:, l, c, :], t[:, k * P:(k + 1) * P], ACT.Identity,
                                scale=conv_w[:, c, TAPS - 1:TAPS], bias=conv_b[:, c:c + 1])
                        if half == 0:
                            nc.scalar.copy(dts[:, l, 0, :], t[:, n * P:n * P + MH])
                        nc.scalar.copy(raw[:, l, half * n:(half + 1) * n, TAPS - 1:],
                                       t[:, 0:n * P].rearrange("p (c k) -> p c k", c=n)).then_inc(read, 1)
                    t, read = filled(it, "z", l)
                    nc.scalar.copy(zs[:, l, :], t[:, :])
                    run(tz[:, l, :], t[:, :], ACT.Tanh, scale=0.5).then_inc(read, 1)

                def mamba_curves(l):
                    act.wait_ge(S["near0"], nth(it, l))
                    run(dts[:, l, 4, :], dts[:, l, 2, :], ACT.Exp).then_inc(S["edt"], 1)
                    act.wait_ge(S["conv"], nth(it, l))
                    run(raw[:, l, :, TAPS - 1:], conv[:, l, :, :], ACT.Tanh, scale=0.5).then_inc(S["tanh"], 1)

                mamba_inputs(0)
                for l in range(G):
                    if l + 1 < G:
                        mamba_inputs(l + 1)
                    mamba_curves(l)
                for l in range(G):
                    act.wait_ge(S["log_decay"], nth(it, l))
                    run(decay[:, l, :, :].rearrange("p (b h) k -> p b (h k)", b=2), score[:, 0:2, :],
                        ACT.Exp).then_inc(S["decay"], 1)
                for l in range(G):
                    act.wait_ge(S["u"], nth(it, l))
                    run(dx[:, l, :], zs[:, l, :], ACT.Square, accum_out=stat[:, l, 12:13]).then_inc(S["ss2"], 1)
                for l in range(G):
                    copy_out(it, "uT", l, uT[:, l], INNER)

                for l in range(G):
                    by_head(it, 1, l)
                copy_out(it, "xnT", 0, actT[:, 0], D)
                for l in range(G):
                    if l + 1 < G:
                        copy_out(it, "xnT", l + 1, actT[:, l + 1], D)
                    t, read = filled(it, "Q1", l)
                    for c in range(DC):
                        last = run(Q[:, l, c, :], t[:, c * P:(c + 1) * P], ACT.Identity, bias=q1_bias[:, c:c + 1])
                    last.then_inc(read, 1)
                exponentials(it, 1, range(G), SCALE8)
                for l in range(G):
                    copy_out(it, "oT", l, actT[:, l], D)

                copy_out(it, "x2T", 0, actT[:, 0], D)
                for l in range(G):
                    if l + 1 < G:
                        copy_out(it, "x2T", l + 1, actT[:, l + 1], D)
                    copy_out(it, "Q2", l, Q[:, l], D)
                    copy_out(it, "K2", l, K2[:, l], D)
                    values_out(it, "V2", l, V2, H16, DH16)
                    by_head(it, 2, l)
                exponentials(it, 2, range(G), 0.25)

                copy_out(it, "x3T", 0, actT[:, 0], D)
                for l in range(G):
                    if l + 1 < G:
                        copy_out(it, "x3T", l + 1, actT[:, l + 1], D)
                    copy_out(it, "Q3", l, Q[:, l], D)
                    act.wait_ge(S["m1"], nth(it, l))
                    values_out(it, "V3", l, V2, H16, DH16, mask1[:, l, 1:2])
                    t, read = filled(it, "row", l)
                    nc.scalar.copy(row_mask[:, l, :], t[:, 0:P]).then_inc(read, 1)
                    by_head(it, 3, l)
                exponentials(it, 3, range(G), 0.25)

                copy_out(it, "x4T", 0, actT[:, 0], D)
                for l in range(G):
                    if l + 1 < G:
                        copy_out(it, "x4T", l + 1, actT[:, l + 1], D)
                    t, read = filled(it, "fc1", l)
                    for c in range(DC):
                        last = run(fc1T[:, l, c, :], t[:, c * P:(c + 1) * P], ACT.Relu, bias=fc1_b[:, c:c + 1])
                    last.then_inc(read, 1)

                for l in range(G):
                    t, read = filled(it, "K4", l)
                    for c in range(DC):
                        last = run(K2[:, l, c, :], t[:, c * P:(c + 1) * P], ACT.Identity, bias=k4_b[:, c:c + 1])
                    last.then_inc(read, 1)
                    by_head(it, 4, l)
                copy_out(it, "x5T", 0, actT[:, 0], D)
                for l in range(G):
                    if l + 1 < G:
                        copy_out(it, "x5T", l + 1, actT[:, l + 1], D)
                    t, read = filled(it, "Q4", l)
                    for c in range(DC):
                        last = run(Q[:, l, c, :], t[:, c * P:(c + 1) * P], ACT.Identity, bias=q4_b[:, c:c + 1])
                    last.then_inc(read, 1)
                exponentials(it, 4, range(G), 0.25)

                copy_out(it, "x6T", 0, actT[:, 0], D)
                for l in range(G):
                    if l + 1 < G:
                        copy_out(it, "x6T", l + 1, actT[:, l + 1], D)
                    for half in range(2):
                        t, read = filled(it, f"up{half}", l)
                        for k in range(FC // 2):
                            c = half * FC // 2 + k
                            last = run(gT[:, l, c, :], t[:, k * P:(k + 1) * P], ACT.Gelu, bias=up_b[:, c:c + 1])
                        last.then_inc(read, 1)

            with act.Fori(0, ITERS) as it:
                stages(it)

        @block.vector
        def _(dve):
            tt, ts, stt = nc.vector.tensor_tensor, nc.vector.tensor_scalar, nc.vector.scalar_tensor_tensor

            def filled(it, what, lane=0):
                b, use = job(it, what, lane)
                dve.wait_ge(bank_full[b], use + 1)
                return bank[b], bank_read[b]

            def evacuated(it, what, lane=0):
                b, use = job(it, what, lane)
                dve.wait_ge(bank_read[b], use + 1)

            def root_guess(l, step, src, scale, offset, done):
                step(ts(stat[:, l, 2:3], src, scale, offset, ALU.mult, ALU.add))
                step(ts(stat[:, l, 3:4].bitcast(I32), stat[:, l, 2:3].bitcast(I32), 1, None, ALU.logical_shift_right))
                ts(stat[:, l, 4:5].bitcast(I32), stat[:, l, 3:4].bitcast(I32), -1.0, MAGIC,
                   ALU.mult, ALU.add).then_inc(done, 1)

            def moments(l, step, done):
                step(nc.vector.bn_stats(bn[:, l, :], res[:, l, :]))
                step(nc.vector.bn_aggr(stat[:, l, 0:2], bn[:, l, :]))
                root_guess(l, step, stat[:, l, 1:2], 1.0, EPS, done)

            def normalise(it, l, root, done):
                dve.wait_ge(S[root], nth(it, l))
                ts(nrm[:, l, :], res[:, l, :], stat[:, l, 0:1], stat[:, l, 10:11],
                   ALU.subtract, ALU.mult).then_inc(S[done], 1)

            def by_head(it, a_, lane):
                evacuated(it, f"K{a_}", lane)
                if a_ == 1:
                    filled(it, "Y", lane)
                    K, keys, heads, share = K1, keys32, head32, SHARE32["dve"]
                else:
                    K, keys, heads, share = K2, keys16, head16, SHARE16["dve"]
                shape = (P, DC, len(share), P)
                tt(keys[:, lane, :, share[0]:share[-1] + 1, :], K[:, lane, :, :].unsqueeze(2).broadcast_to(shape),
                   heads[:, share[0]:share[-1] + 1].unsqueeze(1).unsqueeze(3).broadcast_to(shape),
                   ALU.mult).then_inc(S["keys_dve"], 1)

            def shift(it, a_, n, step):
                dve.wait_ge(S["scores"], part(it, a_, n) + 1)
                s = score[:, n % SCORE_BANKS, :].rearrange("p (h k) -> p h k", h=HEADS)
                step(nc.vector.tensor_reduce(neg_max[:, n % 2, :], s, AX_X, ALU.max, negate=True))
                tt(shifted[:, n % SHIFTED_BUFFERS, :].rearrange("p (h k) -> p h k", h=HEADS), s,
                   neg_max[:, n % 2, :].unsqueeze(2).broadcast_to((P, HEADS, P)), ALU.add).then_inc(S["shifted"], 1)

            def weighted(it, a_, l, step, heads, dh, dst, mask=None):
                t, read = filled(it, f"O{a_}", l)
                o = t[:, 0:heads * (dh + 1)].rearrange("p (h e) -> p h e", h=heads)
                step(nc.vector.reciprocal(rec[:, l, 0:heads], o[:, :, dh]))
                if mask is not None:
                    step(ts(rec[:, l, 0:heads], rec[:, l, 0:heads], mask, None, ALU.mult))
                tt(dst.rearrange("p (h e) -> p h e", h=heads), o[:, :, 0:dh],
                   rec[:, l, 0:heads].unsqueeze(2).broadcast_to((P, heads, dh)), ALU.mult).then_inc(read, 1)
                evacuated(it, f"O{a_}", l)

            def attention(it, a_, step, finish, later):
                T = PARTS[a_]
                for n in range(G * T):
                    shift(it, a_, n, step)
                    if n >= T + 3 and (n - 3) % T == 0:
                        l = (n - 3) // T - 1
                        finish(l)
                        if l:
                            later(l - 1)
                done = (G * T - 4) // T
                for l in range(done, G):
                    finish(l)
                    if l:
                        later(l - 1)
                later(G - 1)

            step = Chain(dve, S["dve_first"])
            dve.wait_ge(S["const_in"], 16)
            nc.vector.memset(ones_bf[:, :], 1.0)
            nc.vector.tensor_copy(ident_bf[:, :], ident)
            nc.vector.tensor_copy(causal_bf[:, :], con("causal")).then_inc(S["ready_consts"], 1)
            by_head(0, 0, 0)
            for n in range(PARTS[0]):
                shift(0, 0, n, step)
            weighted(0, 0, 0, step, H16, DH16, att0[:, :])
            dve.wait_ge(S["wmamba_in"], 16 * 5)
            ts(keep_row[:, :], pad_u8[:, :], -1.0, 1.0, ALU.mult, ALU.add)
            ts(padding_bf[:, :], pad_u8[:, :], MASKED, None, ALU.mult)
            ts(skip, skip, 0.5, None, ALU.mult)
            for c in range(DC):
                ts(w_in[:, c, :], w_in[:, c, :], m_norm[:, c:c + 1], None, ALU.mult)
            for c in range(IC):
                ts(w_out[:, c, :], w_out[:, c, :], g_norm[:, c:c + 1], None, ALU.mult)
            for m in range(DC):
                t, read = filled(0, f"bias{m}")
                nc.vector.tensor_copy(q1_bias[:, m:m + 1], t[:, 0:1]).then_inc(read, 1)
            for c in range(DC):
                ts(square["q1"][:, c, :], square["q1"][:, c, :], ca_w[:, c:c + 1], None, ALU.mult)
            dve.wait_ge(S["rates"], 1)
            ts(decay_rate, decay_rate, -1.0, None, ALU.mult)
            dve.wait_ge(S["w2_in"], 16 * 8)
            dve.wait_ge(S["w3_in"], 16 * 5)
            dve.wait_ge(S["pads_zero"], 1)
            nc.vector.memset(stat[:, :, :], 1.0).then_inc(S["ready_weights"], 1)
            dve.wait_ge(S["ready_weights"], 1)

            def stages(it):
                step = Chain(dve, S["dve_step"])
                dve.wait_ge(S["x_in"], it * 16 + 16)
                for l in range(G):
                    tt(res[:, l, :], x_in[:, l, :], att0[:, :], ALU.add).then_inc(S["x1"], 1)
                for l in range(G):
                    dve.wait_ge(S["ss1"], nth(it, l))
                    root_guess(l, step, stat[:, l, 12:13], 1.0 / D, EPS, S["seed1"])
                for l in range(G):
                    t, read = filled(it, "K1", l)
                    tt(K1[:, l, :, :], t[:, 0:D].rearrange("p (c k) -> p c k", c=DC),
                       keep_row[:, :].unsqueeze(1).broadcast_to((P, DC, P)), ALU.mult).then_inc(read, 1)
                for l in range(G):
                    dve.wait_ge(S["rstd1"], nth(it, l))
                    ts(nrm[:, l, :], res[:, l, :], stat[:, l, 10:11], None, ALU.mult).then_inc(S["xhat"], 1)

                def convolve(l):
                    n = XBC // 2
                    for half in range(2):
                        evacuated(it, f"xbc{half}", l)
                        for k in range(TAPS - 1):
                            for c in range(half * n, (half + 1) * n):
                                last = stt(conv[:, l, c, :], raw[:, l, c, k:k + P], conv_w[:, c, k:k + 1],
                                           conv[:, l, c, :], ALU.mult, ALU.add)
                            if half == 0 or k < TAPS - 2:
                                step(last)
                    last.then_inc(S["conv"], 1)

                def silu(l):
                    dve.wait_ge(S["tanh"], nth(it, l))
                    stt(conv[:, l, :, :], raw[:, l, :, TAPS - 1:], 1.0, conv[:, l, :, :],
                        ALU.add, ALU.mult).then_inc(S["xbc"], 1)

                def softplus(l):
                    def d(k):
                        return dts[:, l, k, :]
                    dve.wait_ge(S["edt"], nth(it, l))
                    step(ts(d(5), d(4), 2.0, None, ALU.add))
                    step(nc.vector.reciprocal(d(6), d(5)))
                    step(tt(d(7), d(4), d(6), ALU.mult))
                    step(tt(d(8), d(7), d(7), ALU.mult))
                    step(ts(d(9), d(8), 1.0 / (2 * LOG1P_TERMS - 1), None, ALU.mult))
                    for k in range(LOG1P_TERMS - 2, 0, -1):
                        step(stt(d(9), d(9), 1.0 / (2 * k + 1), d(8), ALU.add, ALU.mult))
                    step(stt(d(9), d(9), 1.0, d(7), ALU.add, ALU.mult))
                    step(stt(d(10), d(9), 2.0, d(3), ALU.mult, ALU.add))
                    ts(d(11), d(10), 0.5, None, ALU.mult).then_inc(S["dt"], 1)

                convolve(0)
                for l in range(G):
                    softplus(l)
                    if l + 1 < G:
                        convolve(l + 1)
                    silu(l)

                def token_pairs(l):
                    t, read = filled(it, "CB", l)
                    tt(state_gate[:, l, :], t[:, 0:P], gate_mask, ALU.mult).then_inc(read, 1)
                    t, read = filled(it, "xh", l)
                    x3 = t[:, :].rearrange("p (h e) -> p h e", h=MH)
                    tt(dbx[:, l, :].rearrange("p (h e) -> p h e", h=MH), x3,
                       dts[:, l, 11, :].unsqueeze(2).broadcast_to((P, MH, MD)), ALU.mult)
                    tt(dx[:, l, :].rearrange("p (h e) -> p h e", h=MH), x3,
                       skip.unsqueeze(2).broadcast_to((P, MH, MD)), ALU.mult).then_inc(read, 1)

                def decayed(l):
                    dve.wait_ge(S["decay"], nth(it, l))
                    evacuated(it, "CB", l)
                    tt(decay[:, l, :, :], decay[:, l, :, :],
                       state_gate[:, l, :].unsqueeze(1).broadcast_to((P, MH, P)), ALU.mult).then_inc(S["M"], 1)

                token_pairs(0)
                for l in range(G):
                    if l + 1 < G:
                        token_pairs(l + 1)
                    decayed(l)

                def gate(l):
                    t, read = filled(it, "Y", l)
                    evacuated(it, "xh", l)
                    dve.wait_ge(S["gated"], nth(it, l))
                    tt(tz[:, l, :], t[:, :], dx[:, l, :], ALU.add).then_inc(read, 1)
                    evacuated(it, "Y", l)
                    tt(zs[:, l, :], tz[:, l, :], zs[:, l, :], ALU.mult).then_inc(S["u"], 1)

                def gate_norm(l):
                    dve.wait_ge(S["ss2"], nth(it, l))
                    root_guess(l, step, stat[:, l, 12:13], 1.0 / INNER, 4.0 * EPS, S["seed2"])

                gate(0)
                for l in range(G):
                    if l + 1 < G:
                        gate(l + 1)
                    gate_norm(l)

                def mamba_out(l):
                    dve.wait_ge(S["rstd2"], nth(it, l))
                    t, read = filled(it, "proj", l)
                    stt(res[:, l, :], t[:, 0:D], stat[:, l, 10:11], res[:, l, :], ALU.mult, ALU.add).then_inc(read, 1)
                    evacuated(it, "proj", l)
                    moments(l, step, S["seed3"])

                mamba_out(0)
                for l in range(G):
                    if l + 1 < G:
                        mamba_out(l + 1)
                    normalise(it, l, "rstd3", "xn")

                for l in range(G):
                    by_head(it, 1, l)
                attention(it, 1, step, lambda l: weighted(it, 1, l, step, H8, DH8, att[:, l, :]), lambda l: None)
                for l in range(G):
                    t, read = filled(it, "Wo", l)
                    tt(res[:, l, :], t[:, 0:D], res[:, l, :], ALU.add).then_inc(read, 1)
                    evacuated(it, "Wo", l)
                    step(nc.vector.tensor_reduce(mask0[:, l, 0:1], res[:, l, :], AX_X, ALU.max, apply_absolute_value=True))
                    step(ts(mask0[:, l, 1:2], mask0[:, l, 0:1], 0.0, None, ALU.is_gt))

                def lengths(a_):
                    for l in range(G):
                        t, read = filled(it, f"e{a_}", l)
                        ts(nonzero[:, l, :], t[:, 0:H16], 0.0, None, ALU.not_equal).then_inc(read, 1)
                    for l in range(G):
                        t, read = filled(it, f"n{a_}", l)
                        ts(keep[:, l, :], t[:, 0:H16], index, None, ALU.is_gt).then_inc(read, 1)

                def add_attention(a_, mask, seed):
                    def finish(l):
                        weighted(it, a_, l, step, H16, DH16, att[:, l, :], mask and mask(l))
                        step(tt(res[:, l, :], att[:, l, :], res[:, l, :], ALU.add))
                        moments(l, step, S[seed])
                    return finish

                for l in range(G):
                    by_head(it, 2, l)
                lengths(2)
                attention(it, 2, step, add_attention(2, lambda l: mask0[:, l, 1:2], "seed4"),
                          lambda l: normalise(it, l, "rstd4", "t4"))

                def token_mask(l):
                    dve.wait_ge(S["x3"], nth(it, l))
                    step(nc.vector.tensor_reduce(mask1[:, l, 0:1], res[:, l, :], AX_X, ALU.max, apply_absolute_value=True))
                    step(ts(mask1[:, l, 1:2], mask1[:, l, 0:1], 0.0, None, ALU.is_gt))
                    ts(mask1_bf[:, l:l + 1], mask1[:, l, 0:1], 0.0, None, ALU.is_gt).then_inc(S["m1"], 1)

                token_mask(0)
                for l in range(G):
                    if l + 1 < G:
                        token_mask(l + 1)
                    evacuated(it, "row", l)
                    t, read = filled(it, "K3", l)
                    tt(K2[:, l, :, :], t[:, 0:D].rearrange("p (c k) -> p c k", c=DC),
                       row_mask[:, l, :].unsqueeze(1).broadcast_to((P, DC, P)), ALU.mult).then_inc(read, 1)
                    by_head(it, 3, l)
                lengths(3)
                attention(it, 3, step, add_attention(3, lambda l: mask1[:, l, 1:2], "seed5"),
                          lambda l: normalise(it, l, "rstd5", "t5"))

                def feed_forward(l):
                    t, read = filled(it, "fc2", l)
                    tt(att[:, l, :], t[:, 0:D], rows["fc2"], ALU.add).then_inc(read, 1)
                    evacuated(it, "fc2", l)
                    step(stt(res[:, l, :], att[:, l, :], mask0[:, l, 1:2], res[:, l, :], ALU.mult, ALU.add))
                    moments(l, step, S["seed6"])

                def values_biased(l):
                    t, read = filled(it, "V4", l)
                    tt(V2[:, l, :, 0:DH16], t[:, 0:D].rearrange("p (h e) -> p h e", h=H16),
                       rows["v4"].rearrange("p (h e) -> p h e", h=H16), ALU.add).then_inc(read, 1)

                feed_forward(0)
                for l in range(1, G):
                    feed_forward(l)
                    normalise(it, l - 1, "rstd6", "t6")
                for l in range(G - 1):
                    values_biased(l)
                normalise(it, G - 1, "rstd6", "t6")
                values_biased(G - 1)

                for l in range(G):
                    by_head(it, 4, l)
                attention(it, 4, step, add_attention(4, None, "seed7"), lambda l: normalise(it, l, "rstd7", "t7"))
                dve.wait_ge(S["stored"], it * 16 + 16)
                for l in range(G):
                    t, read = filled(it, "down", l)
                    dve.wait_ge(S["plus"], nth(it, l))
                    tt(result[:, l, :], t[:, 0:D], plus[:, l, :], ALU.add).then_inc(read, 1)

            with dve.Fori(0, ITERS) as it:
                stages(it)

        @block.gpsimd
        def _(pool):
            tt, ts, copy = nc.gpsimd.tensor_tensor, nc.gpsimd.tensor_scalar, nc.gpsimd.tensor_copy

            def wait_for(semaphore, value):
                pool.wait_ge(semaphore, value)
                pool.sem_inc(S["pool_waits"], 1)

            def evacuated(it, what, lane=0):
                b, use = job(it, what, lane)
                wait_for(bank_read[b], use + 1)

            def by_head(it, a_, lane):
                evacuated(it, f"K{a_}", lane)
                if a_ == 1:
                    b, use = job(it, "Y", lane)
                    wait_for(bank_full[b], use + 1)
                    K, keys, heads, share = K1, keys32, head32, SHARE32["pool"]
                else:
                    K, keys, heads, share = K2, keys16, head16, SHARE16["pool"]
                for h in share:
                    last = ts(keys[:, lane, :, h, :], K[:, lane, :, :], heads[:, h:h + 1], None, ALU.mult)
                last.then_inc(S["keys_pool"], 1)

            nc.gpsimd.memset(V2[:, 0, :, DH16], 1.0).then_inc(S["ones_col"], 1)
            nc.gpsimd.memset(V1[:, :, :, DH8], 1.0).then_inc(S["ones_col"], 1)
            nc.gpsimd.memset(raw[:, :, :, 0:TAPS - 1], 0.0).then_inc(S["pads_zero"], 1)
            by_head(0, 0, 0)
            pool.wait_ge(S["ready_weights"], 1)

            def stages(it):
                step = Chain(pool, S["pool_step"])

                def root(l, seed, done):
                    wait_for(S[seed], nth(it, l))
                    step(ts(stat[:, l, 5:6], stat[:, l, 2:3], 0.5, None, ALU.mult))
                    y = stat[:, l, 4:5]
                    for k in range(NEWTON):
                        step(ts(stat[:, l, 6:7], y, y, stat[:, l, 5:6], ALU.mult, ALU.mult))
                        step(ts(stat[:, l, 7:8], stat[:, l, 6:7], -1.0, 1.5, ALU.mult, ALU.add))
                        last = ts(stat[:, l, 8 + k:9 + k], y, stat[:, l, 7:8], None, ALU.mult)
                        if k + 1 < NEWTON:
                            step(last)
                        y = stat[:, l, 8 + k:9 + k]
                    last.then_inc(S[done], 1)

                def gain(l, t_ready, g, b, done):
                    wait_for(S[t_ready], nth(it, l))
                    step(tt(nrm[:, l, :], nrm[:, l, :], rows[g], ALU.mult))
                    tt(res[:, l, :], nrm[:, l, :], rows[b], ALU.add).then_inc(S[done], 1)

                def norms(seed, rstd, t_ready, g, b, done, after=None):
                    root(0, seed, rstd)
                    for l in range(G):
                        if l + 1 < G:
                            root(l + 1, seed, rstd)
                        gain(l, t_ready, g, b, done)
                        if after:
                            after(l)

                for l in range(G):
                    root(l, "seed1", "rstd1")
                def near0(l):
                    def d(k):
                        return dts[:, l, k, :]
                    evacuated(it, "xbc0", l)
                    step(tt(d(0), d(0), dt_bias, ALU.add))
                    step(ts(d(3), d(0), 0.0, None, ALU.max))
                    step(ts(d(1), d(3), -2.0, None, ALU.mult))
                    tt(d(2), d(0), d(1), ALU.add).then_inc(S["near0"], 1)

                def gated(l):
                    evacuated(it, "z", l)
                    step(ts(tz[:, l, :], tz[:, l, :], 1.0, None, ALU.add))
                    tt(zs[:, l, :], tz[:, l, :], zs[:, l, :], ALU.mult).then_inc(S["gated"], 1)

                def log_decays(l):
                    wait_for(S["dt"], nth(it, l))
                    step(tt(dts[:, l, 5, :], dts[:, l, 10, :], decay_rate, ALU.mult))
                    tt(decay[:, l, :, :], after.unsqueeze(1).broadcast_to((P, MH, P)),
                       dts[:, l, 5, :].unsqueeze(2).broadcast_to((P, MH, P)), ALU.mult).then_inc(S["am"], 1)

                near0(0)
                for l in range(G):
                    if l + 1 < G:
                        near0(l + 1)
                    log_decays(l)
                    gated(l)
                for l in range(G):
                    root(l, "seed2", "rstd2")
                for l in range(G):
                    root(l, "seed3", "rstd3")
                for l in range(G):
                    by_head(it, 1, l)

                def narrow(a_, first):
                    for l in range(G):
                        if first:
                            evacuated(it, f"Q{a_}", l)
                            tt(q_first[:, l, :, :], Q[:, l, :, 0].unsqueeze(2).broadcast_to((P, DC, 8)),
                               head16.unsqueeze(1).broadcast_to((P, DC, 8)), ALU.mult).then_inc(S[f"q{a_}_first"], 1)
                        by_head(it, a_, l)

                def drop(a_):
                    for l in range(G):
                        evacuated(it, f"V{a_}", l)
                        evacuated(it, f"n{a_}", l)
                        step(tt(V2[:, l, :, 0:DH16], V2[:, l, :, 0:DH16],
                                keep[:, l, :].unsqueeze(2).broadcast_to((P, H16, DH16)), ALU.mult))
                        copy(V2[:, l, :, DH16], keep[:, l, :]).then_inc(S[f"V{a_}"], 1)

                narrow(2, True)
                drop(2)
                norms("seed4", "rstd4", "t4", "g1", "b1", "x3")
                narrow(3, True)
                drop(3)
                norms("seed5", "rstd5", "t5", "g2", "b2", "x4")
                norms("seed6", "rstd6", "t6", "g3", "b3", "x5")
                for l in range(G):
                    evacuated(it, "V4", l)
                    nc.gpsimd.memset(V2[:, l, :, DH16], 1.0).then_inc(S["V4ones"], 1)
                narrow(4, False)

                def plus_bias(l):
                    wait_for(S["x6"], nth(it, l))
                    tt(plus[:, l, :], res[:, l, :], rows["down"], ALU.add).then_inc(S["plus"], 1)

                norms("seed7", "rstd7", "t7", "g4", "b4", "x6", plus_bias)

            with pool.Fori(0, ITERS) as it:
                stages(it)


def constants():
    import numpy as np

    p, k = np.arange(P)[:, None], np.arange(P)[None, :]
    c = {
        "ident": p == k,
        "before": p <= k,
        "gate": 0.25 * (p <= k),
        "after": p > k,
        "causal": np.where(k > p, MASKED, 0),
        "head16": p // DH16 == np.arange(8)[None, :],
        "head32": p // DH8 == np.arange(4)[None, :],
        "index": p,
    }
    return np.concatenate([np.asarray(c[n], np.float32) for n in CONST_COLS], axis=1)


def kernel(**inputs):
    import numpy as np
    import concourse.bacc as bacc
    from concourse.bass_utils import run_bass_kernel_spmd

    def arr(name):
        return np.asarray(inputs[name])

    def by_head(name):
        w = arr(name)
        return w.transpose(1, 0, 2).reshape(w.shape[1], -1)

    a = {"x": arr("x"), "ctx_1024": arr("ctx_1024"), "const": constants(), "pad": arr("mask_1xS2_bf0").view(np.int32)}
    for n in "qkv":
        a[n + "0"] = arr(f"L0_xattn_W{n}").T
        a[n + "1"] = arr(f"L1_xattn_W{n}")
        a[n + "2"] = by_head(f"L2_xattn_W{n}1")
        a[n + "3"] = by_head(f"L2_xattn_W{n}2")
        a[n + "4"] = arr(f"L3_xattn_W{n}").T
    a["o1"] = arr("L1_xattn_Wo")
    a["in_proj"], a["out_proj"] = arr("L1_xattn_in_proj_w"), arr("L1_xattn_out_proj_w")
    a["fc1"], a["fc2"] = arr("L2_xattn_fc1_w").T, arr("L2_xattn_fc2_w").T
    a["up"], a["down"] = arr("L3_xattn_W1").T, arr("L3_xattn_W2").T
    vectors = dict(
        m_norm="L1_xattn_m_norm_w", g_norm="L1_xattn_gnorm_w", conv_w="L1_xattn_conv_w", conv_b="L1_xattn_conv_b",
        ca_w="L1_xattn_ca_ln_w", ca_b="L1_xattn_ca_ln_b", fc1_b="L2_xattn_fc1_b", q4_b="L3_xattn_bq",
        k4_b="L3_xattn_bk", up_b="L3_xattn_b1")
    a["vectors"] = np.concatenate(
        [arr(vectors[n]).reshape(-1, P, arr(vectors[n]).size // len(arr(vectors[n])))
         .transpose(1, 0, 2).reshape(P, VECTORS[n]) for n in VECTORS], axis=1)
    rows = dict(
        g1="L2_xattn_ln1_g", b1="L2_xattn_ln1_b", g2="L2_xattn_ln2_g", b2="L2_xattn_ln2_b", g3="L2_xattn_ln3_g",
        b3="L2_xattn_ln3_b", g4="L3_xattn_ln_g", b4="L3_xattn_ln_b", fc2="L2_xattn_fc2_b", v4="L3_xattn_bv",
        down="L3_xattn_b2", dt_bias="L1_xattn_dt_bias", A_log="L1_xattn_A_log", D_skip="L1_xattn_D_skip")
    a["rows"] = np.concatenate([arr(rows[n]) for n in ROWS])

    nc = bacc.Bacc("TRN2", target_bir_lowering=False, num_devices=1)
    arrays, views = {}, {}
    for n, v in a.items():
        v = np.ascontiguousarray(v)
        arrays["in_" + n] = v
        views[n] = nc.dram_tensor("in_" + n, v.shape, mybir.dt.from_np(v.dtype), kind="ExternalInput").ap()
    out = nc.dram_tensor("out_0", (B, P, D), F32, kind="ExternalOutput").ap()
    decoder_stack(nc, views, out)
    r = run_bass_kernel_spmd(nc, [arrays], core_ids=[0])
    return r.results[0]["out_0"]
```

```python
from contextlib import ExitStack

import concourse.bass as bass
from concourse import mybir

F32 = mybir.dt.float32
BF16 = mybir.dt.bfloat16
I32 = mybir.dt.int32
U8 = mybir.dt.uint8
ALU = mybir.AluOpType
ACT = mybir.ActivationFunctionType
AX_X = mybir.AxisListType.X

P = 128
B = 32
D = 256
DC = D // P
G = 4
ITERS = B // G
INNER = 512
IC = INNER // P
STATE = 128
MH = 8
MD = INNER // MH
TAPS = 4
XBC = (INNER + 2 * STATE) // P
BCH, CCH = XBC - 2, XBC - 1
IN_PROJ = 2 * INNER + 2 * STATE + MH
FF = 1024
FC = FF // P
H16, DH16 = 16, 16
H8, DH8 = 8, 32
EPS = 1e-5
MASKED = -float(2 ** 30)
SCALE8 = 0.1767766922712326
MAGIC = float(0x5F3759DF)
NEWTON = 3
LOG1P_TERMS = 8

CONST_COLS = dict(ident=P, before=P, gate=P, after=P, causal=P, head16=8, head32=4, index=1)
CONST_AT = {n: sum(list(CONST_COLS.values())[:i]) for i, n in enumerate(CONST_COLS)}
CONST_WIDTH = sum(CONST_COLS.values())
VECTORS = dict(m_norm=DC, g_norm=IC, conv_w=XBC * TAPS, conv_b=XBC, ca_w=DC, ca_b=DC, fc1_b=DC, q4_b=DC, k4_b=DC, up_b=FC)
VECTOR_AT = {n: sum(list(VECTORS.values())[:i]) for i, n in enumerate(VECTORS)}
VECTOR_WIDTH = sum(VECTORS.values())
ROWS = dict(g1=D, b1=D, g2=D, b2=D, g3=D, b3=D, g4=D, b4=D, fc2=D, v4=D, down=D, dt_bias=MH, A_log=MH, D_skip=MH)
ROW_AT = {n: sum(list(ROWS.values())[:i]) for i, n in enumerate(ROWS)}
ROW_WIDTH = sum(ROWS.values())

TASKS = dict(
    xhatT=(-45.77, 0.05), dt=(-43.7, 0), xbc=(-20.09, 1.81), z=(-18.3, 2.32), ctxT=(-20.33, 0.09),
    softplus=(-29.19, 0), am=(-21.46, 0.31), conv=(-18.27, 2.33), K1=(-16.59, 3), V1=(-15.95, 2), silu=(-16.37, 2.86),
    pairs=(-16.19, 3.28), decayed=(-14.68, 3.68), Y=(-13.04, 3.2), uT=(-12.57, 3.48), keys1=(-7.12, 3.37),
    proj=(-10.92, 3.73), xnT=(-7.33, 3.37), Q1=(-6.18, 3.72), finish1=(3.75, 2.39), oT=(4.69, 2.74), Wo=(5.3, 2.9),
    x2T=(5.73, 2.88), K2=(6.2, 3.03), keys2=(6.61, 3.32), Q2=(6.79, 3.34), V2=(6.55, 4.03), e2=(8.49, 3.68),
    n2=(9.07, 4.26), finish2=(14.15, 4.14), norm2=(15.61, 3.84), x3T=(17.62, 3.76), row=(19.91, 3.91),
    K3=(20.07, 3.99), keys3=(20.68, 4.66), Q3=(22.85, 2.33), V3=(20.96, 5.18), e3=(24.29, 2.66), n3=(26.05, 3.17),
    finish3=(30.73, 3.91), norm3=(32.97, 3.62), K4=(32.07, 2.2), keys4=(32.55, 4.99), V4=(38.26, 4.52),
    x4T=(33.93, 3.75), fc1=(34.49, 4.07), fc2=(35.57, 3.74), norm4=(38.33, 3.07), x5T=(38.94, 3.32), Q4=(39.06, 3.83),
    finish4=(46.33, 4.11), norm5=(48.52, 3.38), x6T=(51.08, 3.22), up=(56.12, 2.31), down=(62.85, 5.08),
    x1=(52.42, 5.45), xhat=(65.05, 1.67), scores=(0, 1), turn=(1.42, 1), values=(3.17, 1))


def in_order(tasks, lanes):
    order = [(TASKS[task][0] + lane * TASKS[task][1], task, lane) for task in tasks for lane in range(lanes(task))]
    return [(task, lane) for step, task, lane in sorted(order)]


HEADS = 4
PARTS = {0: 4, 1: 2, 2: 4, 3: 4, 4: 4}
PASS_PARTS = [(a_, l, t) for a_ in range(1, 5) for l in range(G) for t in range(PARTS[a_])]
FIRST_PARTS = [(0, 0, t) for t in range(PARTS[0])]
SCORE_BANKS = 3
SHIFTED_BUFFERS = 4
WEIGHT_BUFFERS = 4
assert len(PASS_PARTS) % SHIFTED_BUFFERS == 0 and len(PASS_PARTS) % WEIGHT_BUFFERS == 0
PART_TASKS = ("scores", "turn", "values")
TASK_LANES = dict(dt=1, softplus=1, ctxT=2)
PASS = in_order(TASKS, lambda task: len(PASS_PARTS) if task in PART_TASKS else TASK_LANES.get(task, G))
FIRST = in_order(PART_TASKS, lambda task: len(FIRST_PARTS))

RING_JOBS = dict(xbc="xbc0 xbc1", pairs="CB xh", up="up0 up1")
NO_RING = ("softplus conv silu am decayed keys1 keys2 keys3 keys4 turn scores values finish1 finish2 finish3 finish4 "
           "norm2 norm3 norm4 norm5 x1 xhat").split()
RING_BANKS = 3
JOBS = [(what, lane) for task, lane in PASS if task not in NO_RING for what in RING_JOBS.get(task, task).split()]
JOB_AT = {job: n for n, job in enumerate(JOBS)}
assert len(JOB_AT) == len(JOBS) and len(JOBS) % RING_BANKS == 0
USES = len(JOBS) // RING_BANKS
FIRST_JOBS = ["x0T", "c0T", "Q0", "K0", "V0", "bias0", "bias1"]


def job(it, what, lane=0):
    if what in FIRST_JOBS:
        n = FIRST_JOBS.index(what)
        return n % RING_BANKS, n // RING_BANKS
    n = len(FIRST_JOBS) + JOB_AT[what, lane]
    return n % RING_BANKS, it * USES + n // RING_BANKS


def nth(it, lane):
    return it * G + (lane + 1)


def part_of(it, p):
    return FIRST_PARTS[p] if it is None else PASS_PARTS[p]


def part(it, p):
    return p if it is None else it * len(PASS_PARTS) + (len(FIRST_PARTS) + p)


def nth_output(it, a_, l):
    return 1 if a_ == 0 else it * 4 * G + (1 + (a_ - 1) * G + l + 1)


class Chain:

    def __init__(self, eng, sem):
        self.eng, self.sem, self.count = eng, sem, 0
        eng.sem_clear(sem)

    def __call__(self, instruction):
        self.count += 1
        instruction.then_inc(self.sem, 1)
        self.eng.wait_ge(self.sem, self.count)


def decoder_stack(nc, a, out):
    ctx = ExitStack()
    with ctx:
        def sb(name, shape, dt=F32):
            return ctx.enter_context(nc.sbuf_tensor(name, shape, dt))

        def pb(name, shape):
            return ctx.enter_context(nc.psum_tensor(name, shape, F32))

        def sem(name):
            return ctx.enter_context(nc.semaphore(name))

        const = sb("const", [P, CONST_WIDTH])

        def con(name):
            return const[:, CONST_AT[name]:CONST_AT[name] + CONST_COLS[name]]

        ident, before, gate_mask, after = con("ident"), con("before"), con("gate"), con("after")
        head16, head32, index = con("head16"), con("head32"), con("index")
        ident_bf = sb("ident_bf", [P, P], BF16)
        ones_bf = sb("ones_bf", [P, P], BF16)
        causal_bf = sb("causal_bf", [P, P], BF16)

        w_in = sb("w_in", [P, DC, IN_PROJ])
        w_out = sb("w_out", [P, IC, D])
        square = {n: sb(f"w_{n}", [P, DC, D]) for n in (
            "q1", "k1", "v1", "o1", "q2", "k2", "v2", "q3", "k3", "v3", "fc1", "fc2", "q4", "k4", "v4")}
        w_up = sb("w_up", [P, DC, FF])
        w_down = sb("w_down", [P, FC, D])
        vectors = sb("vectors", [P, VECTOR_WIDTH])

        def vec(name):
            return vectors[:, VECTOR_AT[name]:VECTOR_AT[name] + VECTORS[name]]

        m_norm, g_norm, conv_b, ca_w, ca_b = (vec(n) for n in ("m_norm", "g_norm", "conv_b", "ca_w", "ca_b"))
        conv_w = vec("conv_w").rearrange("p (c k) -> p c k", c=XBC)
        fc1_b, q4_b, k4_b, up_b = (vec(n) for n in ("fc1_b", "q4_b", "k4_b", "up_b"))
        q1_bias = sb("q1_bias", [P, DC])
        row_all = sb("row_all", [P, ROW_WIDTH])
        rows = {n: row_all[:, ROW_AT[n]:ROW_AT[n] + ROWS[n]] for n in ROWS}
        dt_bias, decay_rate, skip = rows["dt_bias"], rows["A_log"], rows["D_skip"]
        pad_u8 = sb("pad_u8", [P, P], U8)
        keep_row = sb("keep_row", [P, P])
        padding_bf = sb("padding_bf", [P, P], BF16)

        x_in = sb("x_in", [P, G, D])
        c_in = sb("c_in", [P, G, D])
        cT = sb("cT", [P, G, DC, P])
        att0 = sb("att0", [P, D])
        res = sb("res", [P, G, D])
        nrm = sb("nrm", [P, G, D])
        actT = sb("actT", [P, G, DC, P])
        raw = sb("raw", [P, G, XBC, TAPS - 1 + P])
        att = sb("att", [P, G, D])
        result = sb("result", [P, G, D])
        fc1T = sb("fc1T", [P, G, DC, P])
        plus = fc1T[:, :, :, :].rearrange("p g c k -> p g (c k)")
        state_gate = sb("state_gate", [P, G, P])
        stat = sb("stat", [P, G, 16])
        bn = sb("bn", [P, G, 6])
        dts = sb("dts", [P, 12, G, MH])
        rec = sb("rec", [P, G, H16])
        mask0 = sb("mask0", [P, G, 2])
        mask1 = sb("mask1", [P, G, 2])
        mask1_bf = sb("mask1_bf", [P, G], BF16)
        row_mask = sb("row_mask", [P, G, P])
        q_first = sb("q_first", [P, G, DC, 8])
        nonzero = sb("nonzero", [P, G, H16], BF16)
        keep = sb("keep", [P, G, H16])
        neg_max = sb("neg_max", [P, 2, HEADS])
        K1 = sb("K1", [P, G, DC, P])
        V1 = sb("V1", [P, G, H8, DH8 + 1])
        V2 = sb("V2", [P, G, H16, DH16 + 1])

        MAMBA = dict(decay=G * MH * P, conv=G * XBC * P, zs=G * INNER, dbx=G * INNER, dx=G * INNER, tz=G * INNER)
        space = sb("space", [P, sum(MAMBA.values())])
        at, mamba = 0, {}
        for n, width in MAMBA.items():
            mamba[n] = space[:, at:at + width]
            at += width
        decay = mamba["decay"].rearrange("p (g h k) -> p g h k", g=G, h=MH)
        conv = mamba["conv"].rearrange("p (g c k) -> p g c k", g=G, c=XBC)
        dbx, dx, zs, tz = (mamba[n].rearrange("p (g n) -> p g n", g=G) for n in ("dbx", "dx", "zs", "tz"))
        uT = mamba["tz"].rearrange("p (g c k) -> p g c k", g=G, c=IC)
        keys32 = space[:, 0:G * DC * 4 * P].rearrange("p (g c h k) -> p g c h k", g=G, c=DC, h=4)
        keys16 = space[:, 0:G * DC * 8 * P].rearrange("p (g c h k) -> p g c h k", g=G, c=DC, h=8)
        K2 = space[:, G * DC * 8 * P:G * DC * 9 * P].rearrange("p (g c k) -> p g c k", g=G, c=DC)
        assert G * DC * 9 * P <= MAMBA["decay"] + MAMBA["conv"] + MAMBA["zs"]
        Q = mamba["dbx"].rearrange("p (g c k) -> p g c k", g=G, c=2 * DC)[:, :, 0:DC, :]
        shifted = mamba["dx"].rearrange("p (s n) -> p s n", s=SHIFTED_BUFFERS)
        weights = mamba["tz"].rearrange("p (s n) -> p s n", s=WEIGHT_BUFFERS)
        gT = decay
        w0 = {n: mamba["conv"][:, i * DC * D:(i + 1) * DC * D].rearrange("p (c n) -> p c n", c=DC)
              for i, n in enumerate(("q0", "k0", "v0"))}

        bank = [pb(f"ring{i}", [P, 512]) for i in range(RING_BANKS)]
        score = pb("score", [P, SCORE_BANKS, 512])
        turned = pb("turned", [P, 512])
        output = pb("output", [P, 512])

        bank_full = [sem(f"bank_full{i}") for i in range(RING_BANKS)]
        bank_read = [sem(f"bank_read{i}") for i in range(RING_BANKS)]
        S = {n: sem(n) for n in (
            "const_in w0_in wmamba_in w1_in w2_in w3_in x_in c_in stored "
            "ready_consts ready_in ready_weights ones_col pads_zero rates "
            "dve_first dve_step pool_step pool_waits "
            "x1 ss1 seed1 rstd1 xhat near0 edt dt am conv tanh xbc gated "
            "log_decay decay M u ss2 seed2 rstd2 seed3 rstd3 xn "
            "q2_first V2 seed4 rstd4 x3 m1 q3_first V3 seed5 rstd5 x4 "
            "seed6 rstd6 x5 V4ones seed7 rstd7 x6 plus "
            "keys0_dve keys0_act keys1_dve keys1_act keys2_dve keys2_act keys3_dve keys3_act keys4_dve keys4_act "
            "output_full output_read scores shifted exps turned weights").split()}

        x_v = a["x"].rearrange("(i g) t d -> i t g d", g=G)
        c_v = a["ctx_1024"].rearrange("(i g) t d -> i t g d", g=G)
        o_v = out.rearrange("(i g) t d -> i t g d", g=G)
        block = ctx.enter_context(nc.Block())

        SHARE16 = dict(dve=range(0, 4), act=range(4, 8))
        SHARE32 = dict(dve=range(0, 2), act=range(2, 4))

        @block.sync
        def _(sp):
            def chunks(name):
                return a[name].rearrange("(c p) n -> p c n", p=P)

            sp.sem_inc(S["stored"], 16)
            sp.dma_start(const[:, :], a["const"]).then_inc(S["const_in"], 16)
            sp.dma_start(x_in[:, :, :], x_v[0]).then_inc(S["x_in"], 16)
            sp.dma_start(c_in[:, :, :], c_v[0]).then_inc(S["c_in"], 16)
            for n in ("q0", "k0", "v0"):
                sp.dma_start(w0[n], chunks(n)).then_inc(S["w0_in"], 16)
            for dst, src in ((w_in[:, :, :], chunks("in_proj")), (w_out[:, :, :], chunks("out_proj")),
                             (vectors[:, :], a["vectors"]), (row_all[:, :], a["rows"].partition_broadcast(P)),
                             (pad_u8[:, :], a["pad"].bitcast(U8)[0].partition_broadcast(P))):
                sp.dma_start(dst, src).then_inc(S["wmamba_in"], 16)
            for n in ("q1", "k1", "v1", "o1"):
                sp.dma_start(square[n][:, :, :], chunks(n)).then_inc(S["w1_in"], 16)
            for n in ("q2", "k2", "v2", "q3", "k3", "v3", "fc1", "fc2"):
                sp.dma_start(square[n][:, :, :], chunks(n)).then_inc(S["w2_in"], 16)
            for dst, src in ([(square[n][:, :, :], chunks(n)) for n in ("q4", "k4", "v4")]
                             + [(w_up[:, :, :], chunks("up")), (w_down[:, :, :], chunks("down"))]):
                sp.dma_start(dst, src).then_inc(S["w3_in"], 16)

            def store(it):
                b, use = job(it, "down", G - 1)
                sp.wait_ge(bank_read[b], use + 1)
                sp.dma_start(o_v[it], result[:, :, :]).then_inc(S["stored"], 16)

            with sp.Fori(0, ITERS - 1) as it:
                sp.wait_ge(S["x1"], nth(it, G - 1))
                sp.dma_start(x_in[:, :, :], x_v[it + 1]).then_inc(S["x_in"], 16)
                bank_, use = job(it, "ctxT", G // 2 - 1)
                sp.wait_ge(bank_full[bank_], use + 1)
                sp.dma_start(c_in[:, :, :], c_v[it + 1]).then_inc(S["c_in"], 16)
                store(it)
            sp.wait_ge(S["x_in"], 16 * ITERS)
            sp.sem_inc(S["x_in"], 16)
            store(ITERS - 1)
            sp.wait_ge(S["stored"], 16 * (ITERS + 1))

        @block.tensor
        def _(pe):
            mm = nc.tensor.matmul

            def claim(it, what, lane=0):
                b, use = job(it, what, lane)
                if what not in FIRST_JOBS or use:
                    pe.wait_ge(bank_read[b], use)
                return bank[b], bank_full[b]

            def evacuated(it, what, lane=0, then=None):
                assert then is None or JOB_AT[what, lane] < JOB_AT[then]
                b, use = job(it, what, lane)
                if then is None or job(it, *then)[0] != b:
                    pe.wait_ge(bank_read[b], use + 1)

            def flip(it, what, lane, src, n):
                t, full = claim(it, what, lane)
                for c in range(n):
                    last = nc.tensor.transpose(t[:, c * P:(c + 1) * P], src[:, c * P:(c + 1) * P], ident)
                last.then_inc(full, 1)

            def to_channels(t, at, w, cols, xT, n=DC):
                for c in range(n):
                    last = mm(t[:, at:at + P], w[:, c, cols:cols + P], xT[:, c, :], start=(c == 0), stop=(c == n - 1))
                return last

            def to_tokens(t, at, w, lo, hi, xT, n=DC):
                for c in range(n):
                    last = mm(t[:, at:at + hi - lo], xT[:, c, :], w[:, c, lo:hi], start=(c == 0), stop=(c == n - 1))
                return last

            def project_T(it, what, lane, w, xT):
                t, full = claim(it, what, lane)
                for m in range(DC):
                    last = to_channels(t, m * P, w, m * P, xT)
                last.then_inc(full, 1)

            def project(it, what, lane, w, xT, n=DC):
                t, full = claim(it, what, lane)
                to_tokens(t, 0, w, 0, D, xT, n).then_inc(full, 1)

            masks = {0: None, 1: padding_bf, 2: causal_bf, 3: None, 4: causal_bf}

            def scores(it, p):
                a_, l, t = part_of(it, p)
                c, h = t * DC // PARTS[a_], t % (PARTS[a_] // DC) * HEADS
                keys = keys32 if a_ == 1 else keys16
                if p >= SCORE_BANKS:
                    pe.wait_ge(S["shifted"], part(it, p - SCORE_BANKS) + 1)
                elif it is not None:
                    pe.wait_ge(S["shifted"], part(it, 0))
                if t == 0:
                    evacuated(it, f"Q{a_}", l)
                    for eng in ("dve", "act"):
                        pe.wait_ge(S[f"keys{a_}_{eng}"], nth(it, l) if a_ else 1)
                to, mask = score[:, p % SCORE_BANKS, :], masks[a_]
                last = mm(to, Q[:, l, c, :], keys[:, l, c, h:h + HEADS, :], start=True, stop=(mask is None))
                if mask is not None:
                    last = mm(to, ident_bf[:, :], mask[:, :].unsqueeze(1).broadcast_to((P, HEADS, P)),
                              start=False, stop=True)
                last.then_inc(S["scores"], 1)

            def turn(it, p):
                if it is not None or p:
                    pe.wait_ge(S["weights"], part(it, p))
                pe.wait_ge(S["exps"], part(it, p) + 1)
                for i in range(HEADS):
                    last = nc.tensor.transpose(turned[:, i * P:(i + 1) * P],
                                               shifted[:, p % SHIFTED_BUFFERS, i * P:(i + 1) * P], ident)
                last.then_inc(S["turned"], 1)

            def values(it, p):
                a_, l, t = part_of(it, p)
                V, dh = (V1, DH8) if a_ == 1 else (V2, DH16)
                if t == 0:
                    if a_:
                        pe.wait_ge(S["output_read"], nth_output(it, a_, l) - 1)
                    if a_ in (0, 1):
                        evacuated(it, f"V{a_}", l)
                        if a_ == 0:
                            pe.wait_ge(S["ones_col"], 2)
                    else:
                        pe.wait_ge(S[{2: "V2", 3: "V3", 4: "V4ones"}[a_]], nth(it, l))
                pe.wait_ge(S["weights"], part(it, p) + 1)
                for i in range(HEADS):
                    h = t * HEADS + i
                    last = mm(output[:, h * (dh + 1):(h + 1) * (dh + 1)],
                              weights[:, p % WEIGHT_BUFFERS, i * P:(i + 1) * P], V[:, l, h, :], start=True, stop=True)
                if t == PARTS[a_] - 1:
                    last.then_inc(S["output_full"], 1)

            pe.wait_ge(S["const_in"], 16)
            pe.wait_ge(S["x_in"], 16)
            flip(0, "x0T", 0, x_in[:, 0, :], DC)
            pe.wait_ge(S["c_in"], 16)
            flip(0, "c0T", 0, c_in[:, 0, :], DC)
            pe.wait_ge(S["w0_in"], 16 * 3)
            evacuated(0, "x0T")
            project_T(0, "Q0", 0, w0["q0"], actT[:, 0])
            evacuated(0, "c0T")
            project_T(0, "K0", 0, w0["k0"], cT[:, 0])
            project(0, "V0", 0, w0["v0"], cT[:, 0])
            pe.wait_ge(S["ready_consts"], 1)
            first = dict(scores=scores, turn=turn, values=values)
            for task, p in FIRST:
                first[task](None, p)
            pe.wait_ge(S["wmamba_in"], 16 * 5)
            pe.wait_ge(S["w1_in"], 16 * 4)
            for m in range(DC):
                t, full = claim(0, f"bias{m}")
                for c in range(DC):
                    last = mm(t[:, 0:1], square["q1"][:, c, m * P:(m + 1) * P], ca_b[:, c:c + 1],
                              start=(c == 0), stop=(c == DC - 1))
                last.then_inc(full, 1)
            pe.wait_ge(S["ready_in"], 1)

            def ctxT(it, half):
                if half == 0:
                    pe.wait_ge(S["c_in"], it * 16 + 16)
                flip(it, "ctxT", half, c_in[:, 2 * half:2 * half + 2, :].rearrange("p l n -> p (l n)"), 2 * DC)

            def K_1(it, l):
                evacuated(it, "ctxT", l // 2, ("K1", l))
                project_T(it, "K1", l, square["k1"], cT[:, l])

            def V_1(it, l):
                evacuated(it, "ctxT", l // 2, ("V1", l))
                project(it, "V1", l, square["v1"], cT[:, l])

            def xhatT(it, l):
                pe.wait_ge(S["xhat"], nth(it, l))
                flip(it, "xhatT", l, nrm[:, l, :], DC)

            def dt(it, _):
                t, full = claim(it, "dt")
                for l in range(G):
                    evacuated(it, "xhatT", l, ("dt", 0))
                    last = to_tokens(t, l * MH, w_in, IN_PROJ - MH, IN_PROJ, actT[:, l])
                last.then_inc(full, 1)

            def xbc(it, l):
                evacuated(it, "xhatT", l, ("xbc0", l))
                for half in range(2):
                    t, full = claim(it, f"xbc{half}", l)
                    for k in range(XBC // 2):
                        last = to_channels(t, k * P, w_in, INNER + (half * XBC // 2 + k) * P, actT[:, l])
                    last.then_inc(full, 1)

            def z(it, l):
                evacuated(it, "xhatT", l, ("z", l))
                t, full = claim(it, "z", l)
                to_tokens(t, 0, w_in, 0, INNER, actT[:, l]).then_inc(full, 1)

            def pairs(it, l):
                pe.wait_ge(S["xbc"], nth(it, l))
                t, full = claim(it, "CB", l)
                mm(t[:, 0:P], conv[:, l, BCH, :], conv[:, l, CCH, :], start=True, stop=True).then_inc(full, 1)
                flip(it, "xh", l, conv[:, l, 0:IC, :].rearrange("p c k -> p (c k)"), IC)
                pe.wait_ge(S["am"], nth(it, l))
                if l:
                    pe.wait_ge(S["decay"], nth(it, l - 1))
                else:
                    pe.wait_ge(S["shifted"], part(it, 0))
                for h in range(MH):
                    b, at = h // 4, h % 4 * P
                    last = mm(score[:, b, at:at + P], decay[:, l, h, :], before, start=(at == 0), stop=(h % 4 == 3))
                last.then_inc(S["log_decay"], 1)

            def Y(it, l):
                t, full = claim(it, "Y", l)
                evacuated(it, "xh", l, ("Y", l))
                pe.wait_ge(S["M"], nth(it, l))
                for h in range(MH):
                    last = mm(t[:, h * MD:(h + 1) * MD], decay[:, l, h, :], dbx[:, l, h * MD:(h + 1) * MD],
                              start=True, stop=True)
                last.then_inc(full, 1)

            def flip_u(it, l):
                pe.wait_ge(S["u"], nth(it, l))
                flip(it, "uT", l, zs[:, l, :], IC)

            def proj(it, l):
                if l == 0:
                    pe.wait_ge(S["ready_weights"], 1)
                evacuated(it, "uT", l, ("proj", l))
                project(it, "proj", l, w_out, uT[:, l], IC)

            def xnT(it, l):
                pe.wait_ge(S["xn"], nth(it, l))
                flip(it, "xnT", l, nrm[:, l, :], DC)

            def Q1(it, l):
                evacuated(it, "xnT", l, ("Q1", l))
                project_T(it, "Q1", l, square["q1"], actT[:, l])

            def oT(it, l):
                pe.wait_ge(S["output_read"], nth_output(it, 1, l))
                flip(it, "oT", l, att[:, l, :], DC)

            def Wo(it, l):
                evacuated(it, "oT", l, ("Wo", l))
                project(it, "Wo", l, square["o1"], actT[:, l])

            def x2T(it, l):
                if l == 0:
                    pe.wait_ge(S["w2_in"], 16 * 8)
                evacuated(it, "Wo", l, ("x2T", l))
                flip(it, "x2T", l, res[:, l, :], DC)

            def Q2(it, l):
                evacuated(it, "x2T", l, ("Q2", l))
                project_T(it, "Q2", l, square["q2"], actT[:, l])

            def K_2(it, l):
                evacuated(it, "x2T", l, ("K2", l))
                project_T(it, "K2", l, square["k2"], actT[:, l])

            def V_2(it, l):
                evacuated(it, "x2T", l, ("V2", l))
                project(it, "V2", l, square["v2"], actT[:, l])

            def first_scores(it, a_, l):
                t, full = claim(it, f"e{a_}", l)
                evacuated(it, f"K{a_}", l, (f"e{a_}", l))
                pe.wait_ge(S[f"q{a_}_first"], nth(it, l))
                for c in range(DC):
                    last = mm(t[:, c * 8:c * 8 + 8], K2[:, l, c, :], q_first[:, l, c, :], start=True, stop=True)
                last.then_inc(full, 1)

            def count_nonzero(it, a_, l):
                t, full = claim(it, f"n{a_}", l)
                evacuated(it, f"e{a_}", l, (f"n{a_}", l))
                mm(t[:, 0:H16], ones_bf[:, :], nonzero[:, l, :], start=True, stop=True).then_inc(full, 1)

            def x3T(it, l):
                pe.wait_ge(S["x3"], nth(it, l))
                flip(it, "x3T", l, res[:, l, :], DC)

            def row(it, l):
                t, full = claim(it, "row", l)
                pe.wait_ge(S["m1"], nth(it, l))
                mm(t[:, 0:P], mask1_bf[:, l:l + 1].broadcast_to((P, P)), ident_bf[:, :],
                   start=True, stop=True).then_inc(full, 1)

            def Q3(it, l):
                evacuated(it, "x3T", l, ("Q3", l))
                project_T(it, "Q3", l, square["q3"], actT[:, l])

            def K3(it, l):
                project_T(it, "K3", l, square["k3"], cT[:, l])

            def V3(it, l):
                project(it, "V3", l, square["v3"], cT[:, l])

            def x4T(it, l):
                pe.wait_ge(S["x4"], nth(it, l))
                flip(it, "x4T", l, res[:, l, :], DC)

            def fc1(it, l):
                evacuated(it, "x4T", l, ("fc1", l))
                project_T(it, "fc1", l, square["fc1"], actT[:, l])

            def fc2(it, l):
                evacuated(it, "fc1", l, ("fc2", l))
                project(it, "fc2", l, square["fc2"], fc1T[:, l])

            def K4(it, l):
                if l == 0:
                    pe.wait_ge(S["w3_in"], 16 * 5)
                project_T(it, "K4", l, square["k4"], cT[:, l])

            def V4(it, l):
                project(it, "V4", l, square["v4"], cT[:, l])

            def x5T(it, l):
                pe.wait_ge(S["x5"], nth(it, l))
                flip(it, "x5T", l, res[:, l, :], DC)

            def Q4(it, l):
                evacuated(it, "x5T", l, ("Q4", l))
                project_T(it, "Q4", l, square["q4"], actT[:, l])

            def x6T(it, l):
                pe.wait_ge(S["x6"], nth(it, l))
                flip(it, "x6T", l, res[:, l, :], DC)

            def up(it, l):
                evacuated(it, "x6T", l, ("up0", l))
                for half in range(2):
                    t, full = claim(it, f"up{half}", l)
                    for k in range(FC // 2):
                        last = to_channels(t, k * P, w_up, (half * FC // 2 + k) * P, actT[:, l])
                    last.then_inc(full, 1)

            def down(it, l):
                evacuated(it, "up0", l, ("down", l))
                evacuated(it, "up1", l, ("down", l))
                project(it, "down", l, w_down, gT[:, l], FC)

            do = dict(ctxT=ctxT, K1=K_1, V1=V_1, xhatT=xhatT, dt=dt, xbc=xbc, z=z, pairs=pairs, Y=Y, uT=flip_u, proj=proj, xnT=xnT,
                      Q1=Q1, oT=oT, Wo=Wo, x2T=x2T, Q2=Q2, K2=K_2, V2=V_2, x3T=x3T, row=row, Q3=Q3, K3=K3, V3=V3, x4T=x4T,
                      fc1=fc1, fc2=fc2, K4=K4, V4=V4,
                      x5T=x5T, Q4=Q4, x6T=x6T, up=up, down=down, scores=scores, turn=turn, values=values,
                      e2=lambda it, l: first_scores(it, 2, l), n2=lambda it, l: count_nonzero(it, 2, l),
                      e3=lambda it, l: first_scores(it, 3, l), n3=lambda it, l: count_nonzero(it, 3, l))
            with pe.Fori(0, ITERS) as it:
                for task, lane in PASS:
                    if task in do:
                        do[task](it, lane)

        @block.scalar
        def _(act):
            run = nc.scalar.activation

            def filled(it, what, lane=0):
                b, use = job(it, what, lane)
                act.wait_ge(bank_full[b], use + 1)
                return bank[b], bank_read[b]

            def copy_out(it, what, lane, dst, n):
                t, read = filled(it, what, lane)
                nc.scalar.copy(dst.rearrange("p c k -> p (c k)"), t[:, 0:n]).then_inc(read, 1)

            def by_head(it, a_, lane):
                evacuated(it, f"K{a_}", lane)
                if a_ == 1:
                    filled(it, "Y", lane)
                    K, keys, heads, share = K1, keys32, head32, SHARE32["act"]
                else:
                    K, keys, heads, share = K2, keys16, head16, SHARE16["act"]
                for h in share:
                    last = run(keys[:, lane, :, h, :], K[:, lane, :, :], ACT.Copy, scale=heads[:, h:h + 1])
                last.then_inc(S[f"keys{a_}_act"], 1)

            def evacuated(it, what, lane=0):
                b, use = job(it, what, lane)
                act.wait_ge(bank_read[b], use + 1)

            def values_out(it, what, lane, V, heads, dh, scale=1.0):
                t, read = filled(it, what, lane)
                run(V[:, lane, :, 0:dh], t[:, 0:D].rearrange("p (h e) -> p h e", h=heads), ACT.Copy,
                    scale=scale).then_inc(read, 1)

            def exponential(it, p):
                a_, l, t = part_of(it, p)
                act.wait_ge(S["shifted"], part(it, p) + 1)
                e = shifted[:, p % SHIFTED_BUFFERS, :]
                run(e, e, ACT.Exp, scale=SCALE8 if a_ == 1 else 0.25).then_inc(S["exps"], 1)

            def turned_out(it, p):
                act.wait_ge(S["turned"], part(it, p) + 1)
                nc.scalar.copy(weights[:, p % WEIGHT_BUFFERS, :], turned[:, :]).then_inc(S["weights"], 1)

            def x1(it, l):
                act.wait_ge(S["x1"], nth(it, l))
                run(nrm[:, l, :], res[:, l, :], ACT.Square, accum_out=stat[:, l, 12:13]).then_inc(S["ss1"], 1)

            copy_out(0, "x0T", 0, actT[:, 0], D)
            copy_out(0, "c0T", 0, cT[:, 0], D)
            copy_out(0, "Q0", 0, Q[:, 0], D)
            copy_out(0, "K0", 0, K2[:, 0], D)
            by_head(0, 0, 0)
            values_out(0, "V0", 0, V2, H16, DH16)
            first = dict(scores=exponential, turn=turned_out)
            for task, p in FIRST:
                if task in first:
                    first[task](None, p)
            act.wait_ge(S["wmamba_in"], 16 * 5)
            run(decay_rate, decay_rate, ACT.Exp).then_inc(S["rates"], 1)
            for l in range(G):
                x1(0, l)
            act.wait_ge(S["pads_zero"], 1)

            def copied(what, n=D):
                return lambda it, l: copy_out(it, what, l, actT[:, l], n)

            def ctxT(it, half):
                t, read = filled(it, "ctxT", half)
                nc.scalar.copy(cT[:, 2 * half:2 * half + 2, :, :].rearrange("p l c k -> p (l c k)"), t[:, :]).then_inc(read, 1)

            def V_1(it, l):
                values_out(it, "V1", l, V1, H8, DH8)

            def dt(it, _):
                t, read = filled(it, "dt")
                nc.scalar.copy(dts[:, 0, :, :], t[:, 0:G * MH].rearrange("p (g h) -> p g h", g=G)).then_inc(read, 1)

            def softplus(it, _):
                act.wait_ge(S["near0"], it + 1)
                run(dts[:, 4, :, :], dts[:, 2, :, :], ACT.Exp).then_inc(S["edt"], 1)

            def xbc(it, l):
                n = XBC // 2
                for half in range(2):
                    t, read = filled(it, f"xbc{half}", l)
                    for k in range(n):
                        c = half * n + k
                        run(conv[:, l, c, :], t[:, k * P:(k + 1) * P], ACT.Identity,
                            scale=conv_w[:, c, TAPS - 1:TAPS], bias=conv_b[:, c:c + 1])
                    nc.scalar.copy(raw[:, l, half * n:(half + 1) * n, TAPS - 1:],
                                   t[:, 0:n * P].rearrange("p (c k) -> p c k", c=n)).then_inc(read, 1)

            def z(it, l):
                t, read = filled(it, "z", l)
                nc.scalar.copy(zs[:, l, :], t[:, :])
                run(tz[:, l, :], t[:, :], ACT.Tanh, scale=0.5).then_inc(read, 1)

            def convolved(it, l):
                act.wait_ge(S["conv"], nth(it, l))
                run(raw[:, l, :, TAPS - 1:], conv[:, l, :, :], ACT.Tanh, scale=0.5).then_inc(S["tanh"], 1)

            def pairs(it, l):
                act.wait_ge(S["log_decay"], nth(it, l))
                run(decay[:, l, :, :].rearrange("p (b h) k -> p b (h k)", b=2), score[:, 0:2, :],
                    ACT.Exp).then_inc(S["decay"], 1)

            def Y(it, l):
                act.wait_ge(S["u"], nth(it, l))
                run(dx[:, l, :], zs[:, l, :], ACT.Square, accum_out=stat[:, l, 12:13]).then_inc(S["ss2"], 1)

            def flip_u(it, l):
                copy_out(it, "uT", l, uT[:, l], INNER)

            def Q1(it, l):
                t, read = filled(it, "Q1", l)
                for c in range(DC):
                    last = run(Q[:, l, c, :], t[:, c * P:(c + 1) * P], ACT.Identity, bias=q1_bias[:, c:c + 1])
                last.then_inc(read, 1)

            def Q2(it, l):
                copy_out(it, "Q2", l, Q[:, l], D)

            def K_2(it, l):
                copy_out(it, "K2", l, K2[:, l], D)

            def V_2(it, l):
                values_out(it, "V2", l, V2, H16, DH16)

            def row(it, l):
                t, read = filled(it, "row", l)
                nc.scalar.copy(row_mask[:, l, :], t[:, 0:P]).then_inc(read, 1)

            def Q3(it, l):
                copy_out(it, "Q3", l, Q[:, l], D)

            def V3(it, l):
                act.wait_ge(S["m1"], nth(it, l))
                values_out(it, "V3", l, V2, H16, DH16, mask1[:, l, 1:2])

            def fc1(it, l):
                t, read = filled(it, "fc1", l)
                for c in range(DC):
                    last = run(fc1T[:, l, c, :], t[:, c * P:(c + 1) * P], ACT.Relu, bias=fc1_b[:, c:c + 1])
                last.then_inc(read, 1)

            def K4(it, l):
                t, read = filled(it, "K4", l)
                for c in range(DC):
                    last = run(K2[:, l, c, :], t[:, c * P:(c + 1) * P], ACT.Identity, bias=k4_b[:, c:c + 1])
                last.then_inc(read, 1)

            def Q4(it, l):
                t, read = filled(it, "Q4", l)
                for c in range(DC):
                    last = run(Q[:, l, c, :], t[:, c * P:(c + 1) * P], ACT.Identity, bias=q4_b[:, c:c + 1])
                last.then_inc(read, 1)

            def up(it, l):
                for half in range(2):
                    t, read = filled(it, f"up{half}", l)
                    for k in range(FC // 2):
                        c = half * FC // 2 + k
                        last = run(gT[:, l, c, :], t[:, k * P:(k + 1) * P], ACT.Gelu, bias=up_b[:, c:c + 1])
                    last.then_inc(read, 1)

            do = dict(ctxT=ctxT, V1=V_1, xhatT=copied("xhatT"), dt=dt, softplus=softplus, xbc=xbc, z=z, conv=convolved,
                      pairs=pairs, Y=Y, uT=flip_u, xnT=copied("xnT"), Q1=Q1, oT=copied("oT"), x2T=copied("x2T"),
                      Q2=Q2, K2=K_2, V2=V_2, x3T=copied("x3T"), row=row, Q3=Q3, V3=V3, x4T=copied("x4T"), fc1=fc1,
                      K4=K4, x5T=copied("x5T"), Q4=Q4, x6T=copied("x6T"), up=up,
                      keys1=lambda it, l: by_head(it, 1, l), keys2=lambda it, l: by_head(it, 2, l),
                      keys3=lambda it, l: by_head(it, 3, l), keys4=lambda it, l: by_head(it, 4, l),
                      x1=lambda it, l: x1(it + 1, l), scores=exponential, turn=turned_out)
            with act.Fori(0, ITERS) as it:
                for task, lane in PASS:
                    if task in do:
                        do[task](it, lane)

        @block.vector
        def _(dve):
            tt, ts, stt = nc.vector.tensor_tensor, nc.vector.tensor_scalar, nc.vector.scalar_tensor_tensor

            def filled(it, what, lane=0):
                b, use = job(it, what, lane)
                dve.wait_ge(bank_full[b], use + 1)
                return bank[b], bank_read[b]

            def evacuated(it, what, lane=0):
                b, use = job(it, what, lane)
                dve.wait_ge(bank_read[b], use + 1)

            def root_guess(l, step, src, scale, offset, done):
                step(ts(stat[:, l, 2:3], src, scale, offset, ALU.mult, ALU.add))
                ts(stat[:, l, 4:5].bitcast(I32), stat[:, l, 2:3].bitcast(I32), -0.5, MAGIC,
                   ALU.mult, ALU.add).then_inc(done, 1)

            def moments(l, step, done):
                step(nc.vector.bn_stats(bn[:, l, :], res[:, l, :]))
                step(nc.vector.bn_aggr(stat[:, l, 0:2], bn[:, l, :]))
                root_guess(l, step, stat[:, l, 1:2], 1.0, EPS, done)

            def normalise(it, l, root, done):
                dve.wait_ge(S[root], nth(it, l))
                ts(nrm[:, l, :], res[:, l, :], stat[:, l, 0:1], stat[:, l, 10:11],
                   ALU.subtract, ALU.mult).then_inc(S[done], 1)

            def normalise_affine(it, l, step, root, g, b, done):
                step(stt(nrm[:, l, :], res[:, l, :], stat[:, l, 0:1], rows[g], ALU.subtract, ALU.mult))
                dve.wait_ge(S[root], nth(it, l))
                stt(res[:, l, :], nrm[:, l, :], stat[:, l, 10:11], rows[b], ALU.mult, ALU.add).then_inc(S[done], 1)

            def by_head(it, a_, lane):
                evacuated(it, f"K{a_}", lane)
                if a_ == 1:
                    filled(it, "Y", lane)
                    K, keys, heads, share = K1, keys32, head32, SHARE32["dve"]
                else:
                    K, keys, heads, share = K2, keys16, head16, SHARE16["dve"]
                shape = (P, DC, len(share), P)
                tt(keys[:, lane, :, share[0]:share[-1] + 1, :], K[:, lane, :, :].unsqueeze(2).broadcast_to(shape),
                   heads[:, share[0]:share[-1] + 1].unsqueeze(1).unsqueeze(3).broadcast_to(shape),
                   ALU.mult).then_inc(S[f"keys{a_}_dve"], 1)

            def shift(it, p, step):
                dve.wait_ge(S["scores"], part(it, p) + 1)
                s = score[:, p % SCORE_BANKS, :].rearrange("p (h k) -> p h k", h=HEADS)
                step(nc.vector.tensor_reduce(neg_max[:, p % 2, :], s, AX_X, ALU.max, negate=True))
                tt(shifted[:, p % SHIFTED_BUFFERS, :].rearrange("p (h k) -> p h k", h=HEADS), s,
                   neg_max[:, p % 2, :].unsqueeze(2).broadcast_to((P, HEADS, P)), ALU.add).then_inc(S["shifted"], 1)

            def weighted(it, a_, l, step, heads, dh, dst):
                dve.wait_ge(S["output_full"], nth_output(it, a_, l))
                o = output[:, 0:heads * (dh + 1)].rearrange("p (h e) -> p h e", h=heads)
                step(nc.vector.reciprocal(rec[:, l, 0:heads], o[:, :, dh]))
                tt(dst.rearrange("p (h e) -> p h e", h=heads), o[:, :, 0:dh],
                   rec[:, l, 0:heads].unsqueeze(2).broadcast_to((P, heads, dh)), ALU.mult).then_inc(S["output_read"], 1)
                dve.wait_ge(S["output_read"], nth_output(it, a_, l))

            def x1(it, l):
                if l == 0:
                    dve.wait_ge(S["x_in"], it * 16 + 16)
                tt(res[:, l, :], x_in[:, l, :], att0[:, :], ALU.add).then_inc(S["x1"], 1)

            def x1_root(it, l, step):
                dve.wait_ge(S["ss1"], nth(it, l))
                root_guess(l, step, stat[:, l, 12:13], 1.0 / D, EPS, S["seed1"])

            def xhat(it, l):
                dve.wait_ge(S["rstd1"], nth(it, l))
                ts(nrm[:, l, :], res[:, l, :], stat[:, l, 10:11], None, ALU.mult).then_inc(S["xhat"], 1)

            step = Chain(dve, S["dve_first"])
            dve.wait_ge(S["const_in"], 16)
            nc.vector.memset(stat[:, :, :], 1.0)
            nc.vector.memset(ones_bf[:, :], 1.0)
            nc.vector.tensor_copy(ident_bf[:, :], ident)
            nc.vector.tensor_copy(causal_bf[:, :], con("causal")).then_inc(S["ready_consts"], 1)
            by_head(0, 0, 0)
            for p in range(len(FIRST_PARTS)):
                shift(None, p, step)
            weighted(0, 0, 0, step, H16, DH16, att0[:, :])
            for l in range(G):
                x1(0, l)
            dve.wait_ge(S["ss1"], G)
            v, minus_half_v, y, t = (stat[:, :, k] for k in (2, 5, 4, 6))
            step(ts(v, stat[:, :, 12], 1.0 / D, EPS, ALU.mult, ALU.add))
            ts(y.bitcast(I32), v.bitcast(I32), -0.5, MAGIC, ALU.mult, ALU.add).then_inc(S["seed1"], G)
            dve.wait_ge(S["seed1"], G)
            step(ts(minus_half_v, v, -0.5, None, ALU.mult))
            for k in range(NEWTON):
                step(tt(t, y, y, ALU.mult))
                step(tt(t, t, minus_half_v, ALU.mult))
                last = stt(stat[:, :, 8 + k], t, 1.5, y, ALU.add, ALU.mult)
                y = stat[:, :, 8 + k]
                if k + 1 < NEWTON:
                    step(last)
            last.then_inc(S["rstd1"], G)
            dve.wait_ge(S["wmamba_in"], 16 * 5)
            for c in range(DC):
                ts(w_in[:, c, :], w_in[:, c, :], m_norm[:, c:c + 1], None, ALU.mult)
            dve.wait_ge(S["rates"], 1)
            ts(decay_rate, decay_rate, -1.0, None, ALU.mult).then_inc(S["ready_in"], 1)
            for l in range(G):
                xhat(0, l)
            ts(keep_row[:, :], pad_u8[:, :], -1.0, 1.0, ALU.mult, ALU.add)
            ts(padding_bf[:, :], pad_u8[:, :], MASKED, None, ALU.mult)
            ts(skip, skip, 0.5, None, ALU.mult)
            for c in range(IC):
                ts(w_out[:, c, :], w_out[:, c, :], g_norm[:, c:c + 1], None, ALU.mult)
            for m in range(DC):
                t, read = filled(0, f"bias{m}")
                nc.vector.tensor_copy(q1_bias[:, m:m + 1], t[:, 0:1]).then_inc(read, 1)
            for c in range(DC):
                last = ts(square["q1"][:, c, :], square["q1"][:, c, :], ca_w[:, c:c + 1], None, ALU.mult)
            last.then_inc(S["ready_weights"], 1)
            dve.wait_ge(S["ready_weights"], 1)
            dve.wait_ge(S["pads_zero"], 1)

            def stages(it):
                step = Chain(dve, S["dve_step"])

                def next_x1(l):
                    b, use = job(it, "x6T", l)
                    dve.wait_ge(bank_full[b], use + 1)
                    dve.wait_ge(S["plus"], nth(it, l))
                    x1(it + 1, l)
                    x1_root(it + 1, l, step)

                def K_1(l):
                    t, read = filled(it, "K1", l)
                    tt(K1[:, l, :, :], t[:, 0:D].rearrange("p (c k) -> p c k", c=DC),
                       keep_row[:, :].unsqueeze(1).broadcast_to((P, DC, P)), ALU.mult).then_inc(read, 1)

                def convolve(l):
                    n = XBC // 2
                    for half in range(2):
                        evacuated(it, f"xbc{half}", l)
                        for k in range(TAPS - 1):
                            for c in range(half * n, (half + 1) * n):
                                last = stt(conv[:, l, c, :], raw[:, l, c, k:k + P], conv_w[:, c, k:k + 1],
                                           conv[:, l, c, :], ALU.mult, ALU.add)
                            if half == 0 or k < TAPS - 2:
                                step(last)
                    last.then_inc(S["conv"], 1)

                def silu(l):
                    dve.wait_ge(S["tanh"], nth(it, l))
                    stt(conv[:, l, :, :], raw[:, l, :, TAPS - 1:], 1.0, conv[:, l, :, :],
                        ALU.add, ALU.mult).then_inc(S["xbc"], 1)

                def softplus(_):
                    def d(k):
                        return dts[:, k, :, :]
                    dve.wait_ge(S["edt"], it + 1)
                    step(ts(d(5), d(4), 2.0, None, ALU.add))
                    step(nc.vector.reciprocal(d(6), d(5)))
                    step(tt(d(7), d(4), d(6), ALU.mult))
                    step(tt(d(8), d(7), d(7), ALU.mult))
                    step(ts(d(9), d(8), 1.0 / (2 * LOG1P_TERMS - 1), None, ALU.mult))
                    for k in range(LOG1P_TERMS - 2, 0, -1):
                        step(stt(d(9), d(9), 1.0 / (2 * k + 1), d(8), ALU.add, ALU.mult))
                    step(stt(d(9), d(9), 1.0, d(7), ALU.add, ALU.mult))
                    step(stt(d(10), d(9), 2.0, d(3), ALU.mult, ALU.add))
                    ts(d(11), d(10), 0.5, None, ALU.mult).then_inc(S["dt"], 1)

                def pairs(l):
                    t, read = filled(it, "CB", l)
                    tt(state_gate[:, l, :], t[:, 0:P], gate_mask, ALU.mult).then_inc(read, 1)
                    t, read = filled(it, "xh", l)
                    x3 = t[:, :].rearrange("p (h e) -> p h e", h=MH)
                    dve.wait_ge(S["dt"], it + 1)
                    tt(dbx[:, l, :].rearrange("p (h e) -> p h e", h=MH), x3,
                       dts[:, 11, l, :].unsqueeze(2).broadcast_to((P, MH, MD)), ALU.mult)
                    tt(dx[:, l, :].rearrange("p (h e) -> p h e", h=MH), x3,
                       skip.unsqueeze(2).broadcast_to((P, MH, MD)), ALU.mult).then_inc(read, 1)

                def decayed(l):
                    dve.wait_ge(S["decay"], nth(it, l))
                    evacuated(it, "CB", l)
                    tt(decay[:, l, :, :], decay[:, l, :, :],
                       state_gate[:, l, :].unsqueeze(1).broadcast_to((P, MH, P)), ALU.mult).then_inc(S["M"], 1)

                def gate(l):
                    t, read = filled(it, "Y", l)
                    evacuated(it, "xh", l)
                    dve.wait_ge(S["gated"], nth(it, l))
                    tt(tz[:, l, :], t[:, :], dx[:, l, :], ALU.add).then_inc(read, 1)
                    evacuated(it, "Y", l)
                    tt(zs[:, l, :], tz[:, l, :], zs[:, l, :], ALU.mult).then_inc(S["u"], 1)

                def gate_norm(l):
                    dve.wait_ge(S["ss2"], nth(it, l))
                    root_guess(l, step, stat[:, l, 12:13], 1.0 / INNER, 4.0 * EPS, S["seed2"])

                def mamba_out(l):
                    dve.wait_ge(S["rstd2"], nth(it, l))
                    t, read = filled(it, "proj", l)
                    stt(res[:, l, :], t[:, 0:D], stat[:, l, 10:11], res[:, l, :], ALU.mult, ALU.add).then_inc(read, 1)
                    evacuated(it, "proj", l)
                    moments(l, step, S["seed3"])

                def Wo(l):
                    t, read = filled(it, "Wo", l)
                    tt(res[:, l, :], t[:, 0:D], res[:, l, :], ALU.add).then_inc(read, 1)
                    evacuated(it, "Wo", l)
                    step(nc.vector.tensor_reduce(mask0[:, l, 0:1], res[:, l, :], AX_X, ALU.max, apply_absolute_value=True))
                    step(ts(mask0[:, l, 1:2], mask0[:, l, 0:1], 0.0, None, ALU.is_gt))

                def is_nonzero(a_, l):
                    t, read = filled(it, f"e{a_}", l)
                    ts(nonzero[:, l, :], t[:, 0:H16], 0.0, None, ALU.not_equal).then_inc(read, 1)

                def below_length(a_, l):
                    t, read = filled(it, f"n{a_}", l)
                    ts(keep[:, l, :], t[:, 0:H16], index, None, ALU.is_gt).then_inc(read, 1)

                def add_attention(a_, l, mask, seed):
                    weighted(it, a_, l, step, H16, DH16, att[:, l, :])
                    if mask is None:
                        step(tt(res[:, l, :], att[:, l, :], res[:, l, :], ALU.add))
                    else:
                        step(stt(res[:, l, :], att[:, l, :], mask, res[:, l, :], ALU.mult, ALU.add))
                    moments(l, step, S[seed])

                def token_mask(l):
                    dve.wait_ge(S["x3"], nth(it, l))
                    step(nc.vector.tensor_reduce(mask1[:, l, 0:1], res[:, l, :], AX_X, ALU.max, apply_absolute_value=True))
                    step(ts(mask1[:, l, 1:2], mask1[:, l, 0:1], 0.0, None, ALU.is_gt))
                    ts(mask1_bf[:, l:l + 1], mask1[:, l, 0:1], 0.0, None, ALU.is_gt).then_inc(S["m1"], 1)

                def K3(l):
                    evacuated(it, "row", l)
                    t, read = filled(it, "K3", l)
                    tt(K2[:, l, :, :], t[:, 0:D].rearrange("p (c k) -> p c k", c=DC),
                       row_mask[:, l, :].unsqueeze(1).broadcast_to((P, DC, P)), ALU.mult).then_inc(read, 1)

                def fc2(l):
                    t, read = filled(it, "fc2", l)
                    tt(att[:, l, :], t[:, 0:D], rows["fc2"], ALU.add).then_inc(read, 1)
                    evacuated(it, "fc2", l)
                    step(stt(res[:, l, :], att[:, l, :], mask0[:, l, 1:2], res[:, l, :], ALU.mult, ALU.add))
                    moments(l, step, S["seed6"])

                def V4(l):
                    t, read = filled(it, "V4", l)
                    tt(V2[:, l, :, 0:DH16], t[:, 0:D].rearrange("p (h e) -> p h e", h=H16),
                       rows["v4"].rearrange("p (h e) -> p h e", h=H16), ALU.add).then_inc(read, 1)

                def down(l):
                    if l == 0:
                        dve.wait_ge(S["stored"], it * 16 + 16)
                    t, read = filled(it, "down", l)
                    dve.wait_ge(S["plus"], nth(it, l))
                    tt(result[:, l, :], t[:, 0:D], plus[:, l, :], ALU.add).then_inc(read, 1)

                do = dict(K1=K_1, softplus=softplus, conv=convolve, silu=silu, pairs=pairs, decayed=decayed, Y=gate,
                          uT=gate_norm, proj=mamba_out, xnT=lambda l: normalise(it, l, "rstd3", "xn"),
                          keys1=lambda l: by_head(it, 1, l), scores=lambda p: shift(it, p, step),
                          finish1=lambda l: weighted(it, 1, l, step, H8, DH8, att[:, l, :]), Wo=Wo,
                          keys2=lambda l: by_head(it, 2, l), keys3=lambda l: by_head(it, 3, l),
                          keys4=lambda l: by_head(it, 4, l),
                          e2=lambda l: is_nonzero(2, l), n2=lambda l: below_length(2, l),
                          finish2=lambda l: add_attention(2, l, mask0[:, l, 1:2], "seed4"),
                          norm2=lambda l: normalise_affine(it, l, step, "rstd4", "g1", "b1", "x3"), x3T=token_mask, K3=K3,
                          e3=lambda l: is_nonzero(3, l), n3=lambda l: below_length(3, l),
                          finish3=lambda l: add_attention(3, l, mask1[:, l, 1:2], "seed5"),
                          norm3=lambda l: normalise_affine(it, l, step, "rstd5", "g2", "b2", "x4"), fc2=fc2, V4=V4,
                          norm4=lambda l: normalise_affine(it, l, step, "rstd6", "g3", "b3", "x5"),
                          finish4=lambda l: add_attention(4, l, None, "seed7"),
                          norm5=lambda l: normalise_affine(it, l, step, "rstd7", "g4", "b4", "x6"), down=down, x1=next_x1,
                          xhat=lambda l: xhat(it + 1, l))
                for task, lane in PASS:
                    if task in do:
                        do[task](lane)

            with dve.Fori(0, ITERS) as it:
                stages(it)

        @block.gpsimd
        def _(pool):
            tt, ts, copy = nc.gpsimd.tensor_tensor, nc.gpsimd.tensor_scalar, nc.gpsimd.tensor_copy

            def wait_for(semaphore, value):
                pool.wait_ge(semaphore, value)
                pool.sem_inc(S["pool_waits"], 1)

            def evacuated(it, what, lane=0):
                b, use = job(it, what, lane)
                wait_for(bank_read[b], use + 1)

            nc.gpsimd.memset(V2[:, 0, :, DH16], 1.0).then_inc(S["ones_col"], 1)
            nc.gpsimd.memset(V1[:, :, :, DH8], 1.0).then_inc(S["ones_col"], 1)
            nc.gpsimd.memset(raw[:, :, :, 0:TAPS - 1], 0.0).then_inc(S["pads_zero"], 1)

            def root(it, l, step, seed, done):
                wait_for(S[seed], nth(it, l))
                step(ts(stat[:, l, 5:6], stat[:, l, 2:3], -0.5, None, ALU.mult))
                y = stat[:, l, 4:5]
                for k in range(NEWTON):
                    step(ts(stat[:, l, 6:7], y, y, stat[:, l, 5:6], ALU.mult, ALU.mult))
                    last = ts(stat[:, l, 8 + k:9 + k], stat[:, l, 6:7], 1.5, y, ALU.add, ALU.mult)
                    if k + 1 < NEWTON:
                        step(last)
                    y = stat[:, l, 8 + k:9 + k]
                last.then_inc(S[done], 1)

            def stages(it):
                step = Chain(pool, S["pool_step"])

                def newton(seed, done):
                    return lambda l: root(it, l, step, seed, done)

                def near0(_):
                    def d(k):
                        return dts[:, k, :, :]
                    evacuated(it, "dt")
                    step(tt(d(0), d(0), dt_bias.unsqueeze(1).broadcast_to((P, G, MH)), ALU.add))
                    step(ts(d(3), d(0), 0.0, None, ALU.max))
                    step(ts(d(1), d(3), -2.0, None, ALU.mult))
                    tt(d(2), d(0), d(1), ALU.add).then_inc(S["near0"], 1)

                def gated(l):
                    evacuated(it, "z", l)
                    step(ts(tz[:, l, :], tz[:, l, :], 1.0, None, ALU.add))
                    tt(zs[:, l, :], tz[:, l, :], zs[:, l, :], ALU.mult).then_inc(S["gated"], 1)

                def log_decays(l):
                    wait_for(S["dt"], it + 1)
                    step(tt(dts[:, 5, l, :], dts[:, 10, l, :], decay_rate, ALU.mult))
                    tt(decay[:, l, :, :], after.unsqueeze(1).broadcast_to((P, MH, P)),
                       dts[:, 5, l, :].unsqueeze(2).broadcast_to((P, MH, P)), ALU.mult).then_inc(S["am"], 1)

                def first_query(a_, l):
                    evacuated(it, f"Q{a_}", l)
                    tt(q_first[:, l, :, :], Q[:, l, :, 0].unsqueeze(2).broadcast_to((P, DC, 8)),
                       head16.unsqueeze(1).broadcast_to((P, DC, 8)), ALU.mult).then_inc(S[f"q{a_}_first"], 1)

                def drop(a_, l):
                    evacuated(it, f"V{a_}", l)
                    evacuated(it, f"n{a_}", l)
                    step(tt(V2[:, l, :, 0:DH16], V2[:, l, :, 0:DH16],
                            keep[:, l, :].unsqueeze(2).broadcast_to((P, H16, DH16)), ALU.mult))
                    copy(V2[:, l, :, DH16], keep[:, l, :]).then_inc(S[f"V{a_}"], 1)

                def V4(l):
                    evacuated(it, "V4", l)
                    nc.gpsimd.memset(V2[:, l, :, DH16], 1.0).then_inc(S["V4ones"], 1)

                def norm5(l):
                    wait_for(S["x6"], nth(it, l))
                    tt(plus[:, l, :], res[:, l, :], rows["down"], ALU.add).then_inc(S["plus"], 1)

                do = dict(dt=near0, z=gated, am=log_decays, uT=newton("seed2", "rstd2"), proj=newton("seed3", "rstd3"),
                          Q2=lambda l: first_query(2, l), n2=lambda l: drop(2, l),
                          finish2=newton("seed4", "rstd4"),
                          Q3=lambda l: first_query(3, l), n3=lambda l: drop(3, l),
                          finish3=newton("seed5", "rstd5"),
                          fc2=newton("seed6", "rstd6"), V4=V4,
                          finish4=newton("seed7", "rstd7"), norm5=norm5,
                          x1=lambda l: root(it + 1, l, step, "seed1", "rstd1"))
                for task, lane in PASS:
                    if task in do:
                        do[task](lane)

            with pool.Fori(0, ITERS) as it:
                stages(it)


def constants():
    import numpy as np

    p, k = np.arange(P)[:, None], np.arange(P)[None, :]
    c = {
        "ident": p == k,
        "before": p <= k,
        "gate": 0.25 * (p <= k),
        "after": p > k,
        "causal": np.where(k > p, MASKED, 0),
        "head16": p // DH16 == np.arange(8)[None, :],
        "head32": p // DH8 == np.arange(4)[None, :],
        "index": p,
    }
    return np.concatenate([np.asarray(c[n], np.float32) for n in CONST_COLS], axis=1)


def kernel(**inputs):
    import numpy as np
    import concourse.bacc as bacc
    from concourse.bass_utils import run_bass_kernel_spmd

    def arr(name):
        return np.asarray(inputs[name])

    def by_head(name):
        w = arr(name)
        return w.transpose(1, 0, 2).reshape(w.shape[1], -1)

    a = {"x": arr("x"), "ctx_1024": arr("ctx_1024"), "const": constants(), "pad": arr("mask_1xS2_bf0").view(np.int32)}
    for n in "qkv":
        a[n + "0"] = arr(f"L0_xattn_W{n}").T
        a[n + "1"] = arr(f"L1_xattn_W{n}")
        a[n + "2"] = by_head(f"L2_xattn_W{n}1")
        a[n + "3"] = by_head(f"L2_xattn_W{n}2")
        a[n + "4"] = arr(f"L3_xattn_W{n}").T
    a["o1"] = arr("L1_xattn_Wo")
    a["in_proj"], a["out_proj"] = arr("L1_xattn_in_proj_w"), arr("L1_xattn_out_proj_w")
    a["fc1"], a["fc2"] = arr("L2_xattn_fc1_w").T, arr("L2_xattn_fc2_w").T
    a["up"], a["down"] = arr("L3_xattn_W1").T, arr("L3_xattn_W2").T
    vectors = dict(
        m_norm="L1_xattn_m_norm_w", g_norm="L1_xattn_gnorm_w", conv_w="L1_xattn_conv_w", conv_b="L1_xattn_conv_b",
        ca_w="L1_xattn_ca_ln_w", ca_b="L1_xattn_ca_ln_b", fc1_b="L2_xattn_fc1_b", q4_b="L3_xattn_bq",
        k4_b="L3_xattn_bk", up_b="L3_xattn_b1")
    a["vectors"] = np.concatenate(
        [arr(vectors[n]).reshape(-1, P, arr(vectors[n]).size // len(arr(vectors[n])))
         .transpose(1, 0, 2).reshape(P, VECTORS[n]) for n in VECTORS], axis=1)
    rows = dict(
        g1="L2_xattn_ln1_g", b1="L2_xattn_ln1_b", g2="L2_xattn_ln2_g", b2="L2_xattn_ln2_b", g3="L2_xattn_ln3_g",
        b3="L2_xattn_ln3_b", g4="L3_xattn_ln_g", b4="L3_xattn_ln_b", fc2="L2_xattn_fc2_b", v4="L3_xattn_bv",
        down="L3_xattn_b2", dt_bias="L1_xattn_dt_bias", A_log="L1_xattn_A_log", D_skip="L1_xattn_D_skip")
    a["rows"] = np.concatenate([arr(rows[n]) for n in ROWS])

    nc = bacc.Bacc("TRN2", target_bir_lowering=False, num_devices=1)
    arrays, views = {}, {}
    for n, v in a.items():
        v = np.ascontiguousarray(v)
        arrays["in_" + n] = v
        views[n] = nc.dram_tensor("in_" + n, v.shape, mybir.dt.from_np(v.dtype), kind="ExternalInput").ap()
    out = nc.dram_tensor("out_0", (B, P, D), F32, kind="ExternalOutput").ap()
    decoder_stack(nc, views, out)
    r = run_bass_kernel_spmd(nc, [arrays], core_ids=[0])
    return r.results[0]["out_0"]
```
